# Optimizing a Trainium2 kernel written in Bass

```python
import numpy as np
import jax
import jax.numpy as jnp

def _softmax(x, axis=-1):
    return jax.nn.softmax(x, axis=axis)

def _gelu(x):
    return jax.nn.gelu(x, approximate=True)

def _silu(x):
    return jax.nn.silu(x)

def _sigmoid(x):
    return jax.nn.sigmoid(x)

def _layernorm(x, axis=-1, eps=1e-05):
    m = jnp.mean(x, axis=axis, keepdims=True)
    v = jnp.var(x, axis=axis, keepdims=True)
    return (x - m) / jnp.sqrt(v + eps)

def _scatter_add(tgt, idx, src, axis=0):
    return tgt.at[idx].add(src)

def _segment_sum(src, seg, n):
    return jax.ops.segment_sum(src, seg, n)
kernel_name = 'mk_flamingo_gated_d4_seqx_r8_f28f54'

def setup_inputs(seed: int=0):
    np.random.seed(seed)
    _w = jnp.asarray

    def _rec_inputs():
        import jax
        import jax.numpy as jnp
        _rk = jax.random.key(seed)
        x = 7.22e-05 + 1 * jax.random.normal(jax.random.fold_in(_rk, 1), (8, 256, 128), jnp.float32)
        _lenS = 256 - jax.random.randint(jax.random.fold_in(_rk, 7), (8,), 0, max(1, 256 // 4) + 1, jnp.int32)
        _lenS2 = 256 - jax.random.randint(jax.random.fold_in(_rk, 8), (8,), 0, max(1, 256 // 4) + 1, jnp.int32)
        _ctx_768P = jax.random.normal(jax.random.fold_in(_rk, 11), (8, 16, 96), jnp.float32)
        _ctx_768c = jax.random.dirichlet(jax.random.fold_in(_rk, 511), 0.3 * jnp.ones((16,), jnp.float32), (8, 256))
        _ctx_768t = jnp.einsum('bsk,bkd->bsd', _ctx_768c, _ctx_768P)
        _ctx_768t = _ctx_768t * jax.lax.rsqrt(jnp.mean(jnp.square(_ctx_768t)) + 1e-12) * 0.953939
        ctx_768 = 2.09791e-05 + 1.00001 * (_ctx_768t + 0.3 * jax.random.normal(jax.random.fold_in(_rk, 611), (8, 256, 96), jnp.float32))
        _validS = jnp.arange(256)[None, :] < _lenS[:, None]
        _validS2 = jnp.arange(256)[None, :] < _lenS2[:, None]
        _causal = jnp.tril(jnp.ones((256, 256), dtype=bool))
        mask_BxS_bk0 = jnp.logical_not(jnp.broadcast_to(_validS[:, :], (8, 256)))
        mask_BxS2_bf1 = jnp.ones((8, 256), dtype=bool)
        mask_BxS2_bk0 = jnp.logical_not(jnp.broadcast_to(_validS2[:, :], (8, 256)))
        _g = jax.random.normal(jax.random.fold_in(_rk, 9001), (2, 4), jnp.float32)
        _g = jnp.sign(_g) * jnp.maximum(jnp.abs(_g), 1.0) + (_g == 0) * 1.0
        g_xattn = _g[0]
        g_ffn = _g[1]
        return (x, ctx_768, mask_BxS_bk0, mask_BxS2_bf1, mask_BxS2_bk0, g_xattn, g_ffn)
    x, ctx_768, mask_BxS_bk0, mask_BxS2_bf1, mask_BxS2_bk0, g_xattn, g_ffn = _rec_inputs()

    def _L0_xattn_setup():
        import jax, jax.numpy as jnp
        import numpy as np
        NUM_HEADS = 16
        key = jax.random.key(seed)
        k1, k2, k3, k4, k5 = jax.random.split(key, 5)
        B, N, C = (4, 256, 128)
        N2, Cy = (128, 96)
        x = jax.random.normal(k1, (B, N, C), dtype=jnp.float32)
        y = jax.random.normal(k2, (B, N2, Cy), dtype=jnp.float32)
        pad_mask = jax.random.randint(k3, (B, N), 0, 2).astype(jnp.bool_)
        Wq = jax.random.normal(k4, (C, C), dtype=jnp.float32) * C ** (-0.5)
        Wkv = jax.random.normal(k5, (2 * C, Cy), dtype=jnp.float32) * Cy ** (-0.5)
        return {'x': x, 'y': y, 'pad_mask': pad_mask, 'Wq': Wq, 'Wkv': Wkv}
    _L0_xattn_all = _L0_xattn_setup()
    _L0_xattn_in = {k: v for k, v in _L0_xattn_all.items() if k in ('Wq', 'Wkv')}
    del _L0_xattn_all

    def _L0_ffn_setup():
        import jax, jax.numpy as jnp
        import numpy as np
        HIDDEN = 128
        INNER = 512

        def _weight_quant(w):
            scale = 1.0 / jnp.clip(jnp.mean(jnp.abs(w)), 1e-05)
            wq = jnp.clip(jnp.round(w * scale), -1.0, 1.0) / scale
            return w + jax.lax.stop_gradient(wq - w)

        def _act_quant(x):
            scale = 127.0 / jnp.clip(jnp.max(jnp.abs(x), axis=-1, keepdims=True), 1e-05)
            xq = jnp.clip(jnp.round(x * scale), -128.0, 127.0) / scale
            return x + jax.lax.stop_gradient(xq - x)

        def _bitlinear(x, w):
            return jnp.einsum('bsi,oi->bso', _act_quant(x), _weight_quant(w))
        key = jax.random.key(seed)
        k0, k1, k2, k3 = jax.random.split(key, 4)
        x = jax.random.normal(k0, (4, 256, HIDDEN), dtype=jnp.float32)
        w_gate = jax.random.normal(k1, (INNER, HIDDEN), dtype=jnp.float32) / np.sqrt(HIDDEN)
        w_up = jax.random.normal(k2, (INNER, HIDDEN), dtype=jnp.float32) / np.sqrt(HIDDEN)
        w_down = jax.random.normal(k3, (HIDDEN, INNER), dtype=jnp.float32) / np.sqrt(INNER)
        return {'x': x, 'w_gate': w_gate, 'w_up': w_up, 'w_down': w_down}
    _L0_ffn_all = _L0_ffn_setup()
    _L0_ffn_in = {k: v for k, v in _L0_ffn_all.items() if k in ('w_gate', 'w_up', 'w_down')}
    del _L0_ffn_all

    def _L1_xattn_setup():
        import jax, jax.numpy as jnp
        import numpy as np
        DIM = 128
        CTX_DIM = 96
        HEADS = 8
        DIM_HEAD = 64
        INNER = HEADS * DIM_HEAD
        SCALE = 8.0
        EPS = 1e-05

        def stable_layernorm(x, g):
            x = x / jax.lax.stop_gradient(jnp.max(x, axis=-1, keepdims=True))
            mean = jnp.mean(x, axis=-1, keepdims=True)
            var = jnp.var(x, axis=-1, keepdims=True)
            return (x - mean) * jax.lax.rsqrt(var + EPS) * g

        def l2norm(t):
            n = jnp.sqrt(jnp.sum(t * t, axis=-1, keepdims=True))
            return t / jnp.maximum(n, 1e-12)
        key = jax.random.key(seed)
        ks = jax.random.split(key, 10)
        b, n, m = (4, 256, 128)
        inp = {'x': jax.random.normal(ks[0], (b, n, DIM), jnp.float32), 'context': jax.random.normal(ks[1], (b, m, CTX_DIM), jnp.float32), 'mask': jnp.ones((b, m), dtype=bool), 'g_norm': jnp.ones((DIM,), jnp.float32), 'Wq': jax.random.normal(ks[2], (DIM, INNER), jnp.float32) * DIM ** (-0.5), 'Wkv': jax.random.normal(ks[3], (CTX_DIM, 2 * INNER), jnp.float32) * CTX_DIM ** (-0.5), 'null_kv': jax.random.normal(ks[4], (2, DIM_HEAD), jnp.float32), 'q_scale': jnp.ones((DIM_HEAD,), jnp.float32), 'k_scale': jnp.ones((DIM_HEAD,), jnp.float32), 'Wo': jax.random.normal(ks[5], (INNER, DIM), jnp.float32) * INNER ** (-0.5), 'g_out': jnp.ones((DIM,), jnp.float32)}
        return inp
    _L1_xattn_all = _L1_xattn_setup()
    _L1_xattn_in = {k: v for k, v in _L1_xattn_all.items() if k in ('g_norm', 'Wq', 'Wkv', 'null_kv', 'q_scale', 'k_scale', 'Wo', 'g_out')}
    del _L1_xattn_all

    def _L1_ffn_setup():
        import jax, jax.numpy as jnp
        import numpy as np
        D_MODEL = 128
        N_HEADS = 16
        HEAD_DIM = D_MODEL // N_HEADS
        KV_LATENT = 64
        N_EXPERTS = 4
        D_HIDDEN = 4 * D_MODEL
        B, T = (2, 128)

        def rmsnorm(x, w, eps=1e-06):
            return w * (x * jax.lax.rsqrt(jnp.mean(x * x, axis=-1, keepdims=True) + eps))

        def layernorm(x, g, b, eps=1e-05):
            mu = jnp.mean(x, axis=-1, keepdims=True)
            var = jnp.mean((x - mu) ** 2, axis=-1, keepdims=True)
            return (x - mu) * jax.lax.rsqrt(var + eps) * g + b

        def apply_rope(x):
            t, d = (x.shape[2], x.shape[3])
            half = d // 2
            pos = jnp.arange(t, dtype=x.dtype)[:, None]
            inv_freq = 1.0 / 10000.0 ** (jnp.arange(half, dtype=x.dtype) / half)
            ang = pos * inv_freq[None, :]
            sin, cos = (jnp.sin(ang), jnp.cos(ang))
            x1, x2 = (x[..., :half], x[..., half:])
            return jnp.concatenate([x1 * cos - x2 * sin, x1 * sin + x2 * cos], axis=-1)

        def mla_attention(x, Wq, Wdkv, Wuk, Wuv, Wo, ln_g, ln_b):
            b, t, _ = x.shape
            q = (x @ Wq.T).reshape(b, t, N_HEADS, HEAD_DIM).transpose(0, 2, 1, 3)
            latent = layernorm(x @ Wdkv.T, ln_g, ln_b)
            k = (latent @ Wuk.T).reshape(b, t, N_HEADS, HEAD_DIM).transpose(0, 2, 1, 3)
            v = (latent @ Wuv.T).reshape(b, t, N_HEADS, HEAD_DIM).transpose(0, 2, 1, 3)
            q = apply_rope(q)
            k = apply_rope(k)
            scores = jnp.einsum('bhqd,bhkd->bhqk', q, k) / np.sqrt(HEAD_DIM)
            causal = jnp.tril(jnp.ones((t, t), dtype=bool))
            scores = jnp.where(causal, scores, -jnp.inf)
            attn = jax.nn.softmax(scores, axis=-1)
            out = jnp.einsum('bhqk,bhkd->bhqd', attn, v).transpose(0, 2, 1, 3).reshape(b, t, D_MODEL)
            return out @ Wo.T

        def moe(x, gate_w, gate_b, W1, b1, W2, b2):
            logits = x @ gate_w.T + gate_b
            top = jnp.argmax(logits, axis=-1)
            onehot = jax.nn.one_hot(top, N_EXPERTS, dtype=x.dtype)
            h = jax.nn.relu(jnp.einsum('btd,ehd->bteh', x, W1) + b1)
            y = jnp.einsum('bteh,edh->bted', h, W2) + b2
            return jnp.einsum('bted,bte->btd', y, onehot)
        key = jax.random.key(seed)
        ks = jax.random.split(key, 16)
        s = lambda fan_in: 1.0 / np.sqrt(fan_in)
        return {'x': jax.random.normal(ks[0], (B, T, D_MODEL), jnp.float32), 'norm1_w': jnp.ones((D_MODEL,), jnp.float32), 'norm2_w': jnp.ones((D_MODEL,), jnp.float32), 'Wq': jax.random.normal(ks[1], (D_MODEL, D_MODEL), jnp.float32) * s(D_MODEL), 'Wdkv': jax.random.normal(ks[2], (KV_LATENT, D_MODEL), jnp.float32) * s(D_MODEL), 'Wuk': jax.random.normal(ks[3], (D_MODEL, KV_LATENT), jnp.float32) * s(KV_LATENT), 'Wuv': jax.random.normal(ks[4], (D_MODEL, KV_LATENT), jnp.float32) * s(KV_LATENT), 'Wo': jax.random.normal(ks[5], (D_MODEL, D_MODEL), jnp.float32) * s(D_MODEL), 'ln_g': jnp.ones((KV_LATENT,), jnp.float32), 'ln_b': jnp.zeros((KV_LATENT,), jnp.float32), 'gate_w': jax.random.normal(ks[6], (N_EXPERTS, D_MODEL), jnp.float32) * s(D_MODEL), 'gate_b': jnp.zeros((N_EXPERTS,), jnp.float32), 'W1': jax.random.normal(ks[7], (N_EXPERTS, D_HIDDEN, D_MODEL), jnp.float32) * s(D_MODEL), 'b1': jnp.zeros((N_EXPERTS, D_HIDDEN), jnp.float32), 'W2': jax.random.normal(ks[8], (N_EXPERTS, D_MODEL, D_HIDDEN), jnp.float32) * s(D_HIDDEN), 'b2': jnp.zeros((N_EXPERTS, D_MODEL), jnp.float32)}
    _L1_ffn_all = _L1_ffn_setup()
    _L1_ffn_in = {k: v for k, v in _L1_ffn_all.items() if k in ('norm1_w', 'norm2_w', 'Wq', 'Wdkv', 'Wuk', 'Wuv', 'Wo', 'ln_g', 'ln_b', 'gate_w', 'gate_b', 'W1', 'b1', 'W2', 'b2')}
    del _L1_ffn_all

    def _L2_xattn_setup():
        import jax, jax.numpy as jnp
        import numpy as np
        N_HEADS = 16
        key = jax.random.key(seed)
        ks = jax.random.split(key, 8)
        b, l, m = (8, 128, 128)
        d_embed, d_cross = (128, 96)
        s_q = 1.0 / np.sqrt(d_embed)
        s_kv = 1.0 / np.sqrt(d_cross)
        return {'x': jax.random.normal(ks[0], (b, l, d_embed), jnp.float32), 'y': jax.random.normal(ks[1], (b, m, d_cross), jnp.float32), 'Wq': jax.random.normal(ks[2], (d_embed, d_embed), jnp.float32) * s_q, 'bq': jax.random.normal(ks[3], (d_embed,), jnp.float32) * 0.01, 'Wkv': jax.random.normal(ks[4], (2 * d_embed, d_cross), jnp.float32) * s_kv, 'bkv': jax.random.normal(ks[5], (2 * d_embed,), jnp.float32) * 0.01, 'Wo': jax.random.normal(ks[6], (d_embed, d_embed), jnp.float32) * s_q, 'bo': jax.random.normal(ks[7], (d_embed,), jnp.float32) * 0.01}
    _L2_xattn_all = _L2_xattn_setup()
    _L2_xattn_in = {k: v for k, v in _L2_xattn_all.items() if k in ('Wq', 'bq', 'Wkv', 'bkv', 'Wo', 'bo')}
    del _L2_xattn_all

    def _L2_ffn_setup():
        import jax, jax.numpy as jnp
        import numpy as np
        B, L, D = (4, 128, 128)
        E, H, K = (16, 64, 8)
        EPS = 1e-12

        def _l2norm(v, axis=-1):
            n = jnp.sqrt(jnp.sum(v * v, axis=axis, keepdims=True))
            return v / jnp.maximum(n, EPS)
        if __name__ == '__main__':
            out = reference(**setup_inputs())
            print(out.shape)
        key = jax.random.key(seed)
        ks = jax.random.split(key, 8)
        s = lambda fan_in: 1.0 / np.sqrt(fan_in)
        return {'x': jax.random.normal(ks[0], (B, L, D), jnp.float32), 'gate_w': jax.random.normal(ks[1], (E, D), jnp.float32) * s(D), 'w_gate': jax.random.normal(ks[2], (E, D, H), jnp.float32) * s(D), 'w_up': jax.random.normal(ks[3], (E, D, H), jnp.float32) * s(D), 'w_down': jax.random.normal(ks[4], (E, H, D), jnp.float32) * s(H), 'sw_gate': jax.random.normal(ks[5], (D, H), jnp.float32) * s(D), 'sw_up': jax.random.normal(ks[6], (D, H), jnp.float32) * s(D), 'sw_down': jax.random.normal(ks[7], (H, D), jnp.float32) * s(H)}
    _L2_ffn_all = _L2_ffn_setup()
    _L2_ffn_in = {k: v for k, v in _L2_ffn_all.items() if k in ('gate_w', 'w_gate', 'w_up', 'w_down', 'sw_gate', 'sw_up', 'sw_down')}
    del _L2_ffn_all

    def _L3_xattn_setup():
        import jax, jax.numpy as jnp
        import numpy as np
        DIM_IN, DIM_LAT, DIM_HEAD = (96, 128, 64)
        INNER = max(DIM_LAT, DIM_IN)
        HEADS = INNER // DIM_HEAD
        SCALE = DIM_HEAD ** (-0.5)
        RMS_EPS = 1e-08
        LN_EPS = 1e-05

        def layernorm(x, g, b):
            mu = jnp.mean(x, axis=-1, keepdims=True)
            var = jnp.mean((x - mu) ** 2, axis=-1, keepdims=True)
            return (x - mu) * jax.lax.rsqrt(var + LN_EPS) * g + b

        def rmsnorm(x, gamma):
            norm = jnp.sqrt(jnp.sum(x * x, axis=-1, keepdims=True)) * x.shape[-1] ** (-0.5)
            return x / jnp.maximum(norm, RMS_EPS) * gamma
        key = jax.random.key(seed)
        ks = jax.random.split(key, 12)
        b, n, m = (4, 512, 64)
        x = jax.random.normal(ks[0], (b, n, DIM_IN), jnp.float32)
        latents = jax.random.normal(ks[1], (b, m, DIM_LAT), jnp.float32)
        mask = jax.random.randint(ks[2], (b, n), 0, 2).astype(bool)
        s = lambda k, sh, fan: jax.random.normal(k, sh, jnp.float32) * fan ** (-0.5)
        return {'x': x, 'latents': latents, 'mask': mask, 'ln_x_g': jnp.ones((DIM_IN,), jnp.float32), 'ln_x_b': jnp.zeros((DIM_IN,), jnp.float32), 'ln_l_g': jnp.ones((DIM_LAT,), jnp.float32), 'ln_l_b': jnp.zeros((DIM_LAT,), jnp.float32), 'qn_g': jnp.ones((DIM_HEAD,), jnp.float32), 'kn_g': jnp.ones((DIM_HEAD,), jnp.float32), 'Wq': s(ks[3], (INNER, DIM_LAT), DIM_LAT), 'Wkv': s(ks[4], (2 * INNER, DIM_IN), DIM_IN), 'Wlkv': s(ks[5], (2 * INNER, DIM_LAT), DIM_LAT), 'Wo': s(ks[6], (DIM_LAT, INNER), INNER), 'bo': jnp.zeros((DIM_LAT,), jnp.float32)}
    _L3_xattn_all = _L3_xattn_setup()
    _L3_xattn_in = {k: v for k, v in _L3_xattn_all.items() if k in ('ln_x_g', 'ln_x_b', 'ln_l_g', 'ln_l_b', 'qn_g', 'kn_g', 'Wq', 'Wkv', 'Wlkv', 'Wo', 'bo')}
    del _L3_xattn_all

    def _L3_ffn_setup():
        import jax, jax.numpy as jnp
        import numpy as np
        E, K, D, H = (8, 2, 128, 256)
        B, S = (1, 128)

        def _grouped_swiglu(x_sorted, counts, w1, w2, w3):
            if hasattr(jax.lax, 'ragged_dot'):
                gs = counts.astype(jnp.int32)
                h = jax.nn.silu(jax.lax.ragged_dot(x_sorted, w1, gs)) * jax.lax.ragged_dot(x_sorted, w3, gs)
                return jax.lax.ragged_dot(h, w2, gs)
            pos = jnp.arange(x_sorted.shape[0])
            eid = jnp.searchsorted(jnp.cumsum(counts), pos, side='right')
            out = jnp.zeros((x_sorted.shape[0], w2.shape[-1]), x_sorted.dtype)
            for e in range(w1.shape[0]):
                xm = jnp.where((eid == e)[:, None], x_sorted, 0.0)
                he = jax.nn.silu(xm @ w1[e]) * (xm @ w3[e])
                out = out + he @ w2[e]
            return out
        key = jax.random.key(seed)
        k0, k1, k2, k3, k4 = jax.random.split(key, 5)
        sD = 1.0 / np.sqrt(D)
        sH = 1.0 / np.sqrt(H)
        return {'hidden_states': jax.random.normal(k0, (B, S, D), jnp.float32), 'gate_w': jax.random.normal(k1, (E, D), jnp.float32) * sD, 'w1': jax.random.normal(k2, (E, D, H), jnp.float32) * sD, 'w2': jax.random.normal(k3, (E, H, D), jnp.float32) * sH, 'w3': jax.random.normal(k4, (E, D, H), jnp.float32) * sD}
    _L3_ffn_all = _L3_ffn_setup()
    _L3_ffn_in = {k: v for k, v in _L3_ffn_all.items() if k in ('gate_w', 'w1', 'w2', 'w3')}
    del _L3_ffn_all
    return {'x': x, 'ctx_768': ctx_768, 'mask_BxS_bk0': mask_BxS_bk0, 'mask_BxS2_bf1': mask_BxS2_bf1, 'mask_BxS2_bk0': mask_BxS2_bk0, 'g_xattn': g_xattn, 'g_ffn': g_ffn, 'L0_xattn_Wq': _L0_xattn_in['Wq'], 'L0_xattn_Wkv': _L0_xattn_in['Wkv'], 'L0_ffn_w_gate': _L0_ffn_in['w_gate'], 'L0_ffn_w_up': _L0_ffn_in['w_up'], 'L0_ffn_w_down': _L0_ffn_in['w_down'], 'L1_xattn_g_norm': _L1_xattn_in['g_norm'], 'L1_xattn_Wq': _L1_xattn_in['Wq'], 'L1_xattn_Wkv': _L1_xattn_in['Wkv'], 'L1_xattn_null_kv': _L1_xattn_in['null_kv'], 'L1_xattn_q_scale': _L1_xattn_in['q_scale'], 'L1_xattn_k_scale': _L1_xattn_in['k_scale'], 'L1_xattn_Wo': _L1_xattn_in['Wo'], 'L1_xattn_g_out': _L1_xattn_in['g_out'], 'L1_ffn_norm1_w': _L1_ffn_in['norm1_w'], 'L1_ffn_norm2_w': _L1_ffn_in['norm2_w'], 'L1_ffn_Wq': _L1_ffn_in['Wq'], 'L1_ffn_Wdkv': _L1_ffn_in['Wdkv'], 'L1_ffn_Wuk': _L1_ffn_in['Wuk'], 'L1_ffn_Wuv': _L1_ffn_in['Wuv'], 'L1_ffn_Wo': _L1_ffn_in['Wo'], 'L1_ffn_ln_g': _L1_ffn_in['ln_g'], 'L1_ffn_ln_b': _L1_ffn_in['ln_b'], 'L1_ffn_gate_w': _L1_ffn_in['gate_w'], 'L1_ffn_gate_b': _L1_ffn_in['gate_b'], 'L1_ffn_W1': _L1_ffn_in['W1'], 'L1_ffn_b1': _L1_ffn_in['b1'], 'L1_ffn_W2': _L1_ffn_in['W2'], 'L1_ffn_b2': _L1_ffn_in['b2'], 'L2_xattn_Wq': _L2_xattn_in['Wq'], 'L2_xattn_bq': _L2_xattn_in['bq'], 'L2_xattn_Wkv': _L2_xattn_in['Wkv'], 'L2_xattn_bkv': _L2_xattn_in['bkv'], 'L2_xattn_Wo': _L2_xattn_in['Wo'], 'L2_xattn_bo': _L2_xattn_in['bo'], 'L2_ffn_gate_w': _L2_ffn_in['gate_w'], 'L2_ffn_w_gate': _L2_ffn_in['w_gate'], 'L2_ffn_w_up': _L2_ffn_in['w_up'], 'L2_ffn_w_down': _L2_ffn_in['w_down'], 'L2_ffn_sw_gate': _L2_ffn_in['sw_gate'], 'L2_ffn_sw_up': _L2_ffn_in['sw_up'], 'L2_ffn_sw_down': _L2_ffn_in['sw_down'], 'L3_xattn_ln_x_g': _L3_xattn_in['ln_x_g'], 'L3_xattn_ln_x_b': _L3_xattn_in['ln_x_b'], 'L3_xattn_ln_l_g': _L3_xattn_in['ln_l_g'], 'L3_xattn_ln_l_b': _L3_xattn_in['ln_l_b'], 'L3_xattn_qn_g': _L3_xattn_in['qn_g'], 'L3_xattn_kn_g': _L3_xattn_in['kn_g'], 'L3_xattn_Wq': _L3_xattn_in['Wq'], 'L3_xattn_Wkv': _L3_xattn_in['Wkv'], 'L3_xattn_Wlkv': _L3_xattn_in['Wlkv'], 'L3_xattn_Wo': _L3_xattn_in['Wo'], 'L3_xattn_bo': _L3_xattn_in['bo'], 'L3_ffn_gate_w': _L3_ffn_in['gate_w'], 'L3_ffn_w1': _L3_ffn_in['w1'], 'L3_ffn_w2': _L3_ffn_in['w2'], 'L3_ffn_w3': _L3_ffn_in['w3']}

def reference(x, ctx_768, mask_BxS_bk0, mask_BxS2_bf1, mask_BxS2_bk0, g_xattn, g_ffn, L0_xattn_Wq, L0_xattn_Wkv, L0_ffn_w_gate, L0_ffn_w_up, L0_ffn_w_down, L1_xattn_g_norm, L1_xattn_Wq, L1_xattn_Wkv, L1_xattn_null_kv, L1_xattn_q_scale, L1_xattn_k_scale, L1_xattn_Wo, L1_xattn_g_out, L1_ffn_norm1_w, L1_ffn_norm2_w, L1_ffn_Wq, L1_ffn_Wdkv, L1_ffn_Wuk, L1_ffn_Wuv, L1_ffn_Wo, L1_ffn_ln_g, L1_ffn_ln_b, L1_ffn_gate_w, L1_ffn_gate_b, L1_ffn_W1, L1_ffn_b1, L1_ffn_W2, L1_ffn_b2, L2_xattn_Wq, L2_xattn_bq, L2_xattn_Wkv, L2_xattn_bkv, L2_xattn_Wo, L2_xattn_bo, L2_ffn_gate_w, L2_ffn_w_gate, L2_ffn_w_up, L2_ffn_w_down, L2_ffn_sw_gate, L2_ffn_sw_up, L2_ffn_sw_down, L3_xattn_ln_x_g, L3_xattn_ln_x_b, L3_xattn_ln_l_g, L3_xattn_ln_l_b, L3_xattn_qn_g, L3_xattn_kn_g, L3_xattn_Wq, L3_xattn_Wkv, L3_xattn_Wlkv, L3_xattn_Wo, L3_xattn_bo, L3_ffn_gate_w, L3_ffn_w1, L3_ffn_w2, L3_ffn_w3):
    import jax
    import jax.numpy as jnp

    def _L0_xattn_ref(x, y, pad_mask, Wq, Wkv):
        import jax, jax.numpy as jnp
        import numpy as np
        NUM_HEADS = 16
        B, N, C = x.shape
        N2 = y.shape[1]
        H = NUM_HEADS
        d = C // H
        scale = d ** (-0.5)
        q = (x @ Wq.T).reshape(B, N, H, d).transpose(0, 2, 1, 3)
        kv = (y @ Wkv.T).reshape(B, N2, 2, H, d).transpose(2, 0, 3, 1, 4)
        k, v = (kv[0], kv[1])
        attn = jnp.einsum('bhnd,bhmd->bhnm', q * scale, k)
        attn = jnp.where(pad_mask[:, None, :, None], attn, jnp.float32(-1000000000.0))
        attn = jax.nn.softmax(attn, axis=-1)
        out = jnp.einsum('bhnm,bhmd->bhnd', attn, v)
        return out.transpose(0, 2, 1, 3).reshape(B, N, C)

    def _L0_ffn_ref(x, w_gate, w_up, w_down):
        import jax, jax.numpy as jnp
        import numpy as np
        HIDDEN = 128
        INNER = 512

        def _weight_quant(w):
            scale = 1.0 / jnp.clip(jnp.mean(jnp.abs(w)), 1e-05)
            wq = jnp.clip(jnp.round(w * scale), -1.0, 1.0) / scale
            return w + jax.lax.stop_gradient(wq - w)

        def _act_quant(x):
            scale = 127.0 / jnp.clip(jnp.max(jnp.abs(x), axis=-1, keepdims=True), 1e-05)
            xq = jnp.clip(jnp.round(x * scale), -128.0, 127.0) / scale
            return x + jax.lax.stop_gradient(xq - x)

        def _bitlinear(x, w):
            return jnp.einsum('bsi,oi->bso', _act_quant(x), _weight_quant(w))
        gate = jax.nn.silu(_bitlinear(x, w_gate))
        up = _bitlinear(x, w_up)
        return _bitlinear(gate * up, w_down)

    def _L1_xattn_ref(x, context, mask, g_norm, Wq, Wkv, null_kv, q_scale, k_scale, Wo, g_out):
        import jax, jax.numpy as jnp
        import numpy as np
        DIM = 128
        CTX_DIM = 96
        HEADS = 8
        DIM_HEAD = 64
        INNER = HEADS * DIM_HEAD
        SCALE = 8.0
        EPS = 1e-05

        def stable_layernorm(x, g):
            x = x / jax.lax.stop_gradient(jnp.max(x, axis=-1, keepdims=True))
            mean = jnp.mean(x, axis=-1, keepdims=True)
            var = jnp.var(x, axis=-1, keepdims=True)
            return (x - mean) * jax.lax.rsqrt(var + EPS) * g

        def l2norm(t):
            n = jnp.sqrt(jnp.sum(t * t, axis=-1, keepdims=True))
            return t / jnp.maximum(n, 1e-12)
        b, n, _ = x.shape
        x = stable_layernorm(x, g_norm)
        q = jnp.einsum('bnd,de->bne', x, Wq)
        kv = jnp.einsum('bmd,de->bme', context, Wkv)
        k, v = jnp.split(kv, 2, axis=-1)

        def split_heads(t):
            return t.reshape(t.shape[0], t.shape[1], HEADS, DIM_HEAD).transpose(0, 2, 1, 3)
        q, k, v = map(split_heads, (q, k, v))
        nk = jnp.broadcast_to(null_kv[0], (b, HEADS, 1, DIM_HEAD))
        nv = jnp.broadcast_to(null_kv[1], (b, HEADS, 1, DIM_HEAD))
        k = jnp.concatenate([nk, k], axis=2)
        v = jnp.concatenate([nv, v], axis=2)
        q = l2norm(q) * q_scale
        k = l2norm(k) * k_scale
        sim = jnp.einsum('bhid,bhjd->bhij', q, k) * SCALE
        max_neg = -jnp.finfo(sim.dtype).max
        m = jnp.pad(mask, ((0, 0), (1, 0)), constant_values=True)[:, None, None, :]
        sim = jnp.where(m, sim, max_neg)
        attn = jax.nn.softmax(sim.astype(jnp.float32), axis=-1).astype(sim.dtype)
        out = jnp.einsum('bhij,bhjd->bhid', attn, v)
        out = out.transpose(0, 2, 1, 3).reshape(b, n, INNER)
        out = jnp.einsum('bne,ed->bnd', out, Wo)
        return stable_layernorm(out, g_out)

    def _L1_ffn_ref(x, norm1_w, norm2_w, Wq, Wdkv, Wuk, Wuv, Wo, ln_g, ln_b, gate_w, gate_b, W1, b1, W2, b2):
        import jax, jax.numpy as jnp
        import numpy as np
        D_MODEL = 128
        N_HEADS = 16
        HEAD_DIM = D_MODEL // N_HEADS
        KV_LATENT = 64
        N_EXPERTS = 4
        D_HIDDEN = 4 * D_MODEL
        B, T = (2, 128)

        def rmsnorm(x, w, eps=1e-06):
            return w * (x * jax.lax.rsqrt(jnp.mean(x * x, axis=-1, keepdims=True) + eps))

        def layernorm(x, g, b, eps=1e-05):
            mu = jnp.mean(x, axis=-1, keepdims=True)
            var = jnp.mean((x - mu) ** 2, axis=-1, keepdims=True)
            return (x - mu) * jax.lax.rsqrt(var + eps) * g + b

        def apply_rope(x):
            t, d = (x.shape[2], x.shape[3])
            half = d // 2
            pos = jnp.arange(t, dtype=x.dtype)[:, None]
            inv_freq = 1.0 / 10000.0 ** (jnp.arange(half, dtype=x.dtype) / half)
            ang = pos * inv_freq[None, :]
            sin, cos = (jnp.sin(ang), jnp.cos(ang))
            x1, x2 = (x[..., :half], x[..., half:])
            return jnp.concatenate([x1 * cos - x2 * sin, x1 * sin + x2 * cos], axis=-1)

        def mla_attention(x, Wq, Wdkv, Wuk, Wuv, Wo, ln_g, ln_b):
            b, t, _ = x.shape
            q = (x @ Wq.T).reshape(b, t, N_HEADS, HEAD_DIM).transpose(0, 2, 1, 3)
            latent = layernorm(x @ Wdkv.T, ln_g, ln_b)
            k = (latent @ Wuk.T).reshape(b, t, N_HEADS, HEAD_DIM).transpose(0, 2, 1, 3)
            v = (latent @ Wuv.T).reshape(b, t, N_HEADS, HEAD_DIM).transpose(0, 2, 1, 3)
            q = apply_rope(q)
            k = apply_rope(k)
            scores = jnp.einsum('bhqd,bhkd->bhqk', q, k) / np.sqrt(HEAD_DIM)
            causal = jnp.tril(jnp.ones((t, t), dtype=bool))
            scores = jnp.where(causal, scores, -jnp.inf)
            attn = jax.nn.softmax(scores, axis=-1)
            out = jnp.einsum('bhqk,bhkd->bhqd', attn, v).transpose(0, 2, 1, 3).reshape(b, t, D_MODEL)
            return out @ Wo.T

        def moe(x, gate_w, gate_b, W1, b1, W2, b2):
            logits = x @ gate_w.T + gate_b
            top = jnp.argmax(logits, axis=-1)
            onehot = jax.nn.one_hot(top, N_EXPERTS, dtype=x.dtype)
            h = jax.nn.relu(jnp.einsum('btd,ehd->bteh', x, W1) + b1)
            y = jnp.einsum('bteh,edh->bted', h, W2) + b2
            return jnp.einsum('bted,bte->btd', y, onehot)
        x = x + mla_attention(rmsnorm(x, norm1_w), Wq, Wdkv, Wuk, Wuv, Wo, ln_g, ln_b)
        x = x + moe(rmsnorm(x, norm2_w), gate_w, gate_b, W1, b1, W2, b2)
        return x

    def _L2_xattn_ref(x, y, Wq, bq, Wkv, bkv, Wo, bo):
        import jax, jax.numpy as jnp
        import numpy as np
        N_HEADS = 16
        b, l, d = x.shape
        m = y.shape[1]
        h = N_HEADS
        dh = d // h
        q = (jnp.einsum('bld,ed->ble', x, Wq) + bq).reshape(b, l, h, dh)
        kv = (jnp.einsum('bmc,ec->bme', y, Wkv) + bkv).reshape(b, m, h, 2 * dh)
        k, v = (kv[..., :dh], kv[..., dh:])
        scale = 1.0 / jnp.sqrt(jnp.asarray(dh, x.dtype))
        att = jax.nn.softmax(jnp.einsum('blhd,bmhd->blmh', q, k) * scale, axis=2)
        out = jnp.einsum('blmh,bmhd->blhd', att, v).reshape(b, l, d)
        return jnp.einsum('bld,ed->ble', out, Wo) + bo

    def _L2_ffn_ref(x, gate_w, w_gate, w_up, w_down, sw_gate, sw_up, sw_down):
        import jax, jax.numpy as jnp
        import numpy as np
        B, L, D = (4, 128, 128)
        E, H, K = (16, 64, 8)
        EPS = 1e-12

        def _l2norm(v, axis=-1):
            n = jnp.sqrt(jnp.sum(v * v, axis=axis, keepdims=True))
            return v / jnp.maximum(n, EPS)
        if __name__ == '__main__':
            out = reference(**setup_inputs())
            print(out.shape)
        b, l, d = x.shape
        xf = x.reshape(-1, d)
        logits = _l2norm(xf) @ _l2norm(gate_w).T
        scores = jax.nn.sigmoid(logits)
        topk_scores, topk_idx = jax.lax.top_k(scores, K)
        topk_w = topk_scores / jnp.sum(topk_scores, axis=-1, keepdims=True)
        combine = jnp.sum(jax.nn.one_hot(topk_idx, E, dtype=xf.dtype) * topk_w[..., None], axis=1)
        g = jnp.einsum('nd,edh->neh', xf, w_gate)
        u = jnp.einsum('nd,edh->neh', xf, w_up)
        y = jnp.einsum('neh,ehd->ned', jax.nn.silu(g) * u, w_down)
        routed = jnp.einsum('ned,ne->nd', y, combine)
        shared = jax.nn.silu(xf @ sw_gate) * (xf @ sw_up) @ sw_down
        return (routed + shared).reshape(b, l, d)

    def _L3_xattn_ref(x, latents, mask, ln_x_g, ln_x_b, ln_l_g, ln_l_b, qn_g, kn_g, Wq, Wkv, Wlkv, Wo, bo):
        import jax, jax.numpy as jnp
        import numpy as np
        DIM_IN, DIM_LAT, DIM_HEAD = (96, 128, 64)
        INNER = max(DIM_LAT, DIM_IN)
        HEADS = INNER // DIM_HEAD
        SCALE = DIM_HEAD ** (-0.5)
        RMS_EPS = 1e-08
        LN_EPS = 1e-05

        def layernorm(x, g, b):
            mu = jnp.mean(x, axis=-1, keepdims=True)
            var = jnp.mean((x - mu) ** 2, axis=-1, keepdims=True)
            return (x - mu) * jax.lax.rsqrt(var + LN_EPS) * g + b

        def rmsnorm(x, gamma):
            norm = jnp.sqrt(jnp.sum(x * x, axis=-1, keepdims=True)) * x.shape[-1] ** (-0.5)
            return x / jnp.maximum(norm, RMS_EPS) * gamma
        b, n, _ = x.shape
        m = latents.shape[1]
        xn = layernorm(x, ln_x_g, ln_x_b)
        ln = layernorm(latents, ln_l_g, ln_l_b)
        q = ln @ Wq.T
        kv = jnp.concatenate([xn @ Wkv.T, ln @ Wlkv.T], axis=1)
        k, v = (kv[..., :INNER], kv[..., INNER:])
        split_heads = lambda t: t.reshape(t.shape[0], t.shape[1], HEADS, DIM_HEAD).transpose(0, 2, 1, 3)
        q, k, v = (split_heads(q), split_heads(k), split_heads(v))
        qn = rmsnorm(q, qn_g) * SCALE
        kn = rmsnorm(k, kn_g)
        attn = jnp.einsum('bhid,bhjd->bhij', qn, kn)
        full_mask = jnp.pad(mask, ((0, 0), (0, m)), constant_values=True)
        attn = jnp.where(full_mask[:, None, None, :], attn, -jnp.finfo(attn.dtype).max)
        attn = jax.nn.softmax(attn, axis=-1)
        out = jnp.einsum('bhij,bhjd->bhid', attn, v)
        out = out.transpose(0, 2, 1, 3).reshape(b, m, INNER)
        return out @ Wo.T + bo

    def _L3_ffn_ref(hidden_states, gate_w, w1, w2, w3):
        import jax, jax.numpy as jnp
        import numpy as np
        E, K, D, H = (8, 2, 128, 256)
        B, S = (1, 128)

        def _grouped_swiglu(x_sorted, counts, w1, w2, w3):
            if hasattr(jax.lax, 'ragged_dot'):
                gs = counts.astype(jnp.int32)
                h = jax.nn.silu(jax.lax.ragged_dot(x_sorted, w1, gs)) * jax.lax.ragged_dot(x_sorted, w3, gs)
                return jax.lax.ragged_dot(h, w2, gs)
            pos = jnp.arange(x_sorted.shape[0])
            eid = jnp.searchsorted(jnp.cumsum(counts), pos, side='right')
            out = jnp.zeros((x_sorted.shape[0], w2.shape[-1]), x_sorted.dtype)
            for e in range(w1.shape[0]):
                xm = jnp.where((eid == e)[:, None], x_sorted, 0.0)
                he = jax.nn.silu(xm @ w1[e]) * (xm @ w3[e])
                out = out + he @ w2[e]
            return out
        x = hidden_states.reshape(-1, D)
        N = x.shape[0]
        scores = jax.nn.softmax(x @ gate_w.T, axis=-1)
        top_scores, sel = jax.lax.top_k(scores, K)
        sel_flat = sel.T.reshape(-1)
        scores_flat = top_scores.T.reshape(-1)
        order = jnp.argsort(sel_flat, stable=True)
        tok_sorted = order % N
        scores_sorted = scores_flat[order]
        counts = jnp.bincount(sel_flat, length=E)
        x_sorted = x[tok_sorted]
        y = _grouped_swiglu(x_sorted, counts, w1, w2, w3)
        weighted = y * scores_sorted[:, None]
        out = jnp.zeros((N, D), x.dtype).at[tok_sorted].add(weighted)
        return out.reshape(hidden_states.shape)
    x = x + jnp.tanh(g_xattn[0]) * _L0_xattn_ref(_layernorm(x, axis=-1), ctx_768, mask_BxS_bk0, L0_xattn_Wq, L0_xattn_Wkv)
    x = x + jnp.tanh(g_ffn[0]) * _L0_ffn_ref(_layernorm(x, axis=-1), L0_ffn_w_gate, L0_ffn_w_up, L0_ffn_w_down)
    x = x + jnp.tanh(g_xattn[1]) * _L1_xattn_ref(_layernorm(x, axis=-1), ctx_768, mask_BxS2_bf1, L1_xattn_g_norm, L1_xattn_Wq, L1_xattn_Wkv, L1_xattn_null_kv, L1_xattn_q_scale, L1_xattn_k_scale, L1_xattn_Wo, L1_xattn_g_out)
    x = x + jnp.tanh(g_ffn[1]) * _L1_ffn_ref(_layernorm(x, axis=-1), L1_ffn_norm1_w, L1_ffn_norm2_w, L1_ffn_Wq, L1_ffn_Wdkv, L1_ffn_Wuk, L1_ffn_Wuv, L1_ffn_Wo, L1_ffn_ln_g, L1_ffn_ln_b, L1_ffn_gate_w, L1_ffn_gate_b, L1_ffn_W1, L1_ffn_b1, L1_ffn_W2, L1_ffn_b2)
    x = x + jnp.tanh(g_xattn[2]) * _L2_xattn_ref(_layernorm(x, axis=-1), ctx_768, L2_xattn_Wq, L2_xattn_bq, L2_xattn_Wkv, L2_xattn_bkv, L2_xattn_Wo, L2_xattn_bo)
    x = x + jnp.tanh(g_ffn[2]) * _L2_ffn_ref(_layernorm(x, axis=-1), L2_ffn_gate_w, L2_ffn_w_gate, L2_ffn_w_up, L2_ffn_w_down, L2_ffn_sw_gate, L2_ffn_sw_up, L2_ffn_sw_down)
    x = x + jnp.tanh(g_xattn[3]) * _L3_xattn_ref(ctx_768, _layernorm(x, axis=-1), mask_BxS2_bk0, L3_xattn_ln_x_g, L3_xattn_ln_x_b, L3_xattn_ln_l_g, L3_xattn_ln_l_b, L3_xattn_qn_g, L3_xattn_kn_g, L3_xattn_Wq, L3_xattn_Wkv, L3_xattn_Wlkv, L3_xattn_Wo, L3_xattn_bo)
    x = x + jnp.tanh(g_ffn[3]) * _L3_ffn_ref(_layernorm(x, axis=-1), L3_ffn_gate_w, L3_ffn_w1, L3_ffn_w2, L3_ffn_w3)
    return x

_drawn_inputs = setup_inputs


def setup_inputs(seed=0):
    import zlib

    import numpy as np

    out = dict(_drawn_inputs(seed))
    spreads = {'L1_xattn_g_norm': (1.0, 0.2),
     'L1_xattn_q_scale': (1.0, 0.2),
     'L1_xattn_k_scale': (1.0, 0.2),
     'L1_xattn_g_out': (1.0, 0.2),
     'L1_ffn_norm1_w': (1.0, 0.2),
     'L1_ffn_norm2_w': (1.0, 0.2),
     'L1_ffn_ln_g': (1.0, 0.2),
     'L1_ffn_ln_b': (0.0, 0.1),
     'L1_ffn_gate_b': (0.0, 0.1),
     'L1_ffn_b1': (0.0, 0.274),
     'L1_ffn_b2': (0.0, 0.1),
     'L3_xattn_ln_x_g': (1.0, 0.6),
     'L3_xattn_ln_x_b': (0.0, 0.8),
     'L3_xattn_ln_l_g': (1.0, 0.2),
     'L3_xattn_ln_l_b': (0.0, 0.319),
     'L3_xattn_qn_g': (1.0, 0.6),
     'L3_xattn_kn_g': (1.0, 0.6),
     'L3_xattn_bo': (0.0, 0.268)}
    factors = {'L2_xattn_bq': 60.201, 'L2_xattn_bkv': 8.0, 'L2_xattn_bo': 8.0}
    for name, (base, spread) in spreads.items():
        noise = np.random.default_rng([zlib.crc32(name.encode()), seed]).standard_normal(out[name].shape)
        drawn = base * np.exp(spread * noise) if base else spread * noise
        out[name] = jnp.asarray(drawn.astype(out[name].dtype))
    for name, factor in factors.items():
        out[name] = (out[name] * factor).astype(out[name].dtype)
    return out
```

```python
from contextlib import ExitStack

import concourse.bass as bass
from concourse import mybir

F32 = mybir.dt.float32
BF16 = mybir.dt.bfloat16
U8 = mybir.dt.uint8
ALU = mybir.AluOpType
ACT = mybir.ActivationFunctionType
AX_X = mybir.AxisListType.X

P = 128
B, S, D = 8, 256, 128
C = 96
T = S // P
ROUND = 12582912.0
HIDE = -1.0e30

SMAX0, ST0, OUT0, MISC = 0, 2, 4, 6


class Signal:

    def __init__(self, sem, base, per):
        self.sem, self.base, self.per = sem, base, per

    def after(self, b, k=None):
        return b * self.per + (self.base + (self.per if k is None else k))

    def before(self, b):
        return b * self.per + self.base


class Chain:

    def __init__(self, rising):
        self.sem, self.rising = rising.sem, rising
        self.b, self.k = 0, 0

    def start(self, b):
        assert self.k in (0, self.rising.per), (self.sem, self.k, self.rising.per)
        self.b, self.k = b, 0

    def next(self):
        self.k += 1
        assert self.k <= self.rising.per, "more steps than the chain's semaphore has in a batch"
        return self.reached()

    def reached(self):
        return self.rising.after(self.b, self.k)


class Core:

    def __init__(self, nc, ctx, arrays):
        self.nc, self.ctx, self.dram = nc, ctx, arrays
        self.sems, self.totals = {}, {}

    def sem(self, name):
        if name not in self.sems:
            self.sems[name] = self.ctx.enter_context(self.nc.semaphore(name))
            self.totals[name] = 0
        return self.sems[name]

    def rising(self, name, per):
        sem = self.sem(name)
        s = Signal(sem, self.totals[name], per)
        self.totals[name] += B * per
        return s

    def sb(self, name, shape, dt=F32):
        return self.ctx.enter_context(self.nc.sbuf_tensor(name, shape, dt))


def settled(eng, K):
    eng.sem_inc(K.sem("passed"), 1)


def software_pipeline(eng, prep, main):
    prep(0, 0)
    with eng.Fori(0, B // 2 - 1) as i:
        prep(2 * i + 1, 1)
        main(2 * i, 0)
        prep(2 * i + 2, 0)
        main(2 * i + 1, 1)
    prep(B - 1, 1)
    main(B - 2, 0)
    main(B - 1, 1)


def cols(tensor, b, n=S):
    return tensor[:, bass.ds(b * n, n)]



def norm_tiles(K):
    st = K.sb("ln_stats", [P, 2, T, 6])
    mv = K.sb("ln_mean_var", [P, 2, T, 2])
    ve = K.sb("ln_var_eps", [P, 2, T])
    rs = K.sb("ln_rstd", [P, 2, T])
    xn = K.sb("xn", [P, 2, T, D])
    xnT = K.sb("xnT", [P, 2, T * P])
    return dict(st=st, mv=mv, ve=ve, rs=rs, xn=xn, xnT=xnT)


def ln_signals(K, turned=True):
    names = dict(stats="ln_stats_ready", rstd="ln_rstd_ready", xn="xn_ready")
    if turned:
        names.update(xnT_ps="xnT_in_psum", xnT="xnT_ready")
    return {k: K.rising(name, 1) for k, name in names.items()}


LN_STEPS = 2 * T


def dve_layernorm(K, dve, chain, s, b, u):
    nc, n = K.nc, K.norm
    for t in range(T):
        settled(dve, K)
        nc.vector.bn_stats(n["st"][:, u, t, :], K.X[:, bass.ds(b * S + t * P, P)]).then_inc(chain.sem, 1)
        chain.next()
    dve.wait_ge(chain.sem, chain.reached())
    settled(dve, K)
    nc.vector.bn_aggr(n["mv"][:, u, 0, :], n["st"][:, u, 0, :]).then_inc(chain.sem, 1)
    chain.next()
    nc.vector.bn_aggr(n["mv"][:, u, 1, :], n["st"][:, u, 1, :]).then_inc(s["stats"].sem, 1)
    dve.wait_ge(s["rstd"].sem, s["rstd"].after(b))
    nc.vector.tensor_scalar(n["xn"][:, u, 0, :], K.X[:, bass.ds(b * S, P)], n["mv"][:, u, 0, 0:1],
                            n["rs"][:, u, 0:1], ALU.subtract, ALU.mult).then_inc(chain.sem, 1)
    chain.next()
    nc.vector.tensor_scalar(n["xn"][:, u, 1, :], K.X[:, bass.ds(b * S + P, P)], n["mv"][:, u, 1, 0:1],
                            n["rs"][:, u, 1:2], ALU.subtract, ALU.mult).then_inc(s["xn"].sem, 1)


def pool_rstd(K, pool, s, b, u, mask=None):
    nc, n = K.nc, K.norm
    pool.wait_ge(s["stats"].sem, s["stats"].after(b))
    pt, ps = K.sem("pool_step"), s["pool_step"]
    nc.gpsimd.tensor_tensor(n["ve"][:, u, :], n["mv"][:, u, :, 1], K.eps5[:, 0:T], ALU.add).then_inc(pt, 1)
    pool.wait_ge(pt, ps.after(b, 1))
    if mask is None:
        nc.gpsimd.tensor_tensor(n["rs"][:, u, :], n["ve"][:, u, :], K.neghalf[:, 0:T], ALU.pow) \
            .then_inc(s["rstd"].sem, 1)
        return 1
    nc.gpsimd.tensor_tensor(n["ve"][:, u, :], n["ve"][:, u, :], K.neghalf[:, 0:T], ALU.pow).then_inc(pt, 1)
    pool.wait_ge(pt, ps.after(b, 2))
    nc.gpsimd.tensor_tensor(n["rs"][:, u, :], n["ve"][:, u, :], mask[:, bass.ds(b * T, T)], ALU.mult) \
        .then_inc(s["rstd"].sem, 1)
    return 2


def pe_xn_transposed(K, pe, s, b, u, bank):
    pe.wait_ge(s["xn"].sem, s["xn"].after(b))
    for t in range(T):
        mm = K.nc.tensor.transpose(K.PS[:, bank, t * P:(t + 1) * P], K.norm["xn"][:, u, t, :], K.ident[:])
    mm.then_inc(s["xnT_ps"].sem, 1)


def act_xn_transposed(K, act, s, b, u, bank, scale=1.0):
    act.wait_ge(s["xnT_ps"].sem, s["xnT_ps"].after(b))
    K.nc.scalar.activation(K.norm["xnT"][:, u, :], K.PS[:, bank, 0:S], ACT.Copy if isinstance(scale, float) else ACT.Identity, scale=scale) \
        .then_inc(s["xnT"].sem, 1)



H, DH, E = 16, 8, 32
G = 4
HG = H // G


def head_tiles(K, ctx, name):
    def sb(what, shape, dt=F32):
        return ctx.enter_context(K.nc.sbuf_tensor(name + "_" + what, shape, dt))

    h = {}
    h["qs"] = sb("q_scaled", [P, 2, T * D])
    h["ks"] = sb("k_rows", [P, 2, T * D])
    h["qe"] = sb("q_expanded", [P, 2, T * H, E], BF16)
    h["ke"] = sb("k_expanded", [P, 2, T * H, E], BF16)
    h["ve"] = sb("v_with_ones", [P, 2, T * H, E])
    h["qT"] = sb("qT", [P, 2, G, S], BF16)
    h["kT"] = sb("kT", [P, 2, G, S], BF16)
    h["nm"] = sb("minus_max", [P, 2, T, H])
    h["nr"] = sb("minus_max_rest", [P, T, H])
    h["p"] = sb("probs", [P, 2, 2 * S])
    h["oT"] = sb("outT", [P, G, S])
    h["rec"] = sb("inverse_sums", [P, T, H])
    h["o"] = sb("attention_out", [P, 2, T * D])
    return h


def dve_clear_heads(K, dve, name):
    nc, h, cleared = K.nc, K.heads, K.sem(name + "_zeroed_by_vector")
    nc.vector.memset(h["qe"][:], 0.0)
    nc.vector.memset(h["ke"][:], 0.0).then_inc(cleared, 1)
    dve.wait_ge(cleared, 1)
    nc.vector.memset(h["ke"][:, :, :, 24:27], 1.0)


def pool_clear_heads(K, pool, name):
    nc, h, cleared = K.nc, K.heads, K.sem(name + "_zeroed_by_gpsimd")
    nc.gpsimd.memset(h["ve"][:], 0.0).then_inc(cleared, 1)
    pool.wait_ge(cleared, 1)
    nc.gpsimd.memset(h["ve"][:, :, :, DH:DH + 1], 1.0)


def head_signals(K):
    names = dict(qs=1, ks=1, v=1, qe=1, ke=1, kT_ps=1, kT=1, qT_ps=1, qT=1, smax_ps=H, smax=H,
                 qm=1, qmT_ps=1, qmT=1, st_ps=H, p=H, oT_ps=2, ob=1, out_banks=1)
    return {k: K.rising("heads_" + k, n) for k, n in names.items()}


def pool_split(K, pool, s, b, u):
    nc, h = K.nc, K.heads
    ps = s["pool_step"]
    ke = h["ke"][:, u].rearrange("p h (c e) -> p h c e", e=DH)
    qe = h["qe"][:, u].rearrange("p h (c e) -> p h c e", e=DH)
    ks = h["ks"][:, u].rearrange("p (h e) -> p h e", e=DH)
    qs = h["qs"][:, u].rearrange("p (h e) -> p h e", e=DH)
    pool.wait_ge(s["ks"].sem, s["ks"].after(b))
    settled(pool, K)
    k0 = s["k0"]
    nc.gpsimd.tensor_copy(ke[:, :, 0], ks).then_inc(ps.sem, 1)
    pool.wait_ge(ps.sem, ps.after(b, k0 + 1))
    nc.gpsimd.tensor_tensor(ke[:, :, 1], ks, ke[:, :, 0], ALU.subtract).then_inc(ps.sem, 1)
    nc.gpsimd.tensor_copy(ke[:, :, 2], ke[:, :, 0]).then_inc(s["ke"].sem, 1)
    pool.wait_ge(s["qs"].sem, s["qs"].after(b))
    settled(pool, K)
    nc.gpsimd.tensor_copy(qe[:, :, 0], qs).then_inc(ps.sem, 1)
    pool.wait_ge(ps.sem, ps.after(b, k0 + 3))
    nc.gpsimd.tensor_tensor(qe[:, :, 2], qs, qe[:, :, 0], ALU.subtract).then_inc(ps.sem, 1)
    nc.gpsimd.tensor_copy(qe[:, :, 1], qe[:, :, 0]).then_inc(s["qe"].sem, 1)
    return 4


def pe_turn_heads(K, pe, src, u, bank):
    out = K.PS[:, bank, :].bitcast(BF16)
    for t in range(T):
        for g in range(G):
            mm = K.nc.tensor.transpose(out[:, g * S + t * P:g * S + (t + 1) * P],
                                       src[:, u, t * H + g * HG:t * H + (g + 1) * HG, :].rearrange("p h e -> p (h e)"),
                                       K.identb[:])
    return mm


def pe_turn_k_and_q(K, pe, s, b, u):
    h = K.heads
    pe.wait_ge(s["ke"].sem, s["ke"].after(b))
    pe_turn_heads(K, pe, h["ke"], u, MISC).then_inc(s["kT_ps"].sem, 1)
    pe.wait_ge(s["qe"].sem, s["qe"].after(b))
    pe_turn_heads(K, pe, h["qe"], u, MISC + 1).then_inc(s["qT_ps"].sem, 1)


def act_copy_kT(K, act, s, b, u):
    act.wait_ge(s["kT_ps"].sem, s["kT_ps"].after(b))
    K.nc.scalar.activation(K.heads["kT"][:, u].rearrange("p g n -> p (g n)"), K.PS[:, MISC, :].bitcast(BF16), ACT.Copy) \
        .then_inc(s["kT"].sem, 1)


def dve_copy_qT(K, dve, s, b, u):
    dve.wait_ge(s["qT_ps"].sem, s["qT_ps"].after(b))
    K.nc.vector.tensor_copy(K.heads["qT"][:, u].rearrange("p g n -> p (g n)"), K.PS[:, MISC + 1, :].bitcast(BF16)) \
        .then_inc(s["qT"].sem, 1)


def pe_scores(K, pe, s, b, u, n, causal):
    nc, h = K.nc, K.heads
    g, j = n // HG, n % HG
    bank = SMAX0 + n % 2
    r = slice(E * j, E * (j + 1))
    if n == 0:
        pe.wait_ge(s["kT"].sem, s["kT"].after(b))
        pe.wait_ge(s["qT"].sem, s["qT"].after(b))
    if n >= 2:
        pe.wait_ge(s["smax"].sem, s["smax"].after(b, n - 1))
    for t in range(T):
        width = P * (t + 1) if causal else S
        o = K.PS[:, bank, t * S:t * S + width]
        if causal:
            nc.tensor.matmul(K.PS[:, bank, t * S:(t + 1) * S], K.identb[:], K.hide_q[:, t, :], start=True, stop=True)
        mm = nc.tensor.matmul(o, h["qT"][r, u, g, t * P:(t + 1) * P], h["kT"][r, u, g, 0:width],
                              start=not causal, stop=True, skip_group_check=causal)
    mm.then_inc(s["smax_ps"].sem, 1)


def dve_row_max(K, dve, s, b, u, n):
    dve.wait_ge(s["smax_ps"].sem, s["smax_ps"].after(b, n + 1))
    K.nc.vector.tensor_reduce(K.heads["nm"][:, u, :, n], K.PS[:, SMAX0 + n % 2, :].rearrange("p (t n) -> p t n", t=T),
                              AX_X, ALU.max, negate=True).then_inc(s["smax"].sem, 1)


def dve_place_max(K, dve, chain, s, b, u):
    nc, h = K.nc, K.heads
    qe = h["qe"][:, u].rearrange("p (t h) e -> p t h e", t=T)
    dve.wait_ge(s["smax"].sem, s["smax"].after(b))
    nc.vector.tensor_copy(qe[:, :, :, 24], h["nm"][:, u]).then_inc(chain.sem, 1)
    dve.wait_ge(chain.sem, chain.next())
    nc.vector.tensor_tensor(h["nr"][:], h["nm"][:, u], qe[:, :, :, 24], ALU.subtract).then_inc(chain.sem, 1)
    dve.wait_ge(chain.sem, chain.next())
    nc.vector.tensor_copy(qe[:, :, :, 25], h["nr"][:]).then_inc(chain.sem, 1)
    dve.wait_ge(chain.sem, chain.next())
    nc.vector.tensor_tensor(qe[:, :, :, 26], h["nr"][:], qe[:, :, :, 25], ALU.subtract).then_inc(s["qm"].sem, 1)


PLACE_MAX_STEPS = 3


def pe_turn_q_with_max(K, pe, s, b, u):
    pe.wait_ge(s["qm"].sem, s["qm"].after(b))
    pe_turn_heads(K, pe, K.heads["qe"], u, MISC).then_inc(s["qmT_ps"].sem, 1)


def act_copy_qmT(K, act, s, b, u):
    act.wait_ge(s["qmT_ps"].sem, s["qmT_ps"].after(b))
    K.nc.scalar.activation(K.heads["qT"][:, u].rearrange("p g n -> p (g n)"), K.PS[:, MISC, :].bitcast(BF16), ACT.Copy) \
        .then_inc(s["qmT"].sem, 1)


def pe_scores_T(K, pe, s, b, u, n, causal):
    nc, h = K.nc, K.heads
    g, j = n // HG, n % HG
    bank = ST0 + n % 2
    r = slice(E * j, E * (j + 1))
    if n == 0:
        pe.wait_ge(s["qmT"].sem, s["qmT"].after(b))
    if not causal:
        for kt in range(T):
            mm = nc.tensor.matmul(K.PS[:, bank, kt * S:(kt + 1) * S], h["kT"][r, u, g, kt * P:(kt + 1) * P],
                                  h["qT"][r, u, g, :], start=True, stop=True)
    else:
        nc.tensor.matmul(K.PS[:, bank, 0:S], h["kT"][r, u, g, 0:P], h["qT"][r, u, g, :], start=True, stop=True)
        nc.tensor.matmul(K.PS[:, bank, 0:P], K.identb[:], K.hide_kT[:], start=False, stop=True, skip_group_check=True)
        nc.tensor.matmul(K.PS[:, bank, S:S + P], h["kT"][r, u, g, P:S], h["qT"][r, u, g, P:S], start=True, stop=False)
        mm = nc.tensor.matmul(K.PS[:, bank, S:S + P], K.identb[:], K.hide_kT[:], start=False, stop=True)
    mm.then_inc(s["st_ps"].sem, 1)


def act_probs(K, act, s, b, u, n, causal):
    act.wait_ge(s["st_ps"].sem, s["st_ps"].after(b, n + 1))
    w = S + P if causal else 2 * S
    K.nc.scalar.activation(K.heads["p"][:, n % 2, 0:w], K.PS[:, ST0 + n % 2, 0:w], ACT.Exp).then_inc(s["p"].sem, 1)


def pe_mix(K, pe, s, b, u, n, causal):
    nc, h = K.nc, K.heads
    g, j = n // HG, n % HG
    if n == 0:
        pe.wait_ge(s["out_banks"].sem, s["out_banks"].before(b))
        pe.wait_ge(s["v"].sem, s["v"].after(b))
    pe.wait_ge(s["p"].sem, s["p"].after(b, n + 1))
    for kt in range(T):
        q0 = kt * P if causal else 0
        mm = nc.tensor.matmul(K.PS[E * j:E * (j + 1), OUT0 + g // 2, (g % 2) * S + q0:(g % 2 + 1) * S],
                              h["ve"][:, u, kt * H + n, :], h["p"][:, n % 2, kt * S:(kt + 1) * S - q0],
                              start=kt == 0, stop=kt == T - 1, skip_group_check=causal)
    if n % (H // 2) == H // 2 - 1:
        mm.then_inc(s["oT_ps"].sem, 1)


def copy_outT(K, eng, s, b, half):
    eng.wait_ge(s["oT_ps"].sem, s["oT_ps"].after(b, half + 1))
    dst = K.heads["oT"][:, 2 * half:2 * half + 2, :].rearrange("p g n -> p (g n)")
    if half == 0:
        K.nc.vector.tensor_copy(dst, K.PS[:, OUT0, :]).then_inc(s["oT0"].sem, 1)
    else:
        K.nc.scalar.activation(dst, K.PS[:, OUT0 + 1, :], ACT.Copy).then_inc(s["oT1"].sem, 1)


def pe_turn_out(K, pe, s, b, u):
    pe.wait_ge(s["oT0"].sem, s["oT0"].after(b))
    pe.wait_ge(s["oT1"].sem, s["oT1"].after(b))
    for t in range(T):
        for g in range(G):
            mm = K.nc.tensor.transpose(K.PS[:, OUT0 + t, g * P:(g + 1) * P], K.heads["oT"][:, g, t * P:(t + 1) * P],
                                       K.ident[:])
    mm.then_inc(s["ob"].sem, 1)


def dve_normalise(K, dve, chain, s, b, u, signal):
    nc, h = K.nc, K.heads
    dve.wait_ge(s["ob"].sem, s["ob"].after(b))
    ob = K.PS[:, OUT0:OUT0 + T, :].rearrange("p t (h e) -> p t h e", e=E)
    nc.vector.reciprocal(h["rec"][:], ob[:, :, :, DH]).then_inc(chain.sem, 1)
    dve.wait_ge(chain.sem, chain.next())
    nc.vector.tensor_tensor(h["o"][:, u].rearrange("p (t h e) -> p t h e", t=T, e=DH), ob[:, :, :, 0:DH],
                            h["rec"][:].unsqueeze(3).broadcast_to([P, T, H, DH]), ALU.mult) \
        .then_inc(signal.sem, 1)


NORMALISE_STEPS = 1


def head_pipeline(eng, prep, fused, first, finish):
    prep(0, 0)
    first(0, 0)

    def both(b, u):
        prep(b + 1, 1 - u)
        fused(b, u, True)
        finish(b, u)

    with eng.Fori(0, B // 2 - 1) as i:
        both(2 * i, 0)
        both(2 * i + 1, 1)
    both(B - 2, 0)
    fused(B - 1, 1, False)
    finish(B - 1, 1)


def cross_attention_layer(K, name, layer, wq, wkv, mask=None, bias=None, wo=None, loaded=()):
    nc = K.nc
    h = K.heads
    s = dict(ln_signals(K), **head_signals(K))
    for extra in ("oT0", "oT1") if wo is None else ("oT0", "oT1", "o", "woT_ps", "woT", "wo_ps"):
        s[extra] = K.rising("heads_" + extra, 1)
    s["ctx"] = K.rising("ctx_tile_ready", 1)
    s["q_ps"], s["kv_ps"] = K.rising("q_in_psum", 1), K.rising("kv_in_psum", 1)
    s["k0"] = 1 + (mask is not None)
    s["pool_step"] = K.rising("pool_step", s["k0"] + 4)
    plain = bias is None
    s["prep_step"] = K.rising("vector_prep_step", LN_STEPS + PLACE_MAX_STEPS)
    s["finish_step"] = K.rising("vector_finish_step", NORMALISE_STEPS + 1)
    scale = DH ** -0.5
    tg = K.gates[:, layer:layer + 1]

    with nc.Block() as block:

        @block.gpsimd
        def _(pool):
            def prep(b, u):
                pool_rstd(K, pool, s, b, u, mask)
                settled(pool, K)
                nc.gpsimd.tensor_copy(K.ctx_tile[:, u, :], K.ctxT[:, bass.ds(b * S, S)]).then_inc(s["ctx"].sem, 1)
                pool_split(K, pool, s, b, u)

            def nothing(b, u, more=None):
                pass
            head_pipeline(pool, prep, nothing, nothing, nothing)

        @block.vector
        def _(dve):
            chain = Chain(s["prep_step"])
            ending = Chain(s["finish_step"])
            if not plain:
                for value, sem in loaded:
                    dve.wait_ge(sem, value)
                nc.vector.tensor_scalar(bias["q"][:], bias["q"][:], scale, None, ALU.mult).then_inc(K.sem("q_bias_scaled"), 1)
                dve.wait_ge(K.sem("q_bias_scaled"), 1)

            def prep(b, u):
                chain.start(b)
                dve_layernorm(K, dve, chain, s, b, u)
                dve.wait_ge(s["q_ps"].sem, s["q_ps"].after(b))
                if plain:
                    nc.vector.tensor_scalar(h["qs"][:, u], K.PS[:, MISC + 1, 0:S], scale, None, ALU.mult) \
                        .then_inc(s["qs"].sem, 1)
                else:
                    nc.vector.scalar_tensor_tensor(
                        h["qs"][:, u].rearrange("p (t d) -> p t d", t=T), K.PS[:, MISC + 1, 0:S].rearrange("p (t d) -> p t d", t=T),
                        scale, bias["q"][:].unsqueeze(1).broadcast_to([P, T, D]), ALU.mult, ALU.add).then_inc(s["qs"].sem, 1)
                    dve.wait_ge(s["kv_ps"].sem, s["kv_ps"].after(b))
                    kv = K.PS[:, MISC, :].rearrange("p (t n) -> p t n", t=T)
                    nc.vector.tensor_tensor(
                        h["ve"][:, u, :, 0:DH].rearrange("p (t h) e -> p t h e", t=T), kv[:, :, D:2 * D].rearrange("p t (h e) -> p t h e", e=DH),
                        bias["v"][:].rearrange("p (h e) -> p h e", e=DH).unsqueeze(1).broadcast_to([P, T, H, DH]), ALU.add) \
                        .then_inc(s["v"].sem, 1)
                    nc.vector.tensor_tensor(
                        h["ks"][:, u].rearrange("p (t d) -> p t d", t=T), kv[:, :, 0:D],
                        bias["k"][:].unsqueeze(1).broadcast_to([P, T, D]), ALU.add).then_inc(s["ks"].sem, 1)
                dve_copy_qT(K, dve, s, b, u)

            def first(b, u):
                for n in range(H):
                    dve_row_max(K, dve, s, b, u, n)
                dve_place_max(K, dve, chain, s, b, u)

            def fused(b, u, more):
                for n in range(H):
                    if more:
                        dve_row_max(K, dve, s, b + 1, 1 - u, n)
                    if n == H - 4:
                        copy_outT(K, dve, s, b, 0)
                if more:
                    dve_place_max(K, dve, chain, s, b + 1, 1 - u)

            def finish(b, u):
                ending.start(b)
                end = s["out_banks"] if wo is None else s["o"]
                dve_normalise(K, dve, ending, s, b, u, end)
                x = cols(K.X, b)
                dve.wait_ge(end.sem, end.after(b))
                if wo is None:
                    nc.vector.scalar_tensor_tensor(x, h["o"][:, u], tg, x, ALU.mult, ALU.add).then_inc(ending.sem, 1)
                    dve.wait_ge(ending.sem, ending.next())
                else:
                    dve.wait_ge(s["wo_ps"].sem, s["wo_ps"].after(b))
                    nc.vector.tensor_tensor(h["o"][:, u].rearrange("p (t d) -> p t d", t=T),
                                            K.PS[:, OUT0 + 1, 0:S].rearrange("p (t d) -> p t d", t=T),
                                            bias["o"][:].unsqueeze(1).broadcast_to([P, T, D]), ALU.add) \
                        .then_inc(s["out_banks"].sem, 1)
                    dve.wait_ge(s["out_banks"].sem, s["out_banks"].after(b))
                    nc.vector.scalar_tensor_tensor(x, h["o"][:, u], tg, x, ALU.mult, ALU.add).then_inc(ending.sem, 1)
                    dve.wait_ge(ending.sem, ending.next())

            head_pipeline(dve, prep, fused, first, finish)

        @block.scalar
        def _(act):
            def prep(b, u):
                act_xn_transposed(K, act, s, b, u, MISC + 1)
                if plain:
                    act.wait_ge(s["kv_ps"].sem, s["kv_ps"].after(b))
                    kv = K.PS[:, MISC, :].rearrange("p (t n) -> p t n", t=T)
                    nc.scalar.activation(h["ve"][:, u, :, 0:DH].rearrange("p (t h) e -> p t h e", t=T),
                                         kv[:, :, D:2 * D].rearrange("p t (h e) -> p t h e", e=DH), ACT.Copy) \
                        .then_inc(s["v"].sem, 1)
                    nc.scalar.activation(h["ks"][:, u].rearrange("p (t d) -> p t d", t=T), kv[:, :, 0:D], ACT.Copy) \
                        .then_inc(s["ks"].sem, 1)
                act_copy_kT(K, act, s, b, u)

            def first(b, u):
                act_copy_qmT(K, act, s, b, u)

            def fused(b, u, more):
                for n in range(H):
                    act_probs(K, act, s, b, u, n, False)
                copy_outT(K, act, s, b, 1)
                if more:
                    act_copy_qmT(K, act, s, b + 1, 1 - u)

            def finish(b, u):
                if wo is not None:
                    act.wait_ge(s["woT_ps"].sem, s["woT_ps"].after(b))
                    nc.scalar.activation(K.norm["xnT"][:, u, :], K.PS[:, OUT0, 0:S], ACT.Copy).then_inc(s["woT"].sem, 1)

            head_pipeline(act, prep, fused, first, finish)

        @block.tensor
        def _(pe):
            for value, sem in loaded:
                pe.wait_ge(sem, value)

            def prep(b, u):
                pe_xn_transposed(K, pe, s, b, u, MISC + 1)
                pe.wait_ge(s["ctx"].sem, s["ctx"].after(b))
                pe.wait_ge(s["qmT"].sem, s["qmT"].before(b))
                for t in range(T):
                    mm = nc.tensor.matmul(K.PS[:, MISC, t * 2 * D:(t + 1) * 2 * D], K.ctx_tile[:, u, t * P:(t + 1) * P],
                                          wkv[:], start=True, stop=True)
                mm.then_inc(s["kv_ps"].sem, 1)
                pe.wait_ge(s["xnT"].sem, s["xnT"].after(b))
                for t in range(T):
                    mm = nc.tensor.matmul(K.PS[:, MISC + 1, t * D:(t + 1) * D], K.norm["xnT"][:, u, t * P:(t + 1) * P],
                                          wq[:], start=True, stop=True)
                mm.then_inc(s["q_ps"].sem, 1)
                pe_turn_k_and_q(K, pe, s, b, u)

            def first(b, u):
                for n in range(H):
                    pe_scores(K, pe, s, b, u, n, False)
                pe_turn_q_with_max(K, pe, s, b, u)

            def fused(b, u, more):
                for n in range(H):
                    pe_scores_T(K, pe, s, b, u, n, False)
                    if more:
                        pe_scores(K, pe, s, b + 1, 1 - u, n, False)
                    if n >= 1:
                        pe_mix(K, pe, s, b, u, n - 1, False)
                pe_mix(K, pe, s, b, u, H - 1, False)
                if more:
                    pe_turn_q_with_max(K, pe, s, b + 1, 1 - u)

            def finish(b, u):
                pe_turn_out(K, pe, s, b, u)
                if wo is not None:
                    pe.wait_ge(s["o"].sem, s["o"].after(b))
                    for t in range(T):
                        mm = nc.tensor.transpose(K.PS[:, OUT0, t * P:(t + 1) * P], h["o"][:, u, t * P:(t + 1) * P],
                                                 K.ident[:])
                    mm.then_inc(s["woT_ps"].sem, 1)
                    pe.wait_ge(s["woT"].sem, s["woT"].after(b))
                    for t in range(T):
                        mm = nc.tensor.matmul(K.PS[:, OUT0 + 1, t * D:(t + 1) * D], K.norm["xnT"][:, u, t * P:(t + 1) * P],
                                              wo[:], start=True, stop=True)
                    mm.then_inc(s["wo_ps"].sem, 1)

            head_pipeline(pe, prep, fused, first, finish)



F0 = 512
F0C = F0 // P


def turned_bank(u):
    return MISC + 1 - 2 * u


def quantised_ffn_layer(K, W, loaded):
    nc = K.nc
    s = ln_signals(K, turned=False)
    s["pool_step"] = K.rising("pool_step", 1)
    s["prep_step"] = K.rising("vector_prep_step", LN_STEPS + 8)
    s["main_step"] = K.rising("vector_finish_step", 12)
    for n, per in dict(qx=1, qxT_ps=1, qxT=1, gu_ps=T, g=T, hq=1, hqT_ps=1, hqT=1, down_ps=1).items():
        s[n] = K.rising("signal_" + n, per)
    ws = Signal(K.sem("f0_weight_step"), 0, 1)
    tg = K.gates[:, 4:5]

    with ExitStack() as ctx:
        def sb(name, shape, dt=F32):
            return ctx.enter_context(nc.sbuf_tensor("f0_" + name, shape, dt))

        wabs, wmean, winv = sb("abs_sums", [P, 3]), sb("w_mean", [P, 3]), sb("w_inverse", [P, 3])
        wr = sb("w_rounded", [P, 3, F0])
        wq = sb("w_ternary", [P, 3, F0], BF16)
        am, r, dq = sb("row_max", [P, 2, T]), sb("row_scale", [P, 2, T]), sb("row_back", [P, 2, T, 2])
        v, qx = sb("rounded", [P, T * D]), sb("row_whole", [P, 2, T * D], BF16)
        qxT = sb("rowT", [P, 2, T * P], BF16)
        g, h = sb("gate", [P, T, F0]), sb("hidden", [P, T, F0])
        am2, r2, dd = sb("hidden_max", [P, T]), sb("hidden_scale", [P, T]), sb("hidden_back", [P, T])
        hq, hqT = sb("hidden_whole", [P, T, F0], BF16), sb("hiddenT", [P, T, F0C, P], BF16)
        weights = [W["f0_wg"], W["f0_wu"], W["f0_wd"]]

        with nc.Block() as block:

            @block.vector
            def _(dve):
                for value, sem in loaded:
                    dve.wait_ge(sem, value)
                for k, w in enumerate(weights):
                    nc.vector.tensor_reduce(wabs[:, k:k + 1], w[:], AX_X, ALU.add, apply_absolute_value=True) \
                        .then_inc(K.sem("f0_abs_sums"), 1)
                dve.wait_ge(K.sem("f0_sums_in_psum"), 1)
                w_step = K.sem("f0_weight_step")
                nc.vector.tensor_scalar(wmean[:], K.PS[:, MISC, 0:3], 1.0 / (F0 * D), 1e-5, ALU.mult, ALU.max).then_inc(w_step, 1)
                dve.wait_ge(w_step, 1)
                nc.vector.reciprocal(winv[:], wmean[:]).then_inc(w_step, 1)
                dve.wait_ge(w_step, 2)
                for k, w in enumerate(weights):
                    nc.vector.tensor_scalar(wr[:, k], w[:], winv[:, k:k + 1], ROUND, ALU.mult, ALU.add).then_inc(w_step, 1)
                dve.wait_ge(w_step, 5)
                nc.vector.tensor_scalar(wr[:], wr[:], ROUND + 1.0, ROUND - 1.0, ALU.min, ALU.max).then_inc(w_step, 1)
                dve.wait_ge(w_step, 6)
                nc.vector.tensor_scalar(wq[:], wr[:], ROUND, None, ALU.subtract).then_inc(w_step, 1)
                nc.vector.tensor_scalar(wmean[:], wmean[:], 1.0 / 127.0, None, ALU.mult).then_inc(w_step, 1)
                dve.wait_ge(w_step, 8)
                nc.vector.tensor_scalar(wmean[:, 2:3], wmean[:, 2:3], tg, None, ALU.mult).then_inc(w_step, 1)
                dve.wait_ge(w_step, 9)

                chain, main_chain = Chain(s["prep_step"]), Chain(s["main_step"])

                def prep(b, u):
                    chain.start(b)
                    dve_layernorm(K, dve, chain, s, b, u)
                    xn = K.norm["xn"][:, u]
                    dve.wait_ge(s["xn"].sem, s["xn"].after(b))
                    nc.vector.tensor_reduce(am[:, u], xn, AX_X, ALU.max, apply_absolute_value=True).then_inc(chain.sem, 1)
                    dve.wait_ge(chain.sem, chain.next())
                    nc.vector.tensor_scalar(am[:, u], am[:, u], 1e-5, None, ALU.max).then_inc(chain.sem, 1)
                    dve.wait_ge(chain.sem, chain.next())
                    nc.vector.reciprocal(r[:, u], am[:, u]).then_inc(chain.sem, 1)
                    dve.wait_ge(chain.sem, chain.next())
                    nc.vector.tensor_scalar(r[:, u], r[:, u], 127.0, None, ALU.mult).then_inc(chain.sem, 1)
                    dve.wait_ge(chain.sem, chain.next())
                    nc.vector.tensor_tensor(dq[:, u], am[:, u].unsqueeze(2).broadcast_to([P, T, 2]),
                                            wmean[:, 0:2].unsqueeze(1).broadcast_to([P, T, 2]), ALU.mult).then_inc(chain.sem, 1)
                    dve.wait_ge(chain.sem, chain.next())
                    nc.vector.tensor_scalar(v[:, 0:D], xn[:, 0], r[:, u, 0:1], ROUND, ALU.mult, ALU.add).then_inc(chain.sem, 1)
                    chain.next()
                    nc.vector.tensor_scalar(v[:, D:2 * D], xn[:, 1], r[:, u, 1:2], ROUND, ALU.mult, ALU.add).then_inc(chain.sem, 1)
                    dve.wait_ge(chain.sem, chain.next())
                    nc.vector.tensor_scalar(v[:], v[:], ROUND + 127.0, ROUND - 128.0, ALU.min, ALU.max).then_inc(chain.sem, 1)
                    dve.wait_ge(chain.sem, chain.next())
                    nc.vector.tensor_scalar(qx[:, u], v[:], ROUND, None, ALU.subtract).then_inc(s["qx"].sem, 1)
                    dve.wait_ge(s["qx"].sem, s["qx"].after(b))

                def main(b, u):
                    c = main_chain
                    c.start(b)
                    for t in range(T):
                        dve.wait_ge(s["g"].sem, s["g"].after(b, t + 1))
                        nc.vector.scalar_tensor_tensor(h[:, t], K.PS[:, 2 * t + 1, :], dq[:, u, t, 1:2], g[:, t],
                                                       ALU.mult, ALU.mult).then_inc(c.sem, 1)
                        c.next()
                    dve.wait_ge(c.sem, c.reached())
                    nc.vector.tensor_reduce(am2[:], h[:], AX_X, ALU.max, apply_absolute_value=True).then_inc(c.sem, 1)
                    dve.wait_ge(c.sem, c.next())
                    nc.vector.tensor_scalar(am2[:], am2[:], 1e-5, None, ALU.max).then_inc(c.sem, 1)
                    dve.wait_ge(c.sem, c.next())
                    nc.vector.reciprocal(r2[:], am2[:]).then_inc(c.sem, 1)
                    dve.wait_ge(c.sem, c.next())
                    nc.vector.tensor_scalar(r2[:], r2[:], 127.0, None, ALU.mult).then_inc(c.sem, 1)
                    dve.wait_ge(c.sem, c.next())
                    nc.vector.tensor_scalar(dd[:], am2[:], wmean[:, 2:3], None, ALU.mult).then_inc(c.sem, 1)
                    dve.wait_ge(c.sem, c.next())
                    for t in range(T):
                        nc.vector.tensor_scalar(h[:, t], h[:, t], r2[:, t:t + 1], ROUND, ALU.mult, ALU.add).then_inc(c.sem, 1)
                        c.next()
                    dve.wait_ge(c.sem, c.reached())
                    nc.vector.tensor_scalar(h[:], h[:], ROUND + 127.0, ROUND - 128.0, ALU.min, ALU.max).then_inc(c.sem, 1)
                    dve.wait_ge(c.sem, c.next())
                    nc.vector.tensor_scalar(hq[:], h[:], ROUND, None, ALU.subtract).then_inc(s["hq"].sem, 1)
                    dve.wait_ge(s["hq"].sem, s["hq"].after(b))
                    dve.wait_ge(s["down_ps"].sem, s["down_ps"].after(b))
                    for t in range(T):
                        x = K.X[:, bass.ds(b * S + t * P, P)]
                        nc.vector.scalar_tensor_tensor(x, K.PS[:, OUT0, t * D:(t + 1) * D], dd[:, t:t + 1], x,
                                                       ALU.mult, ALU.add).then_inc(c.sem, 1)
                        c.next()
                    dve.wait_ge(c.sem, c.reached())

                software_pipeline(dve, prep, main)

            @block.gpsimd
            def _(pool):
                software_pipeline(pool, lambda b, u: pool_rstd(K, pool, s, b, u), lambda b, u: None)

            @block.scalar
            def _(act):
                def prep(b, u):
                    act.wait_ge(s["qxT_ps"].sem, s["qxT_ps"].after(b))
                    nc.scalar.activation(qxT[:, u], K.PS[:, turned_bank(u), 0:P].bitcast(BF16), ACT.Copy).then_inc(s["qxT"].sem, 1)

                def main(b, u):
                    for t in range(T):
                        act.wait_ge(s["gu_ps"].sem, s["gu_ps"].after(b, t + 1))
                        nc.scalar.activation(g[:, t], K.PS[:, 2 * t, :], ACT.Silu, scale=dq[:, u, t, 0:1]).then_inc(s["g"].sem, 1)
                    act.wait_ge(s["hqT_ps"].sem, s["hqT_ps"].after(b))
                    nc.scalar.activation(hqT[:].rearrange("p t c n -> p (t c n)"), K.PS[:, MISC, :].bitcast(BF16), ACT.Copy) \
                        .then_inc(s["hqT"].sem, 1)

                software_pipeline(act, prep, main)

            @block.tensor
            def _(pe):
                pe.wait_ge(K.sem("f0_abs_sums"), 3)
                nc.tensor.matmul(K.PS[:, MISC, 0:3], K.ones[:], wabs[:], start=True, stop=True) \
                    .then_inc(K.sem("f0_sums_in_psum"), 1)
                pe.wait_ge(K.sem("f0_weight_step"), 9)

                def prep(b, u):
                    pe.wait_ge(s["qx"].sem, s["qx"].after(b))
                    out = K.PS[:, turned_bank(u), :].bitcast(BF16)
                    for t in range(T):
                        mm = nc.tensor.transpose(out[:, t * P:(t + 1) * P], qx[:, u, t * D:(t + 1) * D], K.identb[:])
                    mm.then_inc(s["qxT_ps"].sem, 1)

                def main(b, u):
                    pe.wait_ge(s["qxT"].sem, s["qxT"].after(b))
                    for t in range(T):
                        for k in range(2):
                            mm = nc.tensor.matmul(K.PS[:, 2 * t + k, :], qxT[:, u, t * P:(t + 1) * P], wq[:, k], start=True, stop=True)
                        mm.then_inc(s["gu_ps"].sem, 1)
                    pe.wait_ge(s["hq"].sem, s["hq"].after(b))
                    out = K.PS[:, MISC, :].bitcast(BF16)
                    for t in range(T):
                        for c in range(F0C):
                            mm = nc.tensor.transpose(out[:, t * F0 + c * P:t * F0 + (c + 1) * P], hq[:, t, c * P:(c + 1) * P], K.identb[:])
                    mm.then_inc(s["hqT_ps"].sem, 1)
                    pe.wait_ge(s["hqT"].sem, s["hqT"].after(b))
                    for t in range(T):
                        for c in range(F0C):
                            mm = nc.tensor.matmul(K.PS[:, OUT0, t * D:(t + 1) * D], hqT[:, t, c], wq[:, 2, c * D:(c + 1) * D],
                                                  start=c == 0, stop=c == F0C - 1)
                    mm.then_inc(s["down_ps"].sem, 1)

                software_pipeline(pe, prep, main)



H1, DH1 = 8, 64
I1 = H1 * DH1
C1 = I1 // P
V1 = DH1 + 1
MISC1 = 13


def x1_setup(K, W, t, dve, w_step):
    nc = K.nc
    nc.vector.tensor_tensor(t["qk8"][:], W["x1_qs_col"][:], W["x1_ks_col"][:], ALU.mult).then_inc(w_step, 1)
    dve.wait_ge(w_step, 1)
    nc.vector.tensor_scalar(t["qk8"][:], t["qk8"][:], 8.0, None, ALU.mult).then_inc(w_step, 1)
    dve.wait_ge(w_step, 2)
    nc.vector.tensor_tensor(t["nk"][:], W["x1_nk"][:], W["x1_nk"][:], ALU.mult).then_inc(w_step, 1)
    dve.wait_ge(w_step, 3)
    nc.vector.tensor_reduce(t["nk_sq"][:], t["nk"][:], AX_X, ALU.add).then_inc(w_step, 1)
    dve.wait_ge(w_step, 4)
    nc.vector.tensor_scalar(t["nk_sq"][:], t["nk_sq"][:], 1e-24, None, ALU.max).then_inc(w_step, 1)
    dve.wait_ge(w_step, 5)
    dve.wait_ge(K.sem("x1_null_norm"), 1)
    nc.vector.tensor_scalar(t["nk"][:], W["x1_nk"][:], t["nk_r"][:, 0:1], 8.0, ALU.mult, ALU.mult).then_inc(w_step, 1)
    dve.wait_ge(w_step, 6)
    nc.vector.tensor_tensor(t["nk"][:], t["nk"][:], W["x1_qs"][:], ALU.mult).then_inc(w_step, 1)
    dve.wait_ge(w_step, 7)
    nc.vector.tensor_tensor(t["nk"][:], t["nk"][:], W["x1_ks"][:], ALU.mult).then_inc(w_step, 1)
    dve.wait_ge(w_step, 8)
    nc.vector.tensor_tensor(t["sq"][:, 0].rearrange("p (h e) -> p h e", e=DH1), W["x1_wq"][:].rearrange("p (h e) -> p h e", e=DH1),
                            t["nk"][:].unsqueeze(1).broadcast_to([P, H1, DH1]), ALU.mult).then_inc(w_step, 1)
    dve.wait_ge(w_step, 9)
    nc.vector.tensor_reduce(t["wqn"][:], t["sq"][:, 0].rearrange("p (h e) -> p h e", e=DH1), AX_X, ALU.add).then_inc(w_step, 1)
    dve.wait_ge(w_step, 10)
    nc.vector.tensor_scalar(t["gout"][:], W["x1_gout"][:], K.gates[:, 1:2], None, ALU.mult).then_inc(w_step, 1)
    dve.wait_ge(w_step, 11)
    nc.vector.tensor_scalar(K.hide_cols[:], K.mask_k1c[:], 1.0, -HIDE, ALU.subtract, ALU.mult).then_inc(w_step, 1)
    dve.wait_ge(w_step, 12)
    nc.vector.tensor_scalar(K.hide_rows[:], K.mask_k1[:], 1.0, -HIDE, ALU.subtract, ALU.mult).then_inc(w_step, 1)
    dve.wait_ge(w_step, 13)


def normed_attention_layer(K, W, loaded):
    nc = K.nc
    s = ln_signals(K, turned=False)
    s["pool_step"] = K.rising("pool_step", 4)
    s["prep_step"] = K.rising("vector_prep_step", LN_STEPS + 16)
    s["finish_step"] = K.rising("vector_finish_step", 14)
    per = dict(z_stats=1, z_rstd=1, z=1, null=1, null_read=1, sq=4, qk_ssq=2, qk_r=2, q_rows=1, k_rows=1, filled=MISC1, read=MISC1,
               smax_ps=H1, smax=H1, m=1, mT_ps=1, mT=1, null_arg=1, null_p=1, null_v=1,
               st_ps=H1, p=H1, mix=2, half_read=2, o_rows=1, oT_ps=1, oT=1, wo_ps=1, out_banks=1, o_stats=1, o_rstd=1, hide=1)
    for n, k in per.items():
        s[n] = K.rising("signal_" + n, k)

    with ExitStack() as ctx:
        t_ = {}

        def sb(name, shape, dt=F32):
            t_[name] = ctx.enter_context(nc.sbuf_tensor("x1_" + name, shape, dt))
            return t_[name]

        qk8, nk, nk_sq, nk_r = sb("qk8", [P, 1]), sb("nk", [P, DH1]), sb("nk_sq", [P, 1]), sb("nk_r", [P, 1])
        wqn, gout = sb("wqn", [P, H1]), sb("gout", [P, D])
        zm, zr = sb("row_max", [P, 2, T]), sb("row_max_inverse", [P, 2, T])
        z, zst, zmv, zrs = sb("row_scaled", [P, 2, T, D]), sb("z_stats", [P, 2, T, 6]), sb("z_mean_var", [P, 2, T, 2]), sb("z_rstd", [P, 2, T])
        zT = sb("zT", [P, 2, T * P])
        raw, sq = sb("raw", [P, 4, I1]), sb("sq", [P, 4, I1])
        ssq, rn = sb("sum_squares", [P, 2, 4, H1]), sb("inverse_norms", [P, 2, 4, H1])
        qn, kn = sb("q_rows", [P, T, H1, P]), sb("k_rows", [P, T, I1])
        ve = sb("v_with_one", [P, 2, T, H1, V1])
        qT, kT = sb("qT", [P, 2, H1, S]), sb("kT", [P, 2, C1, S])
        nnull, nm, nrest = sb("minus_null", [P, 2, T, H1]), sb("minus_max", [P, 2, T, H1]), sb("rest", [P, T, H1])
        arg, pn, pnv = sb("null_argument", [P, 2, T, H1]), sb("null_prob", [P, 2, T, H1]), sb("null_value", [P, 2, T, H1, DH1])
        mtok, mT = sb("max_rows", [P, T, P], BF16), sb("maxT", [P, 2, S], BF16)
        hide = sb("hide_keys", [P, 2, T])
        p = sb("probs", [P, 2, T, S])
        rec, o, oT = sb("inverse_sums", [P, T, 4]), sb("out_rows", [P, T, H1, DH1]), sb("outT", [P, T, I1])
        ost, omv, ors, om, orr, ol = sb("o_stats", [P, T, 6]), sb("o_mean_var", [P, T, 2]), sb("o_rstd", [P, T]), sb("o_max", [P, T]), sb("o_max_inverse", [P, T]), sb("o_rows", [P, T, D])
        ove = sb("var_eps", [P, 2, T])

        with nc.Block() as block:

            @block.vector
            def _(dve):
                nc.vector.memset(qn[:], 0.0)
                nc.vector.memset(mtok[:], 0.0)
                nc.vector.memset(ve[:, :, :, :, DH1:V1], 1.0)
                for value, sem in loaded:
                    dve.wait_ge(sem, value)
                x1_setup(K, W, t_, dve, K.sem("x1_weight_step"))
                chain, ending = Chain(s["prep_step"]), Chain(s["finish_step"])

                def prep(b, u):
                    chain.start(b)
                    dve_layernorm(K, dve, chain, s, b, u)
                    xn = K.norm["xn"][:, u]
                    dve.wait_ge(s["xn"].sem, s["xn"].after(b))
                    nc.vector.tensor_reduce(zm[:, u], xn, AX_X, ALU.max).then_inc(chain.sem, 1)
                    dve.wait_ge(chain.sem, chain.next())
                    nc.vector.reciprocal(zr[:, u], zm[:, u]).then_inc(chain.sem, 1)
                    dve.wait_ge(chain.sem, chain.next())
                    nc.vector.tensor_tensor(z[:, u], xn, zr[:, u].unsqueeze(2).broadcast_to([P, T, D]), ALU.mult).then_inc(chain.sem, 1)
                    dve.wait_ge(chain.sem, chain.next())
                    for t in range(T):
                        if t == 0:
                            settled(dve, K)
                        nc.vector.bn_stats(zst[:, u, t], z[:, u, t]).then_inc(chain.sem, 1)
                        chain.next()
                    dve.wait_ge(chain.sem, chain.reached())
                    settled(dve, K)
                    nc.vector.bn_aggr(zmv[:, u, 0], zst[:, u, 0]).then_inc(chain.sem, 1)
                    chain.next()
                    nc.vector.bn_aggr(zmv[:, u, 1], zst[:, u, 1]).then_inc(s["z_stats"].sem, 1)
                    dve.wait_ge(s["z_rstd"].sem, s["z_rstd"].after(b))
                    nc.vector.tensor_scalar(z[:, u, 0], z[:, u, 0], zmv[:, u, 0, 0:1], zrs[:, u, 0:1], ALU.subtract, ALU.mult).then_inc(chain.sem, 1)
                    chain.next()
                    nc.vector.tensor_scalar(z[:, u, 1], z[:, u, 1], zmv[:, u, 1, 0:1], zrs[:, u, 1:2], ALU.subtract, ALU.mult) \
                        .then_inc(s["z"].sem, 1)
                    for half, (src, rows) in enumerate((("k", kn), ("q", qn))):
                        dve.wait_ge(s["sq"].sem, s["sq"].after(b, 2 * half + 2))
                        nc.vector.tensor_reduce(ssq[:, u, 2 * half:2 * half + 2], sq[:, 2 * half:2 * half + 2].rearrange("p t (h e) -> p t h e", e=DH1),
                                                AX_X, ALU.add).then_inc(s["qk_ssq"].sem, 1)
                        dve.wait_ge(s["qk_r"].sem, s["qk_r"].after(b, half + 1))
                        dve.wait_ge(s["read"].sem, s["read"].after(b, (4, 9)[half]))
                        for t in range(T):
                            r = raw[:, 2 * half + t].rearrange("p (h e) -> p h e", e=DH1)
                            f = rn[:, u, 2 * half + t].unsqueeze(2).broadcast_to([P, H1, DH1])
                            if src == "k":
                                ins = nc.vector.tensor_tensor(kn[:, t].rearrange("p (h e) -> p h e", e=DH1), r, f, ALU.mult)
                                ins.then_inc(chain.sem if t == 0 else s["k_rows"].sem, 1)
                                if t == 0:
                                    chain.next()
                            else:
                                for odd in range(2):
                                    ins = nc.vector.tensor_tensor(qn[:, t, odd::2, odd * DH1:(odd + 1) * DH1], r[:, odd::2], f[:, odd::2], ALU.mult)
                                    if (t, odd) == (1, 1):
                                        ins.then_inc(s["q_rows"].sem, 1)
                                    else:
                                        ins.then_inc(chain.sem, 1)
                                        chain.next()
                    dve.wait_ge(s["null"].sem, s["null"].after(b))
                    nc.vector.tensor_tensor(nnull[:, u], K.PS[:, SMAX0 + 1, 0:T * H1].rearrange("p (t h) -> p t h", t=T),
                                            rn[:, u, 2:4], ALU.mult).then_inc(s["null_read"].sem, 1)
                    dve.wait_ge(s["null_read"].sem, s["null_read"].after(b))
                    nc.vector.tensor_scalar(nnull[:, u], nnull[:, u], -1.0, None, ALU.mult).then_inc(chain.sem, 1)
                    dve.wait_ge(chain.sem, chain.next())

                def row_max(b, u, n):
                    dve.wait_ge(s["smax_ps"].sem, s["smax_ps"].after(b, n + 1))
                    nc.vector.tensor_reduce(nm[:, u, :, n], K.PS[:, SMAX0 + n % 2, :].rearrange("p (t n) -> p t n", t=T),
                                            AX_X, ALU.max, negate=True).then_inc(s["smax"].sem, 1)

                def place_max(b, u):
                    m = mtok[:, :, 0:3 * H1].rearrange("p t (h i) -> p t h i", i=3)
                    dve.wait_ge(s["smax"].sem, s["smax"].after(b))
                    nc.vector.tensor_tensor(nm[:, u], nm[:, u], nnull[:, u], ALU.min).then_inc(chain.sem, 1)
                    dve.wait_ge(chain.sem, chain.next())
                    nc.vector.tensor_copy(m[:, :, :, 0], nm[:, u]).then_inc(chain.sem, 1)
                    dve.wait_ge(chain.sem, chain.next())
                    nc.vector.tensor_tensor(nrest[:], nm[:, u], m[:, :, :, 0], ALU.subtract).then_inc(chain.sem, 1)
                    dve.wait_ge(chain.sem, chain.next())
                    nc.vector.tensor_copy(m[:, :, :, 1], nrest[:]).then_inc(chain.sem, 1)
                    dve.wait_ge(chain.sem, chain.next())
                    nc.vector.tensor_tensor(m[:, :, :, 2], nrest[:], m[:, :, :, 1], ALU.subtract).then_inc(s["m"].sem, 1)
                    nc.vector.tensor_tensor(arg[:, u], nm[:, u], nnull[:, u], ALU.subtract).then_inc(s["null_arg"].sem, 1)

                def first(b, u):
                    for n in range(H1):
                        row_max(b, u, n)
                    place_max(b, u)

                def out_half(b, u, half):
                    hs = slice(4 * half, 4 * half + 4)
                    dve.wait_ge(s["mix"].sem, s["mix"].after(b, half + 1))
                    if half == 0:
                        dve.wait_ge(s["null_v"].sem, s["null_v"].after(b))
                    ob = K.PS[:, OUT0:OUT0 + T, 0:4 * V1].rearrange("p t (h e) -> p t h e", e=V1)
                    nc.vector.tensor_tensor(rec[:], ob[:, :, :, DH1], pn[:, u, :, hs], ALU.add).then_inc(ending.sem, 1)
                    dve.wait_ge(ending.sem, ending.next())
                    nc.vector.reciprocal(rec[:], rec[:]).then_inc(ending.sem, 1)
                    dve.wait_ge(ending.sem, ending.next())
                    nc.vector.tensor_tensor(o[:, :, hs], ob[:, :, :, 0:DH1], pnv[:, u, :, hs], ALU.add).then_inc(s["half_read"].sem, 1)
                    dve.wait_ge(s["half_read"].sem, s["half_read"].after(b, half + 1))
                    ins = nc.vector.tensor_tensor(o[:, :, hs], o[:, :, hs], rec[:].unsqueeze(3).broadcast_to([P, T, 4, DH1]), ALU.mult)
                    if half == 0:
                        ins.then_inc(ending.sem, 1)
                        dve.wait_ge(ending.sem, ending.next())
                    else:
                        ins.then_inc(s["o_rows"].sem, 1)

                def fused(b, u, more):
                    ending.start(b)
                    for n in range(H1):
                        if more:
                            row_max(b + 1, 1 - u, n)
                        if n == 4:
                            out_half(b, u, 0)
                    out_half(b, u, 1)
                    if more:
                        place_max(b + 1, 1 - u)

                def finish(b, u):
                    dve.wait_ge(s["wo_ps"].sem, s["wo_ps"].after(b))
                    po = K.PS[:, OUT0, 0:T * D].rearrange("p (t d) -> p t d", t=T)
                    nc.vector.tensor_reduce(om[:], po, AX_X, ALU.max).then_inc(ending.sem, 1)
                    dve.wait_ge(ending.sem, ending.next())
                    nc.vector.reciprocal(orr[:], om[:]).then_inc(ending.sem, 1)
                    dve.wait_ge(ending.sem, ending.next())
                    nc.vector.tensor_tensor(ol[:], po, orr[:].unsqueeze(2).broadcast_to([P, T, D]), ALU.mult).then_inc(s["out_banks"].sem, 1)
                    dve.wait_ge(s["out_banks"].sem, s["out_banks"].after(b))
                    settled(dve, K)
                    for t in range(T):
                        nc.vector.bn_stats(ost[:, t], ol[:, t]).then_inc(ending.sem, 1)
                        ending.next()
                    dve.wait_ge(ending.sem, ending.reached())
                    settled(dve, K)
                    nc.vector.bn_aggr(omv[:, 0], ost[:, 0]).then_inc(ending.sem, 1)
                    ending.next()
                    nc.vector.bn_aggr(omv[:, 1], ost[:, 1]).then_inc(s["o_stats"].sem, 1)
                    dve.wait_ge(s["o_rstd"].sem, s["o_rstd"].after(b))
                    for t in range(T):
                        nc.vector.tensor_scalar(ol[:, t], ol[:, t], omv[:, t, 0:1], ors[:, t:t + 1], ALU.subtract, ALU.mult).then_inc(ending.sem, 1)
                        ending.next()
                    dve.wait_ge(ending.sem, ending.reached())
                    nc.vector.tensor_tensor(ol[:], ol[:], gout[:].unsqueeze(1).broadcast_to([P, T, D]), ALU.mult).then_inc(ending.sem, 1)
                    dve.wait_ge(ending.sem, ending.next())
                    x = cols(K.X, b)
                    nc.vector.tensor_tensor(x, ol[:].rearrange("p t d -> p (t d)"), x, ALU.add).then_inc(ending.sem, 1)
                    dve.wait_ge(ending.sem, ending.next())

                head_pipeline(dve, prep, fused, first, finish)

            @block.gpsimd
            def _(pool):
                for value, sem in loaded:
                    pool.wait_ge(sem, value)
                pool.wait_ge(K.sem("x1_weight_step"), 5)
                nc.gpsimd.tensor_tensor(nk_r[:], nk_sq[:], K.neghalf[:, 0:1], ALU.pow).then_inc(K.sem("x1_null_norm"), 1)
                pool.wait_ge(K.sem("x1_weight_step"), 12)
                ps = s["pool_step"]

                def prep(b, u):
                    pool_rstd(K, pool, s, b, u)
                    settled(pool, K)
                    nc.gpsimd.tensor_copy(K.ctx_tile[:, u, :], K.ctxT[:, bass.ds(b * S, S)])
                    nc.gpsimd.tensor_copy(hide[:, u, :], K.hide_cols[:, bass.ds(b * T, T)]).then_inc(s["hide"].sem, 1)
                    pool.wait_ge(s["z_stats"].sem, s["z_stats"].after(b))
                    nc.gpsimd.tensor_tensor(ove[:, 0], zmv[:, u, :, 1], K.eps5[:, 0:T], ALU.add).then_inc(ps.sem, 1)
                    pool.wait_ge(ps.sem, ps.after(b, 2))
                    nc.gpsimd.tensor_tensor(zrs[:, u], ove[:, 0], K.neghalf[:, 0:T], ALU.pow).then_inc(s["z_rstd"].sem, 1)
                    for half in range(2):
                        pool.wait_ge(s["qk_ssq"].sem, s["qk_ssq"].after(b, half + 1))
                        sl = slice(2 * half, 2 * half + 2)
                        settled(pool, K)
                        nc.gpsimd.tensor_scalar(ssq[:, u, sl], ssq[:, u, sl], 1e-24, None, ALU.max) \
                            .then_inc(ps.sem, 1)
                        pool.wait_ge(ps.sem, ps.after(b, 3 + half))
                        nc.gpsimd.tensor_tensor(rn[:, u, sl], ssq[:, u, sl], K.neghalf[:, 0:T].unsqueeze(2).broadcast_to([P, T, H1]), ALU.pow) \
                            .then_inc(s["qk_r"].sem, 1)

                def null_values(b, u):
                    pool.wait_ge(s["null_p"].sem, s["null_p"].after(b))
                    nc.gpsimd.tensor_tensor(pnv[:, u].rearrange("p t h e -> p (t h) e"), pn[:, u].rearrange("p t h -> p (t h)").unsqueeze(2).broadcast_to([P, T * H1, DH1]),
                                            W["x1_nv"][:].unsqueeze(1).broadcast_to([P, T * H1, DH1]), ALU.mult).then_inc(s["null_v"].sem, 1)

                def fused(b, u, more):
                    if more:
                        null_values(b + 1, 1 - u)

                def finish(b, u):
                    pool.wait_ge(s["o_stats"].sem, s["o_stats"].after(b))
                    nc.gpsimd.tensor_tensor(ove[:, 1], omv[:, :, 1], K.eps5[:, 0:T], ALU.add).then_inc(K.sem("x1_pool_ending"), 1)
                    pool.wait_ge(K.sem("x1_pool_ending"), b + 1)
                    nc.gpsimd.tensor_tensor(ors[:], ove[:, 1], K.neghalf[:, 0:T], ALU.pow).then_inc(s["o_rstd"].sem, 1)

                head_pipeline(pool, prep, fused, null_values, finish)

            @block.scalar
            def _(act):
                act.wait_ge(K.sem("x1_weight_step"), 2)

                def read_bank(b, u, f, emit):
                    act.wait_ge(s["filled"].sem, s["filled"].after(b, f + 1))
                    emit(K.PS[:, MISC + (u + f) % 2, :]).then_inc(s["read"].sem, 1)

                def copy(dst, scale=None):
                    def emit(bank):
                        n = 1
                        for k in dst.shape[1:]:
                            n *= k
                        src = bank[:, 0:n]
                        if len(dst.shape) == 3:
                            src = src.rearrange("p (a b) -> p a b", a=dst.shape[1])
                        if scale is None:
                            return nc.scalar.activation(dst, src, ACT.Copy)
                        return nc.scalar.activation(dst, src, ACT.Identity, scale=scale)
                    return emit

                def prep(b, u):
                    f = 0
                    for t in range(T):
                        read_bank(b, u, f, copy(ve[:, u, t, :, 0:DH1])); f += 1
                    for k in range(2):
                        if k == 1:
                            read_bank(b, u, f, copy(zT[:, u], W["x1_gnorm"][:, 0:1])); f += 1
                        for t in range(T):
                            def both(bank, k=k, t=t):
                                nc.scalar.activation(sq[:, 2 * k + t], bank, ACT.Square).then_inc(s["sq"].sem, 1)
                                return nc.scalar.activation(raw[:, 2 * k + t], bank, ACT.Copy)
                            read_bank(b, u, f, both); f += 1
                        if k == 0:
                            for c in range(C1 // 2):
                                read_bank(b, u, f, copy(kT[:, u, 2 * c:2 * c + 2].rearrange("p c n -> p (c n)"))); f += 1
                    for c in range(H1 // 2):
                        read_bank(b, u, f, copy(qT[:, u, 2 * c:2 * c + 2].rearrange("p c n -> p (c n)"), qk8[:, 0:1])); f += 1

                def maxima(b, u):
                    act.wait_ge(s["null_arg"].sem, s["null_arg"].after(b))
                    nc.scalar.activation(pn[:, u], arg[:, u], ACT.Exp).then_inc(s["null_p"].sem, 1)
                    act.wait_ge(s["mT_ps"].sem, s["mT_ps"].after(b))
                    nc.scalar.activation(mT[:, u], K.PS[:, SMAX0, 0:P].bitcast(BF16), ACT.Copy).then_inc(s["mT"].sem, 1)

                def fused(b, u, more):
                    act.wait_ge(s["hide"].sem, s["hide"].after(b))
                    for n in range(H1):
                        act.wait_ge(s["st_ps"].sem, s["st_ps"].after(b, n + 1))
                        for kt in range(T):
                            ins = nc.scalar.activation(p[:, n % 2, kt], K.PS[:, ST0 + n % 2, kt * S:(kt + 1) * S], ACT.Exp, bias=hide[:, u, kt:kt + 1])
                        ins.then_inc(s["p"].sem, 1)
                    if more:
                        maxima(b + 1, 1 - u)

                def finish(b, u):
                    act.wait_ge(s["oT_ps"].sem, s["oT_ps"].after(b))
                    nc.scalar.activation(oT[:], K.PS[:, OUT0:OUT0 + T, :], ACT.Copy).then_inc(s["oT"].sem, 1)

                head_pipeline(act, prep, fused, maxima, finish)

            @block.tensor
            def _(pe):
                for value, sem in loaded:
                    pe.wait_ge(sem, value)
                pe.wait_ge(K.sem("x1_weight_step"), 13)
                def fill(b, u, f, emit):
                    pe.wait_ge(s["read"].sem, b * MISC1 + (s["read"].base + f - 1))
                    emit(K.PS[:, MISC + (u + f) % 2, :]).then_inc(s["filled"].sem, 1)

                def prep(b, u):
                    f = 0
                    pe.wait_ge(s["hide"].sem, s["hide"].after(b))
                    for t in range(T):
                        fill(b, u, f, lambda bank: nc.tensor.matmul(bank, K.ctx_tile[:, u, t * P:(t + 1) * P], W["x1_wv"][:], start=True, stop=True)); f += 1
                    for t in range(T):
                        fill(b, u, f, lambda bank: nc.tensor.matmul(bank, K.ctx_tile[:, u, t * P:(t + 1) * P], W["x1_wk"][:], start=True, stop=True)); f += 1
                    pe.wait_ge(s["k_rows"].sem, s["k_rows"].after(b))

                    def turn_k(c):
                        def emit(bank):
                            for cc in range(2):
                                for t in range(T):
                                    mm = nc.tensor.transpose(bank[:, cc * S + t * P:cc * S + (t + 1) * P], kn[:, t, (2 * c + cc) * P:(2 * c + cc + 1) * P], K.ident[:])
                            return mm
                        return emit
                    for c in range(C1 // 2):
                        fill(b, u, f, turn_k(c)); f += 1
                    pe.wait_ge(s["z"].sem, s["z"].after(b))

                    def turn_z(bank):
                        for t in range(T):
                            mm = nc.tensor.transpose(bank[:, t * P:(t + 1) * P], z[:, u, t], K.ident[:])
                        return mm
                    fill(b, u, f, turn_z); f += 1
                    pe.wait_ge(s["read"].sem, s["read"].after(b, f))
                    for t in range(T):
                        fill(b, u, f, lambda bank: nc.tensor.matmul(bank, zT[:, u, t * P:(t + 1) * P], W["x1_wq"][:], start=True, stop=True)); f += 1
                    for t in range(T):
                        mm = nc.tensor.matmul(K.PS[:, SMAX0 + 1, t * H1:(t + 1) * H1], zT[:, u, t * P:(t + 1) * P], wqn[:], start=True, stop=True)
                    mm.then_inc(s["null"].sem, 1)
                    pe.wait_ge(s["q_rows"].sem, s["q_rows"].after(b))

                    def turn_q(c):
                        def emit(bank):
                            for cc in range(2):
                                for t in range(T):
                                    mm = nc.tensor.transpose(bank[:, cc * S + t * P:cc * S + (t + 1) * P], qn[:, t, 2 * c + cc], K.ident[:])
                            return mm
                        return emit
                    for c in range(H1 // 2):
                        fill(b, u, f, turn_q(c)); f += 1

                def scores(b, u, n):
                    if n == 0:
                        pe.wait_ge(s["read"].sem, s["read"].after(b))
                        pe.wait_ge(s["null_read"].sem, s["null_read"].after(b))
                    if n >= 2:
                        pe.wait_ge(s["smax"].sem, s["smax"].after(b, n - 1))
                    for t in range(T):
                        o_ = K.PS[:, SMAX0 + n % 2, t * S:(t + 1) * S]
                        nc.tensor.matmul(o_, K.identb[:], K.hide_rows[:, bass.ds(b * S, S)], start=True, stop=False)
                        mm = nc.tensor.matmul(o_, qT[:, u, n, t * P:(t + 1) * P], kT[:, u, n // 2, :], start=False, stop=True)
                    mm.then_inc(s["smax_ps"].sem, 1)

                def turn_max(b, u):
                    pe.wait_ge(s["m"].sem, s["m"].after(b))
                    for t in range(T):
                        mm = nc.tensor.transpose(K.PS[:, SMAX0, :].bitcast(BF16)[:, t * P:(t + 1) * P], mtok[:, t], K.identb[:])
                    mm.then_inc(s["mT_ps"].sem, 1)

                def scores_T(b, u, n):
                    if n == 0:
                        pe.wait_ge(s["mT"].sem, s["mT"].after(b))
                    for kt in range(T):
                        o_ = K.PS[:, ST0 + n % 2, kt * S:(kt + 1) * S]
                        nc.tensor.matmul(o_, kT[:, u, n // 2, kt * P:(kt + 1) * P], qT[:, u, n, :], start=True, stop=False)
                        mm = nc.tensor.matmul(o_, K.pick_max[:, n, :], mT[:, u], start=False, stop=True)
                    mm.then_inc(s["st_ps"].sem, 1)

                def mix(b, u, n):
                    if n == 0:
                        pe.wait_ge(s["out_banks"].sem, s["out_banks"].before(b))
                    if n == H1 // 2:
                        pe.wait_ge(s["half_read"].sem, s["half_read"].after(b, 1))
                    pe.wait_ge(s["p"].sem, s["p"].after(b, n + 1))
                    c = (n % 4) * V1
                    for t in range(T):
                        for kt in range(T):
                            mm = nc.tensor.matmul(K.PS[:, OUT0 + t, c:c + V1], p[:, n % 2, kt, t * P:(t + 1) * P], ve[:, u, kt, n, :],
                                                  start=kt == 0, stop=kt == T - 1)
                    if n % 4 == 3:
                        mm.then_inc(s["mix"].sem, 1)

                def first(b, u):
                    for n in range(H1):
                        scores(b, u, n)
                    turn_max(b, u)

                def fused(b, u, more):
                    for n in range(H1):
                        scores_T(b, u, n)
                        if more:
                            scores(b + 1, 1 - u, n)
                        if n >= 1:
                            mix(b, u, n - 1)
                    mix(b, u, H1 - 1)
                    if more:
                        turn_max(b + 1, 1 - u)

                def finish(b, u):
                    pe.wait_ge(s["o_rows"].sem, s["o_rows"].after(b))
                    for t in range(T):
                        for c in range(C1):
                            mm = nc.tensor.transpose(K.PS[:, OUT0 + t, c * P:(c + 1) * P],
                                                     o[:, t, 2 * c:2 * c + 2].rearrange("p h e -> p (h e)"), K.ident[:])
                    mm.then_inc(s["oT_ps"].sem, 1)
                    pe.wait_ge(s["oT"].sem, s["oT"].after(b))
                    for t in range(T):
                        for c in range(C1):
                            mm = nc.tensor.matmul(K.PS[:, OUT0, t * D:(t + 1) * D], oT[:, t, c * P:(c + 1) * P], W["x1_wo"][:, c * D:(c + 1) * D],
                                                  start=c == 0, stop=c == C1 - 1)
                    mm.then_inc(s["wo_ps"].sem, 1)

                head_pipeline(pe, prep, fused, first, finish)



LAT = 64


def latent_attention_layer(K, W, loaded):
    nc = K.nc
    h = K.heads
    s = dict(ln_signals(K), **head_signals(K))
    for extra in ("oT0", "oT1", "o", "woT_ps", "woT", "wo_ps"):
        s[extra] = K.rising("heads_" + extra, 1)
    for extra in ("rms_sum", "rms_r", "rms", "lat_stats", "lat_rstd", "lat", "latT_ps", "latT"):
        s[extra] = K.rising("signal_" + extra, 1)
    s["q_ps"], s["kv_ps"] = K.rising("q_in_psum", 1), K.rising("kv_in_psum", 1)
    s["k0"] = 2
    s["pool_step"] = K.rising("pool_step", 2 + 4)
    s["prep_step"] = K.rising("vector_prep_step", LN_STEPS + 2 + 4 + 6 + PLACE_MAX_STEPS)
    s["finish_step"] = K.rising("vector_finish_step", NORMALISE_STEPS + 1)
    tg = K.gates[:, 5:6]

    with ExitStack() as ctx:
        def sb(name, shape, dt=F32):
            return ctx.enter_context(nc.sbuf_tensor("f1_" + name, shape, dt))

        sq, ss, rr, rn = sb("squares", [P, T, D]), sb("square_sums", [P, 2, T]), sb("inverse_rms", [P, 2, T]), sb("rms_rows", [P, 2, T, D])
        lst, lmv, lve, lrs = sb("lat_stats", [P, T, 6]), sb("lat_mean_var", [P, 2, T, 2]), sb("lat_var_eps", [P, T]), sb("lat_rstd", [P, 2, T])
        lat, latT = sb("lat_rows", [P, T, P]), sb("latT", [P, 2, T * P])
        ra, rb = sb("turned_a", [P, T * H, DH]), sb("turned_b", [P, T * H, DH])
        wukv = sb("w_k_v", [P, 2 * D])
        rope = sb("rope_for_q", [P, 2, T, DH])

        with nc.Block() as block:

            @block.gpsimd
            def _(pool):
                ps = s["pool_step"]

                def prep(b, u):
                    pool_rstd(K, pool, s, b, u)
                    pool.wait_ge(s["rms_sum"].sem, s["rms_sum"].after(b))
                    nc.gpsimd.tensor_tensor(rr[:, u], ss[:, u], K.neghalf[:, 0:T], ALU.pow).then_inc(s["rms_r"].sem, 1)
                    pool.wait_ge(s["lat_stats"].sem, s["lat_stats"].after(b))
                    nc.gpsimd.tensor_tensor(lve[:], lmv[:, u, :, 1], K.eps5[:, 0:T], ALU.add).then_inc(ps.sem, 1)
                    pool.wait_ge(ps.sem, ps.after(b, 2))
                    nc.gpsimd.tensor_tensor(lrs[:, u], lve[:], K.neghalf[:, 0:T], ALU.pow).then_inc(s["lat_rstd"].sem, 1)
                    pool_split(K, pool, s, b, u)

                def nothing(b, u, more=None):
                    pass
                head_pipeline(pool, prep, nothing, nothing, nothing)

            @block.vector
            def _(dve):
                setup = K.sem("f1_setup_step")
                nc.vector.memset(lat[:], 0.0)
                nc.vector.memset(wukv[:], 0.0).then_inc(setup, 1)
                for value, sem in loaded:
                    dve.wait_ge(sem, value)
                dve.wait_ge(setup, 1)
                nc.vector.tensor_copy(wukv[0:LAT, :], W["f1_wukv"][:]).then_inc(setup, 1)
                nc.vector.tensor_scalar(rope[:].rearrange("p a t e -> p (a t e)"), W["f1_rope"][:], DH ** -0.5, None, ALU.mult).then_inc(setup, 1)
                dve.wait_ge(setup, 3)
                chain, ending = Chain(s["prep_step"]), Chain(s["finish_step"])

                def rotate(src, tables, dst, signal, last_reads):
                    x_ = src.rearrange("p t (h e) -> p t h e", e=DH)
                    a4, b4 = (v.rearrange("p (t h) e -> p t h e", t=T) for v in (ra[:], rb[:]))
                    cos, sin = (tables[:, k].unsqueeze(2).broadcast_to([P, T, H, DH]) for k in range(2))
                    hf = DH // 2
                    nc.vector.tensor_tensor(a4, x_, cos, ALU.mult).then_inc(chain.sem, 1)
                    chain.next()
                    nc.vector.tensor_tensor(b4[:, :, :, 0:hf], x_[:, :, :, hf:DH], sin[:, :, :, 0:hf], ALU.mult).then_inc(chain.sem, 1)
                    chain.next()
                    last = nc.vector.tensor_tensor(b4[:, :, :, hf:DH], x_[:, :, :, 0:hf], sin[:, :, :, hf:DH], ALU.mult)
                    last.then_inc(chain.sem, 1)
                    dve.wait_ge(chain.sem, chain.next())
                    nc.vector.tensor_tensor(dst, ra[:].rearrange("p h e -> p (h e)"), rb[:].rearrange("p h e -> p (h e)"), ALU.add).then_inc(signal.sem, 1)

                def prep(b, u):
                    chain.start(b)
                    dve_layernorm(K, dve, chain, s, b, u)
                    y = K.norm["xn"][:, u]
                    dve.wait_ge(s["xn"].sem, s["xn"].after(b))
                    nc.vector.tensor_tensor(sq[:], y, y, ALU.mult).then_inc(chain.sem, 1)
                    dve.wait_ge(chain.sem, chain.next())
                    nc.vector.tensor_reduce(ss[:, u], sq[:], AX_X, ALU.add).then_inc(chain.sem, 1)
                    dve.wait_ge(chain.sem, chain.next())
                    nc.vector.tensor_scalar(ss[:, u], ss[:, u], 1.0 / D, 1e-6, ALU.mult, ALU.add).then_inc(s["rms_sum"].sem, 1)
                    dve.wait_ge(s["rms_r"].sem, s["rms_r"].after(b))
                    nc.vector.tensor_tensor(rn[:, u], y, rr[:, u].unsqueeze(2).broadcast_to([P, T, D]), ALU.mult).then_inc(s["rms"].sem, 1)
                    dve.wait_ge(s["q_ps"].sem, s["q_ps"].after(b))
                    ql = K.PS[:, MISC + 1, 0:T * (D + LAT)].rearrange("p (t n) -> p t n", t=T)
                    settled(dve, K)
                    for t in range(T):
                        nc.vector.bn_stats(lst[:, t], ql[:, t, D:D + LAT]).then_inc(chain.sem, 1)
                        chain.next()
                    dve.wait_ge(chain.sem, chain.reached())
                    settled(dve, K)
                    nc.vector.bn_aggr(lmv[:, u, 0], lst[:, 0]).then_inc(chain.sem, 1)
                    chain.next()
                    nc.vector.bn_aggr(lmv[:, u, 1], lst[:, 1]).then_inc(s["lat_stats"].sem, 1)
                    dve.wait_ge(s["lat_rstd"].sem, s["lat_rstd"].after(b))
                    nc.vector.tensor_scalar(lat[:, 0, 0:LAT], ql[:, 0, D:D + LAT], lmv[:, u, 0, 0:1], lrs[:, u, 0:1], ALU.subtract, ALU.mult).then_inc(chain.sem, 1)
                    chain.next()
                    nc.vector.tensor_scalar(lat[:, 1, 0:LAT], ql[:, 1, D:D + LAT], lmv[:, u, 1, 0:1], lrs[:, u, 1:2], ALU.subtract, ALU.mult) \
                        .then_inc(s["lat"].sem, 1)
                    rotate(ql[:, :, 0:D], rope, h["qs"][:, u], s["qs"], None)
                    dve.wait_ge(s["qs"].sem, s["qs"].after(b))
                    dve.wait_ge(s["kv_ps"].sem, s["kv_ps"].after(b))
                    kv = K.PS[:, MISC, :].rearrange("p (t n) -> p t n", t=T)
                    nc.vector.tensor_copy(h["ve"][:, u, :, 0:DH].rearrange("p (t h) e -> p t h e", t=T),
                                          kv[:, :, D:2 * D].rearrange("p t (h e) -> p t h e", e=DH)).then_inc(s["v"].sem, 1)
                    rotate(kv[:, :, 0:D], W["f1_rope"][:].rearrange("p (a t e) -> p a t e", a=2, t=T), h["ks"][:, u], s["ks"], None)
                    dve_copy_qT(K, dve, s, b, u)

                def first(b, u):
                    for n in range(H):
                        dve_row_max(K, dve, s, b, u, n)
                    dve_place_max(K, dve, chain, s, b, u)

                def fused(b, u, more):
                    for n in range(H):
                        if more:
                            dve_row_max(K, dve, s, b + 1, 1 - u, n)
                        if n == H - 4:
                            copy_outT(K, dve, s, b, 0)
                    if more:
                        dve_place_max(K, dve, chain, s, b + 1, 1 - u)

                def finish(b, u):
                    ending.start(b)
                    dve_normalise(K, dve, ending, s, b, u, s["o"])
                    dve.wait_ge(s["wo_ps"].sem, s["wo_ps"].after(b))
                    y = K.norm["xn"][:, u].rearrange("p t d -> p (t d)")
                    y1 = cols(K.Y, b)
                    nc.vector.tensor_tensor(y1, K.PS[:, OUT0 + 1, 0:S], y, ALU.add).then_inc(s["out_banks"].sem, 1)
                    dve.wait_ge(s["out_banks"].sem, s["out_banks"].after(b))
                    x = cols(K.X, b)
                    nc.vector.scalar_tensor_tensor(x, y1, tg, x, ALU.mult, ALU.add).then_inc(ending.sem, 1)
                    dve.wait_ge(ending.sem, ending.next())

                head_pipeline(dve, prep, fused, first, finish)

            @block.scalar
            def _(act):
                for value, sem in loaded:
                    act.wait_ge(sem, value)

                def prep(b, u):
                    act.wait_ge(s["xnT_ps"].sem, s["xnT_ps"].after(b))
                    nc.scalar.activation(K.norm["xnT"][:, u, :], K.PS[:, MISC + 1, 0:S], ACT.Identity, scale=W["f1_norm1"][:, 0:1]) \
                        .then_inc(s["xnT"].sem, 1)
                    act.wait_ge(s["latT_ps"].sem, s["latT_ps"].after(b))
                    nc.scalar.activation(latT[:, u], K.PS[:, MISC, 0:S], ACT.Identity, scale=W["f1_ln_g"][:, 0:1], bias=W["f1_ln_b"][:, 0:1]) \
                        .then_inc(s["latT"].sem, 1)
                    act_copy_kT(K, act, s, b, u)

                def first(b, u):
                    act_copy_qmT(K, act, s, b, u)

                def fused(b, u, more):
                    for n in range(H):
                        act_probs(K, act, s, b, u, n, True)
                    copy_outT(K, act, s, b, 1)
                    if more:
                        act_copy_qmT(K, act, s, b + 1, 1 - u)

                def finish(b, u):
                    act.wait_ge(s["woT_ps"].sem, s["woT_ps"].after(b))
                    nc.scalar.activation(K.norm["xnT"][:, u, :], K.PS[:, OUT0, 0:S], ACT.Copy).then_inc(s["woT"].sem, 1)

                head_pipeline(act, prep, fused, first, finish)

            @block.tensor
            def _(pe):
                for value, sem in loaded:
                    pe.wait_ge(sem, value)
                pe.wait_ge(K.sem("f1_setup_step"), 3)

                def prep(b, u):
                    pe.wait_ge(s["rms"].sem, s["rms"].after(b))
                    for t in range(T):
                        mm = nc.tensor.transpose(K.PS[:, MISC + 1, t * P:(t + 1) * P], rn[:, u, t], K.ident[:])
                    mm.then_inc(s["xnT_ps"].sem, 1)
                    pe.wait_ge(s["xnT"].sem, s["xnT"].after(b))
                    for t in range(T):
                        mm = nc.tensor.matmul(K.PS[:, MISC + 1, t * (D + LAT):(t + 1) * (D + LAT)], K.norm["xnT"][:, u, t * P:(t + 1) * P],
                                              W["f1_wqd"][:], start=True, stop=True)
                    mm.then_inc(s["q_ps"].sem, 1)
                    pe.wait_ge(s["lat"].sem, s["lat"].after(b))
                    pe.wait_ge(s["qmT"].sem, s["qmT"].before(b))
                    for t in range(T):
                        mm = nc.tensor.transpose(K.PS[:, MISC, t * P:(t + 1) * P], lat[:, t], K.ident[:])
                    mm.then_inc(s["latT_ps"].sem, 1)
                    pe.wait_ge(s["latT"].sem, s["latT"].after(b))
                    for t in range(T):
                        mm = nc.tensor.matmul(K.PS[:, MISC, t * 2 * D:(t + 1) * 2 * D], latT[:, u, t * P:(t + 1) * P], wukv[:],
                                              start=True, stop=True)
                    mm.then_inc(s["kv_ps"].sem, 1)
                    pe_turn_k_and_q(K, pe, s, b, u)

                def first(b, u):
                    for n in range(H):
                        pe_scores(K, pe, s, b, u, n, True)
                    pe_turn_q_with_max(K, pe, s, b, u)

                def fused(b, u, more):
                    for n in range(H):
                        pe_scores_T(K, pe, s, b, u, n, True)
                        if more:
                            pe_scores(K, pe, s, b + 1, 1 - u, n, True)
                        if n >= 1:
                            pe_mix(K, pe, s, b, u, n - 1, True)
                    pe_mix(K, pe, s, b, u, H - 1, True)
                    if more:
                        pe_turn_q_with_max(K, pe, s, b + 1, 1 - u)

                def finish(b, u):
                    pe_turn_out(K, pe, s, b, u)
                    pe.wait_ge(s["o"].sem, s["o"].after(b))
                    for t in range(T):
                        mm = nc.tensor.transpose(K.PS[:, OUT0, t * P:(t + 1) * P], h["o"][:, u, t * P:(t + 1) * P], K.ident[:])
                    mm.then_inc(s["woT_ps"].sem, 1)
                    pe.wait_ge(s["woT"].sem, s["woT"].after(b))
                    for t in range(T):
                        mm = nc.tensor.matmul(K.PS[:, OUT0 + 1, t * D:(t + 1) * D], K.norm["xnT"][:, u, t * P:(t + 1) * P],
                                              W["f1_wo"][:], start=True, stop=True)
                    mm.then_inc(s["wo_ps"].sem, 1)

                head_pipeline(pe, prep, fused, first, finish)


NE1, HE1 = 4, 512
CE1 = HE1 // P


def first_of_four(nc, dve, chain, lg, mx, eq, oh, run):
    nc.vector.tensor_reduce(mx, lg, AX_X, ALU.max).then_inc(chain.sem, 1)
    dve.wait_ge(chain.sem, chain.next())
    nc.vector.tensor_tensor(eq, lg, mx.unsqueeze(2).broadcast_to([P, T, NE1]), ALU.is_ge).then_inc(chain.sem, 1)
    dve.wait_ge(chain.sem, chain.next())
    nc.vector.tensor_copy(oh[:, :, 0], eq[:, :, 0]).then_inc(chain.sem, 1)
    chain.next()
    nc.vector.tensor_tensor(oh[:, :, 1], eq[:, :, 1], eq[:, :, 0], ALU.is_gt).then_inc(chain.sem, 1)
    chain.next()
    nc.vector.tensor_tensor(run[:, :, 0], eq[:, :, 0], eq[:, :, 1], ALU.max).then_inc(chain.sem, 1)
    dve.wait_ge(chain.sem, chain.next())
    nc.vector.tensor_tensor(oh[:, :, 2], eq[:, :, 2], run[:, :, 0], ALU.is_gt).then_inc(chain.sem, 1)
    chain.next()
    nc.vector.tensor_tensor(run[:, :, 1], run[:, :, 0], eq[:, :, 2], ALU.max).then_inc(chain.sem, 1)
    dve.wait_ge(chain.sem, chain.next())
    nc.vector.tensor_tensor(oh[:, :, 3], eq[:, :, 3], run[:, :, 1], ALU.is_gt).then_inc(chain.sem, 1)
    dve.wait_ge(chain.sem, chain.next())


def expert_layer(K, W, loaded):
    nc = K.nc
    s = {}
    per = dict(rms_sum=1, rms_r=1, rms=1, rT_ps=1, rT=1, logits=1, up_a=NE1, up_b=NE1, ha=NE1, hb=NE1, down_ps=NE1, one_hot=1, bias=1)
    for n, k in per.items():
        s[n] = K.rising("signal_" + n, k)
    s["pool_step"] = K.rising("pool_step", 2)
    s["prep_step"] = K.rising("vector_prep_step", 2 + 1 + 8)
    s["main_step"] = K.rising("vector_finish_step", NE1 * T + 1)
    tg = K.gates[:, 5:6]

    with ExitStack() as ctx:
        def sb(name, shape, dt=F32):
            return ctx.enter_context(nc.sbuf_tensor("m1_" + name, shape, dt))

        sq, ss, rr, rn = sb("squares", [P, T, D]), sb("square_sums", [P, 2, T]), sb("inverse_rms", [P, 2, T]), sb("rms_rows", [P, 2, T, D])
        rT = sb("rowsT", [P, 2, T * P])
        lg, mx, eq, run = sb("logits", [P, T, NE1]), sb("logit_max", [P, T]), sb("equals_max", [P, T, NE1]), sb("taken", [P, T, 2])
        oh, ohg = sb("one_hot", [P, T, NE1]), sb("gated_one_hot", [P, 2, T, NE1])
        hT = sb("hiddenT", [P, 2, CE1, S])
        bt = sb("biases", [P, 2, NE1, S])

        with nc.Block() as block:

            @block.gpsimd
            def _(pool):
                for value, sem in loaded:
                    pool.wait_ge(sem, value)
                ps = s["pool_step"]

                def prep(b, u):
                    pool.wait_ge(s["rms_sum"].sem, s["rms_sum"].after(b))
                    nc.gpsimd.tensor_tensor(rr[:, u], ss[:, u], K.neghalf[:, 0:T], ALU.pow).then_inc(s["rms_r"].sem, 1)
                    pool.wait_ge(s["one_hot"].sem, s["one_hot"].after(b))
                    nc.gpsimd.tensor_tensor(bt[:, u].rearrange("p e (t d) -> p e t d", t=T),
                                            W["f1_b2"][:].rearrange("p (e d) -> p e d", e=NE1).unsqueeze(2).broadcast_to([P, NE1, T, D]),
                                            ohg[:, u].rearrange("p t e -> p e t").unsqueeze(3).broadcast_to([P, NE1, T, D]), ALU.mult) \
                        .then_inc(ps.sem, 1)
                    pool.wait_ge(ps.sem, ps.after(b, 1))
                    nc.gpsimd.tensor_tensor(bt[:, u, 0:2], bt[:, u, 0:2], bt[:, u, 2:4], ALU.add).then_inc(ps.sem, 1)
                    pool.wait_ge(ps.sem, ps.after(b, 2))
                    nc.gpsimd.tensor_tensor(bt[:, u, 0], bt[:, u, 0], bt[:, u, 1], ALU.add).then_inc(s["bias"].sem, 1)
                software_pipeline(pool, prep, lambda b, u: None)

            @block.vector
            def _(dve):
                for value, sem in loaded:
                    dve.wait_ge(sem, value)
                chain, ending = Chain(s["prep_step"]), Chain(s["main_step"])

                def prep(b, u):
                    chain.start(b)
                    y1 = cols(K.Y, b)
                    nc.vector.tensor_tensor(sq[:].rearrange("p t d -> p (t d)"), y1, y1, ALU.mult).then_inc(chain.sem, 1)
                    dve.wait_ge(chain.sem, chain.next())
                    nc.vector.tensor_reduce(ss[:, u], sq[:], AX_X, ALU.add).then_inc(chain.sem, 1)
                    dve.wait_ge(chain.sem, chain.next())
                    nc.vector.tensor_scalar(ss[:, u], ss[:, u], 1.0 / D, 1e-6, ALU.mult, ALU.add).then_inc(s["rms_sum"].sem, 1)
                    dve.wait_ge(s["rms_r"].sem, s["rms_r"].after(b))
                    nc.vector.tensor_tensor(rn[:, u], y1.rearrange("p (t d) -> p t d", t=T), rr[:, u].unsqueeze(2).broadcast_to([P, T, D]), ALU.mult) \
                        .then_inc(s["rms"].sem, 1)
                    dve.wait_ge(s["logits"].sem, s["logits"].after(b))
                    nc.vector.tensor_tensor(lg[:], K.PS[:, MISC + 1, 0:T * NE1].rearrange("p (t e) -> p t e", t=T),
                                            W["f1_gate_b"][:].unsqueeze(1).broadcast_to([P, T, NE1]), ALU.add).then_inc(chain.sem, 1)
                    dve.wait_ge(chain.sem, chain.next())
                    first_of_four(nc, dve, chain, lg[:], mx[:], eq[:], oh, run)
                    nc.vector.tensor_scalar(ohg[:, u], oh[:], tg, None, ALU.mult).then_inc(s["one_hot"].sem, 1)
                    dve.wait_ge(s["one_hot"].sem, s["one_hot"].after(b))

                def main(b, u):
                    ending.start(b)

                    def add_expert(e):
                        dve.wait_ge(s["down_ps"].sem, s["down_ps"].after(b, e + 1))
                        for t in range(T):
                            x = K.X[:, bass.ds(b * S + t * P, P)]
                            if t == 0 and e > 0:
                                dve.wait_ge(ending.sem, ending.reached())
                            ins = nc.vector.scalar_tensor_tensor(x, K.PS[:, OUT0 + e % 2, t * D:(t + 1) * D], ohg[:, u, t, e:e + 1], x, ALU.mult, ALU.add)
                            ins.then_inc(ending.sem, 1)
                            ending.next()

                    for e in range(NE1):
                        dve.wait_ge(s["up_b"].sem, s["up_b"].after(b, e + 1))
                        for c in range(2, CE1):
                            ins = nc.vector.tensor_scalar(hT[:, e % 2, c], K.PS[:, 2 * (e % 2) + 1, (c - 2) * S:(c - 1) * S],
                                                          W["f1_b1"][:, e * CE1 + c:e * CE1 + c + 1], 0.0, ALU.add, ALU.max)
                        ins.then_inc(s["hb"].sem, 1)
                        if e >= 1:
                            add_expert(e - 1)
                    add_expert(NE1 - 1)
                    dve.wait_ge(ending.sem, ending.reached())
                    dve.wait_ge(s["bias"].sem, s["bias"].after(b))
                    x = cols(K.X, b)
                    nc.vector.tensor_tensor(x, x, bt[:, u, 0], ALU.add).then_inc(ending.sem, 1)
                    dve.wait_ge(ending.sem, ending.next())

                software_pipeline(dve, prep, main)

            @block.scalar
            def _(act):
                for value, sem in loaded:
                    act.wait_ge(sem, value)

                def prep(b, u):
                    act.wait_ge(s["rT_ps"].sem, s["rT_ps"].after(b))
                    nc.scalar.activation(rT[:, u, :], K.PS[:, MISC, 0:S], ACT.Identity, scale=W["f1_norm2"][:, 0:1]).then_inc(s["rT"].sem, 1)

                def main(b, u):
                    for e in range(NE1):
                        act.wait_ge(s["up_a"].sem, s["up_a"].after(b, e + 1))
                        for c in range(2):
                            ins = nc.scalar.activation(hT[:, e % 2, c], K.PS[:, 2 * (e % 2), c * S:(c + 1) * S], ACT.Relu,
                                                       bias=W["f1_b1"][:, e * CE1 + c:e * CE1 + c + 1])
                        ins.then_inc(s["ha"].sem, 1)

                software_pipeline(act, prep, main)

            @block.tensor
            def _(pe):
                for value, sem in loaded:
                    pe.wait_ge(sem, value)

                def prep(b, u):
                    pe.wait_ge(s["rms"].sem, s["rms"].after(b))
                    for t in range(T):
                        mm = nc.tensor.transpose(K.PS[:, MISC, t * P:(t + 1) * P], rn[:, u, t], K.ident[:])
                    mm.then_inc(s["rT_ps"].sem, 1)
                    pe.wait_ge(s["rT"].sem, s["rT"].after(b))
                    for t in range(T):
                        mm = nc.tensor.matmul(K.PS[:, MISC + 1, t * NE1:(t + 1) * NE1], rT[:, u, t * P:(t + 1) * P], W["f1_gate_w"][:],
                                              start=True, stop=True)
                    mm.then_inc(s["logits"].sem, 1)

                def main(b, u):
                    def up(e):
                        for c in range(CE1):
                            mm = nc.tensor.matmul(K.PS[:, 2 * (e % 2) + c // 2, (c % 2) * S:(c % 2 + 1) * S],
                                                  W["f1_w1"][:, (e * CE1 + c) * P:(e * CE1 + c + 1) * P], rT[:, u, :], start=True, stop=True)
                            if c % 2:
                                mm.then_inc(s["up_a" if c == 1 else "up_b"].sem, 1)

                    def down(e):
                        pe.wait_ge(s["ha"].sem, s["ha"].after(b, e + 1))
                        pe.wait_ge(s["hb"].sem, s["hb"].after(b, e + 1))
                        for t in range(T):
                            for c in range(CE1):
                                mm = nc.tensor.matmul(K.PS[:, OUT0 + e % 2, t * D:(t + 1) * D], hT[:, e % 2, c, t * P:(t + 1) * P],
                                                      W["f1_w2"][:, (e * CE1 + c) * D:(e * CE1 + c + 1) * D], start=c == 0, stop=c == CE1 - 1)
                        mm.then_inc(s["down_ps"].sem, 1)

                    for e in range(NE1):
                        up(e)
                        if e >= 1:
                            down(e - 1)
                    down(NE1 - 1)

                software_pipeline(pe, prep, main)


def latent_moe_layer(K, W, loaded):
    latent_attention_layer(K, W, loaded)
    expert_layer(K, W, loaded)



NE2, HE2, K2 = 16, 64, 8
F2 = NE2 * HE2
HC2 = 512
F2C = F2 // P


def routed_ffn_layer(K, W, loaded, load_late):
    nc = K.nc
    s = ln_signals(K)
    s["pool_step"] = K.rising("pool_step", 1)
    s["prep_step"] = K.rising("vector_prep_step", LN_STEPS + 2 + 2 * T + 3)
    s["main_step"] = K.rising("vector_finish_step", T)
    per = dict(row_sum=1, row_r=1, logits=1, scores=1, weights=1, gu_ps=3 * T, g=3 * T, h=3 * T, hw=2 * T, hT_ps=3 * T, hT=3 * T, down_ps=1)
    for n, k in per.items():
        s[n] = K.rising("signal_" + n, k)
    tg = K.gates[:, 6:7]

    with ExitStack() as ctx:
        def sb(name, shape, dt=F32):
            return ctx.enter_context(nc.sbuf_tensor("f2_" + name, shape, dt))

        gsq, gss, gr, gn, gT = sb("gate_squares", [NE2, D]), sb("gate_sum", [NE2, 1]), sb("gate_r", [NE2, 1]), sb("gate_rows", [NE2, D]), sb("gateT", [P, NE2])
        sq, ss, rr = sb("squares", [P, T, D]), sb("square_sums", [P, 2, T]), sb("inverse_norms", [P, 2, T])
        sc, top, left, sel = sb("scores", [P, 2, T, NE2]), sb("top", [P, T, K2]), sb("left", [P, T, NE2]), sb("selected", [P, T, NE2])
        tot, wt = sb("top_sum", [P, T]), sb("weights", [P, 2, T, NE2])
        g, h = sb("gate", [P, 2, HC2]), sb("hidden", [P, 2, HC2])
        hT = sb("hiddenT", [P, 2, HC2])

        steps = [(t, c) for t in range(T) for c in range(3)]
        width = (HC2, HC2, HE2)

        with nc.Block() as block:

            @block.sync
            def _(sp):
                load_late(sp)

            @block.vector
            def _(dve):
                for value, sem in loaded:
                    dve.wait_ge(sem, value)
                setup = K.sem("f2_setup_step")
                nc.vector.tensor_tensor(gsq[:], W["f2_gate_w"][:], W["f2_gate_w"][:], ALU.mult).then_inc(setup, 1)
                dve.wait_ge(setup, 1)
                nc.vector.tensor_reduce(gss[:], gsq[:], AX_X, ALU.add).then_inc(setup, 1)
                dve.wait_ge(setup, 2)
                nc.vector.tensor_scalar(gss[:], gss[:], 1e-24, None, ALU.max).then_inc(setup, 1)
                dve.wait_ge(K.sem("f2_gate_norm"), 1)
                nc.vector.tensor_scalar(gn[:], W["f2_gate_w"][:], gr[:, 0:1], None, ALU.mult).then_inc(setup, 1)
                dve.wait_ge(K.sem("f2_gate_turned"), 1)
                nc.vector.tensor_copy(gT[:], K.PS[:, MISC, 0:NE2]).then_inc(setup, 1)
                chain, ending = Chain(s["prep_step"]), Chain(s["main_step"])

                def prep(b, u):
                    chain.start(b)
                    dve_layernorm(K, dve, chain, s, b, u)
                    y = K.norm["xn"][:, u]
                    dve.wait_ge(s["xn"].sem, s["xn"].after(b))
                    nc.vector.tensor_tensor(sq[:], y, y, ALU.mult).then_inc(chain.sem, 1)
                    dve.wait_ge(chain.sem, chain.next())
                    nc.vector.tensor_reduce(ss[:, u], sq[:], AX_X, ALU.add).then_inc(chain.sem, 1)
                    dve.wait_ge(chain.sem, chain.next())
                    nc.vector.tensor_scalar(ss[:, u], ss[:, u], 1e-24, None, ALU.max).then_inc(s["row_sum"].sem, 1)
                    dve.wait_ge(s["scores"].sem, s["scores"].after(b))
                    settled(dve, K)
                    for t in range(T):
                        nc.vector.max(top[:, t], sc[:, u, t]).then_inc(chain.sem, 1)
                        chain.next()
                    dve.wait_ge(chain.sem, chain.reached())
                    settled(dve, K)
                    for t in range(T):
                        nc.vector.match_replace(left[:, t], top[:, t], sc[:, u, t], -1.0).then_inc(chain.sem, 1)
                        chain.next()
                    dve.wait_ge(chain.sem, chain.reached())
                    nc.vector.tensor_reduce(tot[:], top[:], AX_X, ALU.add).then_inc(chain.sem, 1)
                    chain.next()
                    nc.vector.scalar_tensor_tensor(sel[:], left[:], 0.0, sc[:, u], ALU.is_lt, ALU.mult).then_inc(chain.sem, 1)
                    dve.wait_ge(chain.sem, chain.next())
                    nc.vector.reciprocal(tot[:], tot[:]).then_inc(chain.sem, 1)
                    dve.wait_ge(chain.sem, chain.next())
                    nc.vector.tensor_tensor(wt[:, u], sel[:], tot[:].unsqueeze(2).broadcast_to([P, T, NE2]), ALU.mult).then_inc(s["weights"].sem, 1)

                def main(b, u):
                    ending.start(b)
                    for n, (t, c) in enumerate(steps):
                        w = width[c]
                        dve.wait_ge(s["g"].sem, s["g"].after(b, n + 1))
                        nc.vector.tensor_tensor(h[:, n % 2, 0:w], K.PS[:, 2 * (n % 2) + 1, 0:w], g[:, n % 2, 0:w], ALU.mult).then_inc(s["h"].sem, 1)
                    dve.wait_ge(s["down_ps"].sem, s["down_ps"].after(b))
                    for t in range(T):
                        x = K.X[:, bass.ds(b * S + t * P, P)]
                        nc.vector.scalar_tensor_tensor(x, K.PS[:, OUT0, t * D:(t + 1) * D], tg, x, ALU.mult, ALU.add).then_inc(ending.sem, 1)
                        ending.next()
                    dve.wait_ge(ending.sem, ending.reached())

                software_pipeline(dve, prep, main)

            @block.gpsimd
            def _(pool):
                pool.wait_ge(K.sem("f2_setup_step"), 3)
                nc.gpsimd.tensor_tensor(gr[:], gss[:], K.neghalf[0:NE2, 0:1], ALU.pow).then_inc(K.sem("f2_gate_norm"), 1)

                def prep(b, u):
                    pool_rstd(K, pool, s, b, u)
                    pool.wait_ge(s["row_sum"].sem, s["row_sum"].after(b))
                    nc.gpsimd.tensor_tensor(rr[:, u], ss[:, u], K.neghalf[:, 0:T], ALU.pow).then_inc(s["row_r"].sem, 1)

                def main(b, u):
                    pool.wait_ge(s["weights"].sem, s["weights"].after(b))
                    k = 0
                    for n, (t, c) in enumerate(steps):
                        if c == 2:
                            continue
                        k += 1
                        pool.wait_ge(s["h"].sem, s["h"].after(b, n + 1))
                        hw = h[:, n % 2].rearrange("p (e j) -> p e j", j=HE2)
                        ne = HC2 // HE2
                        nc.gpsimd.tensor_tensor(hw, hw, wt[:, u, t, c * ne:(c + 1) * ne].unsqueeze(2).broadcast_to([P, ne, HE2]), ALU.mult) \
                            .then_inc(s["hw"].sem, 1)

                software_pipeline(pool, prep, main)

            @block.scalar
            def _(act):
                def prep(b, u):
                    act_xn_transposed(K, act, s, b, u, MISC + 1 - 2 * u)
                    act.wait_ge(s["row_r"].sem, s["row_r"].after(b))
                    act.wait_ge(s["logits"].sem, s["logits"].after(b))
                    for t in range(T):
                        ins = nc.scalar.activation(sc[:, u, t], K.PS[:, MISC + 1 - 2 * u, S + t * NE2:S + (t + 1) * NE2], ACT.Sigmoid, scale=rr[:, u, t:t + 1])
                    ins.then_inc(s["scores"].sem, 1)

                def main(b, u):
                    def turned(n):
                        act.wait_ge(s["hT_ps"].sem, s["hT_ps"].after(b, n + 1))
                        w = width[steps[n][1]]
                        if w == HC2:
                            ins = nc.scalar.activation(hT[:, n % 2], K.PS[:, MISC, :], ACT.Copy)
                        else:
                            ins = nc.scalar.activation(hT[0:HE2, n % 2, 0:P], K.PS[0:HE2, MISC, 0:P], ACT.Copy)
                        ins.then_inc(s["hT"].sem, 1)

                    for n, (t, c) in enumerate(steps):
                        w = width[c]
                        act.wait_ge(s["gu_ps"].sem, s["gu_ps"].after(b, n + 1))
                        if n >= 2:
                            act.wait_ge(s["h"].sem, s["h"].after(b, n - 1))
                        nc.scalar.activation(g[:, n % 2, 0:w], K.PS[:, 2 * (n % 2), 0:w], ACT.Silu).then_inc(s["g"].sem, 1)
                        if n >= 1:
                            turned(n - 1)
                    turned(len(steps) - 1)

                software_pipeline(act, prep, main)

            @block.tensor
            def _(pe):
                pe.wait_ge(K.sem("f2_setup_step"), 4)
                nc.tensor.transpose(K.PS[:, MISC, 0:NE2], gn[:], K.ident[0:NE2, 0:NE2]).then_inc(K.sem("f2_gate_turned"), 1)
                pe.wait_ge(K.sem("f2_setup_step"), 5)

                def prep(b, u):
                    bank = MISC + 1 - 2 * u
                    pe_xn_transposed(K, pe, s, b, u, bank)
                    pe.wait_ge(s["xnT"].sem, s["xnT"].after(b))
                    for t in range(T):
                        mm = nc.tensor.matmul(K.PS[:, bank, S + t * NE2:S + (t + 1) * NE2], K.norm["xnT"][:, u, t * P:(t + 1) * P], gT[:], start=True, stop=True)
                    mm.then_inc(s["logits"].sem, 1)

                def main(b, u):
                    def up(n):
                        t, c = steps[n]
                        w = width[c]
                        for k, name in enumerate(("f2_wg", "f2_wu")):
                            mm = nc.tensor.matmul(K.PS[:, 2 * (n % 2) + k, 0:w], K.norm["xnT"][:, u, t * P:(t + 1) * P], W[name][:, c * HC2:c * HC2 + w],
                                                  start=True, stop=True)
                        mm.then_inc(s["gu_ps"].sem, 1)

                    def turn(n):
                        t, c = steps[n]
                        if n >= 1:
                            pe.wait_ge(s["hT"].sem, s["hT"].after(b, n))
                        if c < 2:
                            pe.wait_ge(s["hw"].sem, s["hw"].after(b, 2 * t + c + 1))
                            for k in range(HC2 // P):
                                mm = nc.tensor.transpose(K.PS[:, MISC, k * P:(k + 1) * P], h[:, n % 2, k * P:(k + 1) * P], K.ident[:])
                        else:
                            pe.wait_ge(s["h"].sem, s["h"].after(b, n + 1))
                            settled(pe, K)
                            mm = nc.tensor.transpose(K.PS[0:HE2, MISC, 0:P], h[:, n % 2, 0:HE2], K.ident[:])
                        mm.then_inc(s["hT_ps"].sem, 1)

                    def down(n):
                        t, c = steps[n]
                        pe.wait_ge(s["hT"].sem, s["hT"].after(b, n + 1))
                        out = K.PS[:, OUT0, t * D:(t + 1) * D]
                        if c < 2:
                            for k in range(HC2 // P):
                                mm = nc.tensor.matmul(out, hT[:, n % 2, k * P:(k + 1) * P], W["f2_wd"][:, (4 * c + k) * D:(4 * c + k + 1) * D],
                                                      start=c == 0 and k == 0, stop=False)
                        else:
                            mm = nc.tensor.matmul(out, hT[0:HE2, n % 2, 0:P], W["f2_sd"][:], start=False, stop=True)
                        return mm

                    for n in range(len(steps)):
                        up(n)
                        if n >= 1:
                            turn(n - 1)
                        if n >= 2:
                            down(n - 2)
                    down(len(steps) - 2)
                    turn(len(steps) - 1)
                    down(len(steps) - 1).then_inc(s["down_ps"].sem, 1)

                software_pipeline(pe, prep, main)



H3, DH3 = 2, 64
KT3 = 2 * T
V3 = DH3 + 1
U3 = 4
MISC3 = 7


def perceiver_attention_layer(K, W, loaded):
    nc = K.nc
    s = ln_signals(K, turned=False)
    s["pool_step"] = K.rising("pool_step", 3)
    s["prep_step"] = K.rising("vector_prep_step", LN_STEPS + 4 + 4 + 1 + 1 + 3)
    s["finish_step"] = K.rising("vector_finish_step", 1 + 1)
    per = dict(c_stats=1, c_rstd=1, c_rows=1, z_stats=1, z_rstd=1, z=1, sq=1, ssq=1, r=1, q_rows=1, k_rows=1, filled=MISC3, read=MISC3,
               smax_ps=U3, smax=U3, m=1, mT_ps=1, mT=1, st_ps=U3, p=U3, mix=1, o=1, oT_ps=1, oT=1, wo_ps=1, out_banks=1, hide=1)
    for n, k in per.items():
        s[n] = K.rising("signal_" + n, k)
    tg = K.gates[:, 3:4]

    with ExitStack() as ctx:
        def sb(name, shape, dt=F32):
            return ctx.enter_context(nc.sbuf_tensor("x3_" + name, shape, dt))

        qk = sb("qk_gain", [P, 1])
        cst, cmv, cve, crs = sb("c_stats", [P, T, 6]), sb("c_mean_var", [P, 2, T, 2]), sb("c_var_eps", [P, T]), sb("c_rstd", [P, 2, T])
        cn, cnT = sb("c_rows", [P, 2, T, C]), sb("cT", [C, 2, S])
        zst, zmv, zve, zrs = sb("z_stats", [P, T, 6]), sb("z_mean_var", [P, 2, T, 2]), sb("z_var_eps", [P, T]), sb("z_rstd", [P, 2, T])
        z, zT = sb("latent_rows", [P, 2, T, D]), sb("latentT", [P, 2, S])
        raw, sq = sb("raw", [P, 3, T, D]), sb("sq", [P, 3, T, D])
        ssq, rn = sb("sum_squares", [P, 2, 3, T, H3]), sb("inverse_norms", [P, 2, 3, T, H3])
        qn, kn = sb("q_rows", [P, T, H3, P]), sb("k_rows", [P, KT3, P])
        ve = sb("v_with_one", [P, 2, KT3, H3, V3])
        qT, kT = sb("qT", [P, 2, H3, S]), sb("kT", [P, 2, KT3 * P])
        nm, nrest = sb("minus_max", [P, 2, T, H3]), sb("rest", [P, T, H3])
        mtok, mT = sb("max_rows", [P, T, P], BF16), sb("maxT", [P, 2, S], BF16)
        hide = sb("hide_keys", [P, 2, T])
        p = sb("probs", [P, 2, 2, S])
        rec, o, oT = sb("inverse_sums", [P, T, H3]), sb("out_rows", [P, 2, T, H3, DH3]), sb("outT", [P, S])

        with nc.Block() as block:

            @block.vector
            def _(dve):
                nc.vector.memset(qn[:], 0.0)
                nc.vector.memset(mtok[:], 0.0)
                nc.vector.memset(ve[:, :, :, :, DH3:V3], 1.0)
                for value, sem in loaded:
                    dve.wait_ge(sem, value)
                setup = K.sem("x3_setup_step")
                nc.vector.tensor_tensor(qk[:], W["x3_qg"][:], W["x3_kg"][:], ALU.mult).then_inc(setup, 1)
                dve.wait_ge(setup, 1)
                nc.vector.tensor_scalar(qk[:], qk[:], DH3 ** -0.5, None, ALU.mult).then_inc(setup, 1)
                nc.vector.tensor_scalar(K.hide_cols[:], K.mask_k3c[:], 1.0, -HIDE, ALU.subtract, ALU.mult).then_inc(setup, 1)
                nc.vector.tensor_scalar(K.hide_rows[:], K.mask_k3[:], 1.0, -HIDE, ALU.subtract, ALU.mult).then_inc(setup, 1)
                dve.wait_ge(setup, 4)
                chain, ending = Chain(s["prep_step"]), Chain(s["finish_step"])

                def stats(b, u, st, mv, rows, signal):
                    settled(dve, K)
                    for t in range(T):
                        nc.vector.bn_stats(st[:, t], rows(t)).then_inc(chain.sem, 1)
                        chain.next()
                    dve.wait_ge(chain.sem, chain.reached())
                    settled(dve, K)
                    nc.vector.bn_aggr(mv[:, u, 0], st[:, 0]).then_inc(chain.sem, 1)
                    chain.next()
                    nc.vector.bn_aggr(mv[:, u, 1], st[:, 1]).then_inc(signal.sem, 1)

                def normalise(b, u, dst, rows, mv, rs, rstd, signal):
                    dve.wait_ge(rstd.sem, rstd.after(b))
                    nc.vector.tensor_scalar(dst[:, u, 0], rows(0), mv[:, u, 0, 0:1], rs[:, u, 0:1], ALU.subtract, ALU.mult).then_inc(chain.sem, 1)
                    chain.next()
                    nc.vector.tensor_scalar(dst[:, u, 1], rows(1), mv[:, u, 1, 0:1], rs[:, u, 1:2], ALU.subtract, ALU.mult).then_inc(signal.sem, 1)

                def prep(b, u):
                    chain.start(b)
                    c_rows = lambda t: K.ctx_rows[:, bass.ds(b * (T * C) + t * C, C)]
                    stats(b, u, cst, cmv, c_rows, s["c_stats"])
                    normalise(b, u, cn, c_rows, cmv, crs, s["c_rstd"], s["c_rows"])
                    dve_layernorm(K, dve, chain, s, b, u)
                    dve.wait_ge(s["xn"].sem, s["xn"].after(b))
                    y = lambda t: K.norm["xn"][:, u, t]
                    stats(b, u, zst, zmv, y, s["z_stats"])
                    normalise(b, u, z, y, zmv, zrs, s["z_rstd"], s["z"])
                    dve.wait_ge(s["sq"].sem, s["sq"].after(b))
                    nc.vector.tensor_reduce(ssq[:, u].rearrange("p k t h -> p (k t h)"), sq[:].rearrange("p k t (h e) -> p (k t h) e", e=DH3), AX_X, ALU.add).then_inc(chain.sem, 1)
                    dve.wait_ge(chain.sem, chain.next())
                    nc.vector.tensor_scalar(ssq[:, u], ssq[:, u], 1.0 / DH3, 1e-16, ALU.mult, ALU.max).then_inc(s["ssq"].sem, 1)
                    dve.wait_ge(s["r"].sem, s["r"].after(b))
                    nc.vector.tensor_tensor(kn[:].rearrange("p k (h e) -> p (k h) e", e=DH3), raw[:, 1:3].rearrange("p k t (h e) -> p (k t h) e", e=DH3),
                                            rn[:, u, 1:3].rearrange("p k t h -> p (k t h)").unsqueeze(2).broadcast_to([P, KT3 * H3, DH3]), ALU.mult) \
                        .then_inc(s["k_rows"].sem, 1)
                    for hd in range(H3):
                        es = slice(hd * DH3, (hd + 1) * DH3)
                        ins = nc.vector.tensor_tensor(qn[:, :, hd, es], raw[:, 0, :, es], rn[:, u, 0, :, hd:hd + 1].broadcast_to([P, T, DH3]), ALU.mult)
                        if hd == 0:
                            ins.then_inc(chain.sem, 1)
                            chain.next()
                    ins.then_inc(s["q_rows"].sem, 1)

                def row_max(b, u, i):
                    dve.wait_ge(s["smax_ps"].sem, s["smax_ps"].after(b, i + 1))
                    nc.vector.tensor_reduce(nm[:, u, i % 2, i // 2:i // 2 + 1], K.PS[:, SMAX0 + i % 2, :], AX_X, ALU.max, negate=True) \
                        .then_inc(s["smax"].sem, 1)

                def place_max(b, u):
                    m = mtok[:, :, 0:3 * H3].rearrange("p t (h i) -> p t h i", i=3)
                    dve.wait_ge(s["smax"].sem, s["smax"].after(b))
                    nc.vector.tensor_copy(m[:, :, :, 0], nm[:, u]).then_inc(chain.sem, 1)
                    dve.wait_ge(chain.sem, chain.next())
                    nc.vector.tensor_tensor(nrest[:], nm[:, u], m[:, :, :, 0], ALU.subtract).then_inc(chain.sem, 1)
                    dve.wait_ge(chain.sem, chain.next())
                    nc.vector.tensor_copy(m[:, :, :, 1], nrest[:]).then_inc(chain.sem, 1)
                    dve.wait_ge(chain.sem, chain.next())
                    nc.vector.tensor_tensor(m[:, :, :, 2], nrest[:], m[:, :, :, 1], ALU.subtract).then_inc(s["m"].sem, 1)

                def first(b, u):
                    for i in range(U3):
                        row_max(b, u, i)
                    place_max(b, u)

                def fused(b, u, more):
                    if more:
                        first(b + 1, 1 - u)

                def finish(b, u):
                    ending.start(b)
                    dve.wait_ge(s["mix"].sem, s["mix"].after(b))
                    ob = K.PS[:, OUT0:OUT0 + T, 0:H3 * V3].rearrange("p t (h e) -> p t h e", e=V3)
                    nc.vector.reciprocal(rec[:], ob[:, :, :, DH3]).then_inc(ending.sem, 1)
                    dve.wait_ge(ending.sem, ending.next())
                    nc.vector.tensor_tensor(o[:, u], ob[:, :, :, 0:DH3], rec[:].unsqueeze(3).broadcast_to([P, T, H3, DH3]), ALU.mult).then_inc(s["o"].sem, 1)
                    dve.wait_ge(s["wo_ps"].sem, s["wo_ps"].after(b))
                    o3 = o[:, u].rearrange("p t h e -> p t (h e)")
                    nc.vector.tensor_tensor(o3, K.PS[:, OUT0 + 1, 0:S].rearrange("p (t d) -> p t d", t=T),
                                            W["x3_bo"][:].unsqueeze(1).broadcast_to([P, T, D]), ALU.add).then_inc(s["out_banks"].sem, 1)
                    dve.wait_ge(s["out_banks"].sem, s["out_banks"].after(b))
                    x = cols(K.X, b)
                    nc.vector.scalar_tensor_tensor(x, o[:, u].rearrange("p t h e -> p (t h e)"), tg, x, ALU.mult, ALU.add).then_inc(ending.sem, 1)
                    dve.wait_ge(ending.sem, ending.next())

                head_pipeline(dve, prep, fused, first, finish)

            @block.gpsimd
            def _(pool):
                pool.wait_ge(K.sem("x3_setup_step"), 3)
                ps = s["pool_step"]

                def rstd(b, u, k, stats, mv, ve_, rs, signal):
                    pool.wait_ge(stats.sem, stats.after(b))
                    nc.gpsimd.tensor_tensor(ve_[:], mv[:, u, :, 1], K.eps5[:, 0:T], ALU.add).then_inc(ps.sem, 1)
                    pool.wait_ge(ps.sem, ps.after(b, k))
                    nc.gpsimd.tensor_tensor(rs[:, u], ve_[:], K.neghalf[:, 0:T], ALU.pow).then_inc(signal.sem, 1)

                def prep(b, u):
                    rstd(b, u, 1, s["c_stats"], cmv, cve, crs, s["c_rstd"])
                    nc.gpsimd.tensor_copy(hide[:, u, :], K.hide_cols[:, bass.ds(b * T, T)]).then_inc(s["hide"].sem, 1)
                    pool.wait_ge(s["stats"].sem, s["stats"].after(b))
                    n = K.norm
                    nc.gpsimd.tensor_tensor(n["ve"][:, u, :], n["mv"][:, u, :, 1], K.eps5[:, 0:T], ALU.add).then_inc(ps.sem, 1)
                    pool.wait_ge(ps.sem, ps.after(b, 2))
                    nc.gpsimd.tensor_tensor(n["rs"][:, u, :], n["ve"][:, u, :], K.neghalf[:, 0:T], ALU.pow).then_inc(s["rstd"].sem, 1)
                    rstd(b, u, 3, s["z_stats"], zmv, zve, zrs, s["z_rstd"])
                    pool.wait_ge(s["ssq"].sem, s["ssq"].after(b))
                    nc.gpsimd.tensor_tensor(rn[:, u].rearrange("p k t h -> p (k t h)"), ssq[:, u].rearrange("p k t h -> p (k t h)"),
                                            K.neghalf[:, 0:1].broadcast_to([P, 3 * T * H3]), ALU.pow).then_inc(s["r"].sem, 1)

                def nothing(b, u, more=None):
                    pass
                head_pipeline(pool, prep, nothing, nothing, nothing)

            @block.scalar
            def _(act):
                for value, sem in loaded:
                    act.wait_ge(sem, value)
                act.wait_ge(K.sem("x3_setup_step"), 2)

                def bank_of(b, u, f):
                    act.wait_ge(s["filled"].sem, s["filled"].after(b, f + 1))
                    return K.PS[:, MISC + (u + f) % 2, :]

                def prep(b, u):
                    read = s["read"].sem
                    nc.scalar.activation(cnT[:, u], bank_of(b, u, 0)[0:C, 0:S], ACT.Identity, scale=W["x3_lx_g"][:, 0:1], bias=W["x3_lx_b"][:, 0:1]).then_inc(read, 1)
                    bank = bank_of(b, u, 1)[:, :].rearrange("p (t n) -> p t n", t=T)
                    nc.scalar.activation(raw[:, 1], bank[:, :, 0:D], ACT.Copy)
                    nc.scalar.activation(sq[:, 1], bank[:, :, 0:D], ACT.Square)
                    nc.scalar.activation(ve[:, u, 0:T, :, 0:DH3], bank[:, :, D:2 * D].rearrange("p t (h e) -> p t h e", e=DH3), ACT.Copy).then_inc(read, 1)
                    nc.scalar.activation(zT[:, u], bank_of(b, u, 2)[:, 0:S], ACT.Identity, scale=W["x3_ll_g"][:, 0:1], bias=W["x3_ll_b"][:, 0:1]).then_inc(read, 1)
                    for t in range(T):
                        bank = bank_of(b, u, 3 + t)
                        nc.scalar.activation(raw[:, 0::2, t], bank[:, 0:2 * D].rearrange("p (k d) -> p k d", k=2), ACT.Copy)
                        ins = nc.scalar.activation(sq[:, 0::2, t], bank[:, 0:2 * D].rearrange("p (k d) -> p k d", k=2), ACT.Square)
                        if t == T - 1:
                            ins.then_inc(s["sq"].sem, 1)
                        nc.scalar.activation(ve[:, u, T + t, :, 0:DH3], bank[:, 2 * D:3 * D].rearrange("p (h e) -> p h e", e=DH3), ACT.Copy).then_inc(read, 1)
                    nc.scalar.activation(kT[:, u], bank_of(b, u, 5), ACT.Copy).then_inc(read, 1)
                    nc.scalar.activation(qT[:, u].rearrange("p h n -> p (h n)"), bank_of(b, u, 6), ACT.Identity, scale=qk[:, 0:1]).then_inc(read, 1)

                def maxima(b, u):
                    act.wait_ge(s["mT_ps"].sem, s["mT_ps"].after(b))
                    nc.scalar.activation(mT[:, u], K.PS[:, SMAX0, 0:P].bitcast(BF16), ACT.Copy).then_inc(s["mT"].sem, 1)

                def fused(b, u, more):
                    act.wait_ge(s["hide"].sem, s["hide"].after(b))
                    for i in range(U3):
                        act.wait_ge(s["st_ps"].sem, s["st_ps"].after(b, i + 1))
                        bank = K.PS[:, ST0 + i % 2, :]
                        if i % 2 == 0:
                            for kt in range(2):
                                ins = nc.scalar.activation(p[:, 0, kt], bank[:, kt * S:(kt + 1) * S], ACT.Exp, bias=hide[:, u, kt:kt + 1])
                        else:
                            ins = nc.scalar.activation(p[:, 1].rearrange("p k n -> p (k n)"), bank, ACT.Exp)
                        ins.then_inc(s["p"].sem, 1)
                    if more:
                        maxima(b + 1, 1 - u)

                def finish(b, u):
                    act.wait_ge(s["oT_ps"].sem, s["oT_ps"].after(b))
                    nc.scalar.activation(oT[:], K.PS[:, OUT0, 0:S], ACT.Copy).then_inc(s["oT"].sem, 1)

                head_pipeline(act, prep, fused, maxima, finish)

            @block.tensor
            def _(pe):
                for value, sem in loaded:
                    pe.wait_ge(sem, value)
                pe.wait_ge(K.sem("x3_setup_step"), 4)

                def bank_for(b, u, f):
                    pe.wait_ge(s["read"].sem, b * MISC3 + (s["read"].base + f - 1))
                    return K.PS[:, MISC + (u + f) % 2, :]

                def prep(b, u):
                    filled = s["filled"].sem
                    pe.wait_ge(s["c_rows"].sem, s["c_rows"].after(b))
                    bank = bank_for(b, u, 0)
                    for t in range(T):
                        mm = nc.tensor.transpose(bank[0:C, t * P:(t + 1) * P], cn[:, u, t], K.ident[:])
                    mm.then_inc(filled, 1)
                    pe.wait_ge(s["read"].sem, s["read"].after(b, 1))
                    bank = bank_for(b, u, 1)
                    for t in range(T):
                        mm = nc.tensor.matmul(bank[:, t * 2 * D:(t + 1) * 2 * D], cnT[:, u, t * P:(t + 1) * P], W["x3_wkv"][:], start=True, stop=True)
                    mm.then_inc(filled, 1)
                    pe.wait_ge(s["z"].sem, s["z"].after(b))
                    bank = bank_for(b, u, 2)
                    for t in range(T):
                        mm = nc.tensor.transpose(bank[:, t * P:(t + 1) * P], z[:, u, t], K.ident[:])
                    mm.then_inc(filled, 1)
                    pe.wait_ge(s["read"].sem, s["read"].after(b, 3))
                    for t in range(T):
                        bank = bank_for(b, u, 3 + t)
                        nc.tensor.matmul(bank[:, 0:3 * D], zT[:, u, t * P:(t + 1) * P], W["x3_wql"][:], start=True, stop=True).then_inc(filled, 1)
                    pe.wait_ge(s["k_rows"].sem, s["k_rows"].after(b))
                    bank = bank_for(b, u, 5)
                    for kt in range(KT3):
                        mm = nc.tensor.transpose(bank[:, kt * P:(kt + 1) * P], kn[:, kt], K.ident[:])
                    mm.then_inc(filled, 1)
                    pe.wait_ge(s["q_rows"].sem, s["q_rows"].after(b))
                    bank = bank_for(b, u, 6)
                    for hd in range(H3):
                        for t in range(T):
                            mm = nc.tensor.transpose(bank[:, hd * S + t * P:hd * S + (t + 1) * P], qn[:, t, hd], K.ident[:])
                    mm.then_inc(filled, 1)

                def scores(b, u, i):
                    n, t = i // 2, i % 2
                    if i == 0:
                        pe.wait_ge(s["read"].sem, s["read"].after(b))
                    if i >= 2:
                        pe.wait_ge(s["smax"].sem, s["smax"].after(b, i - 1))
                    bank = K.PS[:, SMAX0 + i % 2, :]
                    nc.tensor.matmul(bank[:, 0:S], K.identb[:], K.hide_rows[:, bass.ds(b * S, S)], start=True, stop=True)
                    nc.tensor.matmul(bank, qT[:, u, n, t * P:(t + 1) * P], kT[:, u, :], start=False, stop=True, skip_group_check=True) \
                        .then_inc(s["smax_ps"].sem, 1)

                def turn_max(b, u):
                    pe.wait_ge(s["m"].sem, s["m"].after(b))
                    for t in range(T):
                        mm = nc.tensor.transpose(K.PS[:, SMAX0, :].bitcast(BF16)[:, t * P:(t + 1) * P], mtok[:, t], K.identb[:])
                    mm.then_inc(s["mT_ps"].sem, 1)

                def scores_T(b, u, i):
                    n, half = i // 2, i % 2
                    if i == 0:
                        pe.wait_ge(s["mT"].sem, s["mT"].after(b))
                    for k in range(2):
                        kt = 2 * half + k
                        o_ = K.PS[:, ST0 + i % 2, k * S:(k + 1) * S]
                        nc.tensor.matmul(o_, kT[:, u, kt * P:(kt + 1) * P], qT[:, u, n, :], start=True, stop=False)
                        mm = nc.tensor.matmul(o_, K.pick_max[:, n, :], mT[:, u], start=False, stop=True)
                    mm.then_inc(s["st_ps"].sem, 1)

                def mix(b, u, i):
                    n, half = i // 2, i % 2
                    if i == 0:
                        pe.wait_ge(s["out_banks"].sem, s["out_banks"].before(b))
                    pe.wait_ge(s["p"].sem, s["p"].after(b, i + 1))
                    for t in range(T):
                        for k in range(2):
                            mm = nc.tensor.matmul(K.PS[:, OUT0 + t, n * V3:(n + 1) * V3], p[:, i % 2, k, t * P:(t + 1) * P], ve[:, u, 2 * half + k, n, :],
                                                  start=half == 0 and k == 0, stop=half == 1 and k == 1)
                    if i == U3 - 1:
                        mm.then_inc(s["mix"].sem, 1)

                def first(b, u):
                    for i in range(U3):
                        scores(b, u, i)
                    turn_max(b, u)

                def fused(b, u, more):
                    for i in range(U3):
                        scores_T(b, u, i)
                        if more:
                            scores(b + 1, 1 - u, i)
                        if i >= 1:
                            mix(b, u, i - 1)
                    mix(b, u, U3 - 1)
                    if more:
                        turn_max(b + 1, 1 - u)

                def finish(b, u):
                    pe.wait_ge(s["o"].sem, s["o"].after(b))
                    for t in range(T):
                        mm = nc.tensor.transpose(K.PS[:, OUT0, t * P:(t + 1) * P], o[:, u, t].rearrange("p h e -> p (h e)"), K.ident[:])
                    mm.then_inc(s["oT_ps"].sem, 1)
                    pe.wait_ge(s["oT"].sem, s["oT"].after(b))
                    for t in range(T):
                        mm = nc.tensor.matmul(K.PS[:, OUT0 + 1, t * D:(t + 1) * D], oT[:, t * P:(t + 1) * P], W["x3_wo"][:], start=True, stop=True)
                    mm.then_inc(s["wo_ps"].sem, 1)

                head_pipeline(pe, prep, fused, first, finish)



NE3, HE3, K3 = 8, 256, 2
CE3 = HE3 // P


def top2_moe_layer(K, W, loaded):
    nc = K.nc
    s = ln_signals(K)
    s["pool_step"] = K.rising("pool_step", 1)
    s["prep_step"] = K.rising("vector_prep_step", LN_STEPS + 3 + T + 3 + 6 + 3)
    s["main_step"] = K.rising("vector_finish_step", NE3 * T)
    per = dict(logits=1, minus_max=1, e=1, weights=1, gu_ps=NE3, g=NE3, h=NE3, down_ps=NE3)
    for n, k in per.items():
        s[n] = K.rising("signal_" + n, k)
    tg = K.gates[:, 7:8]

    with ExitStack() as ctx:
        def sb(name, shape, dt=F32):
            return ctx.enter_context(nc.sbuf_tensor("f3_" + name, shape, dt))

        nm, e_, tot = sb("minus_max", [P, 2, T]), sb("exps", [P, 2, T, NE3]), sb("sums", [P, T])
        sc, top = sb("scores", [P, T, NE3]), sb("top", [P, T, 8])
        gt, eq, ca, cb, ngt = (sb(n, [P, T, NE3]) for n in ("greater", "equal", "count_a", "count_b", "n_greater_pad"))
        wt = sb("weights", [P, 2, T, NE3])
        g, hT = sb("gate", [P, 2, 2 * S]), sb("hiddenT", [P, 2, CE3, S])

        with nc.Block() as block:

            @block.vector
            def _(dve):
                chain, ending = Chain(s["prep_step"]), Chain(s["main_step"])

                def prep(b, u):
                    chain.start(b)
                    dve_layernorm(K, dve, chain, s, b, u)
                    dve.wait_ge(s["logits"].sem, s["logits"].after(b))
                    lg = K.PS[:, MISC + u, S:S + T * NE3].rearrange("p (t e) -> p t e", t=T)
                    nc.vector.tensor_reduce(nm[:, u], lg, AX_X, ALU.max, negate=True).then_inc(s["minus_max"].sem, 1)
                    dve.wait_ge(s["e"].sem, s["e"].after(b))
                    nc.vector.tensor_reduce(tot[:], e_[:, u], AX_X, ALU.add).then_inc(chain.sem, 1)
                    dve.wait_ge(chain.sem, chain.next())
                    nc.vector.reciprocal(tot[:], tot[:]).then_inc(chain.sem, 1)
                    dve.wait_ge(chain.sem, chain.next())
                    last = nc.vector.tensor_tensor(sc[:], e_[:, u], tot[:].unsqueeze(2).broadcast_to([P, T, NE3]), ALU.mult)
                    last.then_inc(chain.sem, 1)
                    dve.wait_ge(chain.sem, chain.next())
                    settled(dve, K)
                    for t in range(T):
                        nc.vector.max(top[:, t], sc[:, t]).then_inc(chain.sem, 1)
                        chain.next()
                    dve.wait_ge(chain.sem, chain.reached())
                    second = top[:, :, 1:2].broadcast_to([P, T, NE3])
                    nc.vector.tensor_tensor(gt[:], sc[:], second, ALU.is_gt).then_inc(chain.sem, 1)
                    chain.next()
                    nc.vector.tensor_tensor(eq[:], sc[:], second, ALU.is_equal).then_inc(chain.sem, 1)
                    dve.wait_ge(chain.sem, chain.next())
                    nc.vector.tensor_reduce(ngt[:, :, 0], gt[:], AX_X, ALU.add).then_inc(chain.sem, 1)
                    dve.wait_ge(chain.sem, chain.next())
                    src = eq
                    for sh, dst in ((1, ca), (2, cb), (4, ca)):
                        nc.vector.tensor_copy(dst[:, :, 0:sh], src[:, :, 0:sh]).then_inc(chain.sem, 1)
                        chain.next()
                        nc.vector.tensor_tensor(dst[:, :, sh:], src[:, :, sh:], src[:, :, 0:NE3 - sh], ALU.add).then_inc(chain.sem, 1)
                        dve.wait_ge(chain.sem, chain.next())
                        src = dst
                    nc.vector.tensor_tensor(ca[:], ca[:], ngt[:, :, 0:1].broadcast_to([P, T, NE3]), ALU.add).then_inc(chain.sem, 1)
                    dve.wait_ge(chain.sem, chain.next())
                    nc.vector.scalar_tensor_tensor(eq[:], ca[:], float(K3), eq[:], ALU.is_le, ALU.mult).then_inc(chain.sem, 1)
                    dve.wait_ge(chain.sem, chain.next())
                    nc.vector.tensor_tensor(gt[:], gt[:], eq[:], ALU.add).then_inc(chain.sem, 1)
                    dve.wait_ge(chain.sem, chain.next())
                    nc.vector.scalar_tensor_tensor(wt[:, u], gt[:], tg, sc[:], ALU.mult, ALU.mult).then_inc(s["weights"].sem, 1)
                    dve.wait_ge(s["weights"].sem, s["weights"].after(b))

                def main(b, u):
                    ending.start(b)

                    def add_expert(e):
                        dve.wait_ge(s["down_ps"].sem, s["down_ps"].after(b, e + 1))
                        if e > 0:
                            dve.wait_ge(ending.sem, ending.reached())
                        for t in range(T):
                            x = K.X[:, bass.ds(b * S + t * P, P)]
                            nc.vector.scalar_tensor_tensor(x, K.PS[:, OUT0 + e % 2, t * D:(t + 1) * D], wt[:, u, t, e:e + 1], x, ALU.mult, ALU.add).then_inc(ending.sem, 1)
                            ending.next()

                    for e in range(NE3):
                        dve.wait_ge(s["g"].sem, s["g"].after(b, e + 1))
                        nc.vector.tensor_tensor(hT[:, e % 2].rearrange("p c n -> p (c n)"), K.PS[:, 2 * (e % 2) + 1, :], g[:, e % 2], ALU.mult) \
                            .then_inc(s["h"].sem, 1)
                        if e >= 1:
                            add_expert(e - 1)
                    add_expert(NE3 - 1)
                    dve.wait_ge(ending.sem, ending.reached())

                software_pipeline(dve, prep, main)

            @block.gpsimd
            def _(pool):
                software_pipeline(pool, lambda b, u: pool_rstd(K, pool, s, b, u), lambda b, u: None)

            @block.scalar
            def _(act):
                def prep(b, u):
                    act_xn_transposed(K, act, s, b, u, MISC + u)
                    act.wait_ge(s["minus_max"].sem, s["minus_max"].after(b))
                    for t in range(T):
                        ins = nc.scalar.activation(e_[:, u, t], K.PS[:, MISC + u, S + t * NE3:S + (t + 1) * NE3], ACT.Exp, bias=nm[:, u, t:t + 1])
                    ins.then_inc(s["e"].sem, 1)

                def main(b, u):
                    for e in range(NE3):
                        act.wait_ge(s["gu_ps"].sem, s["gu_ps"].after(b, e + 1))
                        nc.scalar.activation(g[:, e % 2], K.PS[:, 2 * (e % 2), :], ACT.Silu).then_inc(s["g"].sem, 1)

                software_pipeline(act, prep, main)

            @block.tensor
            def _(pe):
                for value, sem in loaded:
                    pe.wait_ge(sem, value)

                def prep(b, u):
                    pe_xn_transposed(K, pe, s, b, u, MISC + u)
                    pe.wait_ge(s["xnT"].sem, s["xnT"].after(b))
                    for t in range(T):
                        mm = nc.tensor.matmul(K.PS[:, MISC + u, S + t * NE3:S + (t + 1) * NE3], K.norm["xnT"][:, u, t * P:(t + 1) * P], W["f3_gate_w"][:],
                                              start=True, stop=True)
                    mm.then_inc(s["logits"].sem, 1)

                def main(b, u):
                    def up(e):
                        for k, name in enumerate(("f3_w1", "f3_w3")):
                            for c in range(CE3):
                                mm = nc.tensor.matmul(K.PS[:, 2 * (e % 2) + k, c * S:(c + 1) * S], W[name][:, e * HE3 + c * P:e * HE3 + (c + 1) * P],
                                                      K.norm["xnT"][:, u, :], start=True, stop=True)
                        mm.then_inc(s["gu_ps"].sem, 1)

                    def down(e):
                        pe.wait_ge(s["h"].sem, s["h"].after(b, e + 1))
                        for t in range(T):
                            for c in range(CE3):
                                mm = nc.tensor.matmul(K.PS[:, OUT0 + e % 2, t * D:(t + 1) * D], hT[:, e % 2, c, t * P:(t + 1) * P],
                                                      W["f3_w2"][:, (e * CE3 + c) * D:(e * CE3 + c + 1) * D], start=c == 0, stop=c == CE3 - 1)
                        mm.then_inc(s["down_ps"].sem, 1)

                    for e in range(NE3):
                        up(e)
                        if e >= 1:
                            down(e - 1)
                    down(NE3 - 1)

                software_pipeline(pe, prep, main)



def build(nc, a, out):
    with ExitStack() as ctx:
        K = Core(nc, ctx, a)
        K.X = K.sb("x_resident", [P, B * S])
        K.ident = K.sb("identity", [P, P])
        K.identb = K.sb("identity_bf16", [P, P], BF16)
        K.eps5 = K.sb("eps_1e5", [P, 2 * T])
        K.neghalf = K.sb("minus_half", [P, 4 * T])
        K.ctxT = K.sb("contextT", [C, B * S])
        K.ctx_tile = K.sb("context_tile", [C, 2, S])
        K.ones = K.sb("ones", [P, P])
        K.mask_u8 = K.sb("mask_queries_u8", [P, B * T], U8)
        K.mask_q = K.sb("mask_queries", [P, B * T])
        K.g_all = K.sb("gate_values", [P, 8])
        K.gates = K.sb("gate_tanh", [P, 8])
        K.mask_k1, K.mask_k1c = K.sb("mask_keys_u8", [P, B * S], U8), K.sb("mask_key_columns_u8", [P, B * T], U8)
        K.hide_rows, K.hide_cols = K.sb("hide_key_rows", [P, B * S], BF16), K.sb("hide_key_columns", [P, B * T])
        K.pick_max = K.sb("pick_max", [P, H1, P], BF16)
        K.hide_q, K.hide_kT = K.sb("hide_later_keys", [P, T, S], BF16), K.sb("hide_later_keysT", [P, P], BF16)
        K.ctx_rows = K.sb("context_rows", [P, B * T * C])
        K.mask_k3, K.mask_k3c = K.sb("mask_ctx_u8", [P, B * S], U8), K.sb("mask_ctx_columns_u8", [P, B * T], U8)
        K.PS = ctx.enter_context(nc.psum_tensor("banks", [P, 8, 512], F32))
        K.norm = norm_tiles(K)
        W = {}
        for name, shape in WEIGHTS.items():
            if name[:2] not in LATE:
                W[name] = K.sb("w_" + name, list(shape))
        heads_memory = ctx.enter_context(ExitStack())
        K.heads = head_tiles(K, heads_memory, "early_heads")
        first_loaded = K.sem("first_inputs_loaded")
        for name in CREDITS:
            K.sem(name)
            K.totals[name] = CREDITS[name]
        groups = {}
        setup_memory = ExitStack()
        pick_f = setup_memory.enter_context(nc.sbuf_tensor("pick_max_f32", [P, H1, P], F32))
        hide_f = setup_memory.enter_context(nc.sbuf_tensor("hide_later_f32", [P, T * S + P], F32))

        def load(sp, wanted):
            for name in WEIGHTS:
                g = name[:2]
                if wanted(g):
                    sp.dma_start(W[name][:], a[name]).then_inc(K.sem("weights_loaded_" + g), 16)
                    groups[g] = groups.get(g, 0) + 16

        def place_late():
            for name, shape in WEIGHTS.items():
                if name[:2] in LATE:
                    W[name] = K.sb("w_" + name, list(shape))

        with nc.Block() as block:

            @block.sync
            def _(sp):
                sp.dma_start(K.X[:].rearrange("p (n d) -> p n d", d=D), a["x"].rearrange("(n p) d -> p n d", p=P)) \
                    .then_inc(first_loaded, 16)
                sp.dma_start(K.ctxT[:], a["ctxT"]).then_inc(first_loaded, 16)
                sp.dma_start(K.ident[:], a["identity"]).then_inc(first_loaded, 16)
                sp.dma_start(K.mask_u8[:], a["mask_queries"]).then_inc(first_loaded, 16)
                sp.dma_start(K.g_all[:], a["gates"]).then_inc(first_loaded, 16)
                sp.dma_start(K.mask_k1[:], a["mask_keys"]).then_inc(first_loaded, 16)
                sp.dma_start(K.mask_k1c[:], a["mask_key_columns"]).then_inc(first_loaded, 16)
                sp.dma_start(pick_f[:].rearrange("p h n -> p (h n)"), a["pick_max"]).then_inc(first_loaded, 16)
                sp.dma_start(hide_f[:], a["hide_later"]).then_inc(first_loaded, 16)
                sp.dma_start(K.ctx_rows[:].rearrange("p (n d) -> p n d", d=C), a["ctx"].rearrange("(n p) d -> p n d", p=P)).then_inc(first_loaded, 16)
                sp.dma_start(K.mask_k3[:], a["mask_ctx"]).then_inc(first_loaded, 16)
                sp.dma_start(K.mask_k3c[:], a["mask_ctx_columns"]).then_inc(first_loaded, 16)
                load(sp, lambda g: g not in LATE)

            @block.gpsimd
            def _(pool):
                nc.gpsimd.memset(K.eps5[:], 1e-5)
                nc.gpsimd.memset(K.neghalf[:], -0.5)
                pool_clear_heads(K, pool, "early_heads")
                for name, n in CREDITS.items():
                    pool.sem_inc(K.sem(name), n)

            @block.vector
            def _(dve):
                nc.vector.memset(K.ones[:], 1.0)
                dve_clear_heads(K, dve, "early_heads")
                dve.wait_ge(first_loaded, 16 * 12)
                nc.vector.tensor_copy(K.identb[:], K.ident[:])
                nc.vector.tensor_copy(K.pick_max[:], pick_f[:])
                nc.vector.tensor_copy(K.hide_q[:].rearrange("p t n -> p (t n)"), hide_f[:, 0:T * S])
                nc.vector.tensor_copy(K.hide_kT[:], hide_f[:, T * S:T * S + P])
                nc.vector.tensor_copy(K.mask_q[:], K.mask_u8[:])

            @block.scalar
            def _(act):
                act.wait_ge(first_loaded, 16 * 12)
                nc.scalar.activation(K.gates[:], K.g_all[:], ACT.Tanh)

        setup_memory.close()

        def loaded(g):
            return [(groups[g], K.sem("weights_loaded_" + g))]

        def heads_again():
            K.heads = head_tiles(K, heads_memory, "late_heads")
            K.Y = heads_memory.enter_context(nc.sbuf_tensor("y1_resident", [P, B * S], F32))
            with nc.Block() as block:

                @block.gpsimd
                def _(pool):
                    pool_clear_heads(K, pool, "late_heads")

                @block.vector
                def _(dve):
                    dve_clear_heads(K, dve, "late_heads")

        cross_attention_layer(K, "x0", 0, W["x0_wq"], W["x0_wkv"], mask=K.mask_q, loaded=loaded("x0"))
        quantised_ffn_layer(K, W, loaded("f0"))
        heads_memory.close()
        normed_attention_layer(K, W, loaded("x1"))
        heads_again()
        latent_moe_layer(K, W, loaded("f1"))
        cross_attention_layer(K, "x2", 2, W["x2_wq"], W["x2_wkv"], bias=dict(q=W["x2_bq"], k=W["x2_bk"], v=W["x2_bv"], o=W["x2_bo"]), wo=W["x2_wo"], loaded=loaded("x2"))
        heads_memory.close()
        place_late()
        routed_ffn_layer(K, W, loaded("f2"), lambda sp: load(sp, lambda g: g in LATE))
        perceiver_attention_layer(K, W, loaded("x3"))
        top2_moe_layer(K, W, loaded("f3"))

        stored = K.sem("result_stored")
        with nc.Block() as block:

            @block.sync
            def _(sp):
                sp.dma_start(out.rearrange("(n p) d -> p n d", p=P), K.X[:].rearrange("p (n d) -> p n d", d=D)) \
                    .then_inc(stored, 16)
                sp.wait_ge(stored, 16)


LATE = ("x3", "f3")
CREDITS = {"heads_out_banks": 1, "heads_qmT": 1, "signal_out_banks": 1, "signal_read": 2}
WEIGHTS = {
    "x0_wq": (P, D), "x0_wkv": (C, 2 * D),
    "f0_wg": (P, F0), "f0_wu": (P, F0), "f0_wd": (P, F0),
    "x1_wq": (P, I1), "x1_wk": (C, I1), "x1_wv": (C, I1), "x1_wo": (P, C1 * D), "x1_gnorm": (P, 1), "x1_gout": (P, D),
    "x1_nk": (P, DH1), "x1_nv": (P, DH1), "x1_qs": (P, DH1), "x1_ks": (P, DH1), "x1_qs_col": (P, 1), "x1_ks_col": (P, 1),
    "x2_wq": (P, D), "x2_wkv": (C, 2 * D), "x2_bq": (P, D), "x2_bk": (P, D), "x2_bv": (P, D), "x2_wo": (P, D), "x2_bo": (P, D),
    "f2_gate_w": (NE2, D), "f2_wg": (P, F2 + HE2), "f2_wu": (P, F2 + HE2), "f2_wd": (P, F2C * D), "f2_sd": (HE2, D),
    "x3_wql": (P, 3 * D), "x3_wkv": (C, 2 * D), "x3_wo": (P, D), "x3_bo": (P, D), "x3_qg": (P, 1), "x3_kg": (P, 1),
    "x3_lx_g": (C, 1), "x3_lx_b": (C, 1), "x3_ll_g": (P, 1), "x3_ll_b": (P, 1),
    "f3_gate_w": (P, NE3), "f3_w1": (P, NE3 * HE3), "f3_w3": (P, NE3 * HE3), "f3_w2": (P, NE3 * CE3 * D),
    "f1_norm1": (P, 1), "f1_norm2": (P, 1), "f1_ln_g": (P, 1), "f1_ln_b": (P, 1), "f1_wqd": (P, D + LAT), "f1_wukv": (LAT, 2 * D),
    "f1_wo": (P, D), "f1_rope": (P, 2 * T * DH), "f1_gate_w": (P, NE1), "f1_gate_b": (P, NE1), "f1_w1": (P, NE1 * HE1),
    "f1_b1": (P, NE1 * CE1), "f1_w2": (P, NE1 * CE1 * D), "f1_b2": (P, NE1 * D),
}


def lay_out(i):
    import numpy as np

    def T_(m):
        return np.ascontiguousarray(np.asarray(m).T)

    def rows(v):
        return np.ascontiguousarray(np.broadcast_to(np.asarray(v).reshape(1, -1), (P, np.asarray(v).size)))

    a = {}
    a["x"] = np.ascontiguousarray(np.asarray(i["x"]).reshape(B * S, D))
    a["ctxT"] = T_(np.asarray(i["ctx_768"]).reshape(B * S, C))
    a["identity"] = np.eye(P, dtype=np.float32)
    a["mask_queries"] = np.ascontiguousarray(np.asarray(i["mask_BxS_bk0"]).reshape(B * T, P).T)
    a["gates"] = rows(np.concatenate([np.asarray(i["g_xattn"]), np.asarray(i["g_ffn"])]))
    a["x0_wq"] = T_(i["L0_xattn_Wq"])
    a["x0_wkv"] = T_(i["L0_xattn_Wkv"])
    def chunked(m):
        m = np.asarray(m)
        return np.ascontiguousarray(m.reshape(-1, P, m.shape[-1]).transpose(1, 0, 2).reshape(P, -1))

    a["f0_wg"] = T_(i["L0_ffn_w_gate"])
    a["f0_wu"] = T_(i["L0_ffn_w_up"])
    a["f0_wd"] = chunked(T_(i["L0_ffn_w_down"]))
    def col(v, n=1):
        return np.ascontiguousarray(np.tile(np.asarray(v), n).reshape(-1, 1))

    mask1 = np.asarray(i["mask_BxS2_bf1"])
    a["mask_keys"] = rows(mask1)
    a["mask_key_columns"] = np.ascontiguousarray(mask1.reshape(B * T, P).T)
    pick = np.zeros((P, H1, P), np.float32)
    for n in range(H1):
        pick[3 * n:3 * n + 3, n] = 1.0
    a["pick_max"] = pick.reshape(P, -1)
    wkv = np.asarray(i["L1_xattn_Wkv"])
    a["x1_wq"] = np.ascontiguousarray(i["L1_xattn_Wq"])
    a["x1_wk"] = np.ascontiguousarray(wkv[:, :I1])
    a["x1_wv"] = np.ascontiguousarray(wkv[:, I1:])
    a["x1_wo"] = chunked(i["L1_xattn_Wo"])
    a["x1_gnorm"] = col(i["L1_xattn_g_norm"])
    a["x1_gout"] = rows(i["L1_xattn_g_out"])
    a["x1_nk"], a["x1_nv"] = rows(np.asarray(i["L1_xattn_null_kv"])[0]), rows(np.asarray(i["L1_xattn_null_kv"])[1])
    a["x1_qs"], a["x1_ks"] = rows(i["L1_xattn_q_scale"]), rows(i["L1_xattn_k_scale"])
    a["x1_qs_col"], a["x1_ks_col"] = col(i["L1_xattn_q_scale"], 2), col(i["L1_xattn_k_scale"], 2)
    def padded_col(v):
        v = np.asarray(v)
        return np.ascontiguousarray(np.concatenate([v, np.zeros(P - v.size, v.dtype)]).reshape(-1, 1))

    def cat(*ms):
        return np.ascontiguousarray(np.concatenate(ms, axis=1))

    a["f1_norm1"], a["f1_norm2"] = col(i["L1_ffn_norm1_w"]), col(i["L1_ffn_norm2_w"])
    a["f1_ln_g"], a["f1_ln_b"] = padded_col(i["L1_ffn_ln_g"]), padded_col(i["L1_ffn_ln_b"])
    a["f1_wqd"] = cat(T_(i["L1_ffn_Wq"]), T_(i["L1_ffn_Wdkv"]))
    a["f1_wukv"] = cat(T_(i["L1_ffn_Wuk"]), T_(i["L1_ffn_Wuv"]))
    a["f1_wo"] = T_(i["L1_ffn_Wo"])
    half = DH // 2
    freq = (np.float32(1.0) / np.float32(10000.0) ** (np.arange(half, dtype=np.float32) / np.float32(half))).astype(np.float32)
    ang = np.arange(S, dtype=np.float32)[:, None] * freq[None, :]
    cos, sin = np.cos(ang).astype(np.float32), np.sin(ang).astype(np.float32)
    tables = np.stack([np.concatenate([cos, cos], 1), np.concatenate([-sin, sin], 1)])
    a["f1_rope"] = np.ascontiguousarray(tables.reshape(2, T, P, DH).transpose(2, 0, 1, 3).reshape(P, -1))
    later = np.arange(S)[None, :] > np.arange(S)[:, None]
    hide = np.where(later, np.float32(HIDE), np.float32(0.0)).astype(np.float32)
    a["hide_later"] = cat(hide.reshape(T, P, S).transpose(1, 0, 2).reshape(P, -1), hide[:P, :P].T)
    a["f1_gate_w"], a["f1_gate_b"] = T_(i["L1_ffn_gate_w"]), rows(i["L1_ffn_gate_b"])
    a["f1_w1"] = np.ascontiguousarray(np.asarray(i["L1_ffn_W1"]).reshape(NE1 * HE1, D).T)
    a["f1_b1"] = np.ascontiguousarray(np.asarray(i["L1_ffn_b1"]).reshape(NE1 * CE1, P).T)
    a["f1_w2"] = np.ascontiguousarray(np.asarray(i["L1_ffn_W2"]).reshape(NE1, D, CE1, P).transpose(3, 0, 2, 1).reshape(P, -1))
    a["f1_b2"] = rows(i["L1_ffn_b2"])
    wkv2, bkv2 = np.asarray(i["L2_xattn_Wkv"]).reshape(H, 2, DH, C), np.asarray(i["L2_xattn_bkv"]).reshape(H, 2, DH)
    a["x2_wq"], a["x2_wo"] = T_(i["L2_xattn_Wq"]), T_(i["L2_xattn_Wo"])
    a["x2_wkv"] = T_(wkv2.transpose(1, 0, 2, 3).reshape(2 * D, C))
    a["x2_bq"], a["x2_bo"] = rows(i["L2_xattn_bq"]), rows(i["L2_xattn_bo"])
    a["x2_bk"], a["x2_bv"] = rows(bkv2[:, 0]), rows(bkv2[:, 1])
    a["f2_gate_w"] = np.ascontiguousarray(i["L2_ffn_gate_w"])

    def side_by_side(m):
        return np.asarray(m).transpose(1, 0, 2).reshape(D, -1)

    a["f2_wg"] = cat(side_by_side(i["L2_ffn_w_gate"]), np.asarray(i["L2_ffn_sw_gate"]))
    a["f2_wu"] = cat(side_by_side(i["L2_ffn_w_up"]), np.asarray(i["L2_ffn_sw_up"]))
    a["f2_wd"] = chunked(np.asarray(i["L2_ffn_w_down"]).reshape(F2, D))
    a["f2_sd"] = np.ascontiguousarray(i["L2_ffn_sw_down"])
    a["ctx"] = np.ascontiguousarray(np.asarray(i["ctx_768"]).reshape(B * S, C))
    mask3 = np.asarray(i["mask_BxS2_bk0"])
    a["mask_ctx"] = rows(mask3)
    a["mask_ctx_columns"] = np.ascontiguousarray(mask3.reshape(B * T, P).T)
    a["x3_wql"] = cat(T_(i["L3_xattn_Wq"]), T_(i["L3_xattn_Wlkv"]))
    a["x3_wkv"], a["x3_wo"], a["x3_bo"] = T_(i["L3_xattn_Wkv"]), T_(i["L3_xattn_Wo"]), rows(i["L3_xattn_bo"])
    a["x3_qg"], a["x3_kg"] = col(i["L3_xattn_qn_g"], 2), col(i["L3_xattn_kn_g"], 2)
    a["x3_lx_g"], a["x3_lx_b"] = col(i["L3_xattn_ln_x_g"]), col(i["L3_xattn_ln_x_b"])
    a["x3_ll_g"], a["x3_ll_b"] = col(i["L3_xattn_ln_l_g"]), col(i["L3_xattn_ln_l_b"])
    a["f3_gate_w"] = T_(i["L3_ffn_gate_w"])
    a["f3_w1"], a["f3_w3"] = np.ascontiguousarray(side_by_side(i["L3_ffn_w1"])), np.ascontiguousarray(side_by_side(i["L3_ffn_w3"]))
    a["f3_w2"] = chunked(np.asarray(i["L3_ffn_w2"]).reshape(NE3 * HE3, D))
    return a


def kernel(**inputs):
    import numpy as np
    import concourse.bacc as bacc
    from concourse.bass_utils import run_bass_kernel_spmd

    nc = bacc.Bacc("TRN2", target_bir_lowering=False, num_devices=1)
    arrays = {f"in_{n}": v for n, v in lay_out(inputs).items()}
    a = {n[3:]: nc.dram_tensor(n, v.shape, mybir.dt.from_np(v.dtype), kind="ExternalInput").ap() for n, v in arrays.items()}
    out = nc.dram_tensor("out", (B * S, D), F32, kind="ExternalOutput").ap()
    build(nc, a, out)
    r = run_bass_kernel_spmd(nc, [arrays], core_ids=[0])
    return np.asarray(r.results[0]["out"]).reshape(B, S, D)
```

```python
from contextlib import ExitStack

import concourse.bass as bass
from concourse import mybir

F32 = mybir.dt.float32
BF16 = mybir.dt.bfloat16
U8 = mybir.dt.uint8
ALU = mybir.AluOpType
ACT = mybir.ActivationFunctionType
AX_X = mybir.AxisListType.X

P = 128
B, S, D = 8, 256, 128
C = 96
T = S // P
ROUND = 12582912.0
HIDE = -1.0e30

SMAX0, ST0, OUT0, MISC = 0, 2, 4, 6


class Signal:

    def __init__(self, sem, base, per):
        self.sem, self.base, self.per = sem, base, per

    def after(self, b, k=None):
        return b * self.per + (self.base + (self.per if k is None else k))

    def before(self, b):
        return b * self.per + self.base


class Chain:

    def __init__(self, rising):
        self.sem, self.rising = rising.sem, rising
        self.b, self.k = 0, 0

    def start(self, b):
        assert self.k in (0, self.rising.per), (self.sem, self.k, self.rising.per)
        self.b, self.k = b, 0

    def next(self):
        self.k += 1
        assert self.k <= self.rising.per, "more steps than the chain's semaphore has in a batch"
        return self.reached()

    def reached(self):
        return self.rising.after(self.b, self.k)


class Core:

    def __init__(self, nc, ctx, arrays):
        self.nc, self.ctx, self.dram = nc, ctx, arrays
        self.sems, self.totals = {}, {}

    def sem(self, name):
        if name not in self.sems:
            self.sems[name] = self.ctx.enter_context(self.nc.semaphore(name))
            self.totals[name] = 0
        return self.sems[name]

    def rising(self, name, per):
        sem = self.sem(name)
        s = Signal(sem, self.totals[name], per)
        self.totals[name] += B * per
        return s

    def sb(self, name, shape, dt=F32):
        return self.ctx.enter_context(self.nc.sbuf_tensor(name, shape, dt))


def settled(eng, K):
    eng.sem_inc(K.sem("passed"), 1)


def software_pipeline(eng, prep, main):
    all_stages(prep(0, 0))
    with eng.Fori(0, B // 2 - 1) as i:
        main(2 * i, 0, prep(2 * i + 1, 1))
        main(2 * i + 1, 1, prep(2 * i + 2, 0))
    main(B - 2, 0, prep(B - 1, 1))
    main(B - 1, 1, None)


def all_stages(stages):
    if stages:
        for _ in stages:
            pass


def next_stage(stages):
    if stages:
        next(stages)


def cols(tensor, b, n=S):
    return tensor[:, bass.ds(b * n, n)]



def norm_tiles(K):
    st = K.sb("ln_stats", [P, 2, T, 6])
    mv = K.sb("ln_mean_var", [P, 2, T, 2])
    ve = K.sb("ln_var_eps", [P, 2, T])
    rs = K.sb("ln_rstd", [P, 2, T])
    xn = K.sb("xn", [P, 2, T, D])
    xnT = K.sb("xnT", [P, 2, T * P])
    return dict(st=st, mv=mv, ve=ve, rs=rs, xn=xn, xnT=xnT)


def ln_signals(K, turned=True):
    names = dict(stats="ln_stats_ready", rstd="ln_rstd_ready", xn="xn_ready")
    if turned:
        names.update(xnT_ps="xnT_in_psum", xnT="xnT_ready")
    return {k: K.rising(name, 1) for k, name in names.items()}


LN_STEPS = 2 * T


def dve_layernorm(K, dve, chain, s, b, u, dst=None):
    dve_ln_stats(K, dve, chain, s, b, u)
    dve_ln_rows(K, dve, chain, s, b, u, dst)


def dve_ln_stats(K, dve, chain, s, b, u):
    nc, n = K.nc, K.norm
    for t in range(T):
        settled(dve, K)
        nc.vector.bn_stats(n["st"][:, u, t, :], K.X[:, bass.ds(b * S + t * P, P)]).then_inc(chain.sem, 1)
        chain.next()
    dve.wait_ge(chain.sem, chain.reached())
    settled(dve, K)
    nc.vector.bn_aggr(n["mv"][:, u, 0, :], n["st"][:, u, 0, :]).then_inc(chain.sem, 1)
    chain.next()
    nc.vector.bn_aggr(n["mv"][:, u, 1, :], n["st"][:, u, 1, :]).then_inc(s["stats"].sem, 1)


def dve_ln_rows(K, dve, chain, s, b, u, dst=None):
    nc, n = K.nc, K.norm
    dst = n["xn"][:, u] if dst is None else dst
    dve.wait_ge(s["rstd"].sem, s["rstd"].after(b))
    nc.vector.tensor_scalar(dst[:, 0, :], K.X[:, bass.ds(b * S, P)], n["mv"][:, u, 0, 0:1],
                            n["rs"][:, u, 0:1], ALU.subtract, ALU.mult).then_inc(chain.sem, 1)
    chain.next()
    nc.vector.tensor_scalar(dst[:, 1, :], K.X[:, bass.ds(b * S + P, P)], n["mv"][:, u, 1, 0:1],
                            n["rs"][:, u, 1:2], ALU.subtract, ALU.mult).then_inc(s["xn"].sem, 1)


def pool_rstd(K, pool, s, b, u, mask=None):
    nc, n = K.nc, K.norm
    pool.wait_ge(s["stats"].sem, s["stats"].after(b))
    pt, ps = K.sem("pool_step"), s["pool_step"]
    nc.gpsimd.tensor_tensor(n["ve"][:, u, :], n["mv"][:, u, :, 1], K.eps5[:, 0:T], ALU.add).then_inc(pt, 1)
    pool.wait_ge(pt, ps.after(b, 1))
    if mask is None:
        nc.gpsimd.tensor_tensor(n["rs"][:, u, :], n["ve"][:, u, :], K.neghalf[:, 0:T], ALU.pow) \
            .then_inc(s["rstd"].sem, 1)
        return 1
    nc.gpsimd.tensor_tensor(n["ve"][:, u, :], n["ve"][:, u, :], K.neghalf[:, 0:T], ALU.pow).then_inc(pt, 1)
    pool.wait_ge(pt, ps.after(b, 2))
    nc.gpsimd.tensor_tensor(n["rs"][:, u, :], n["ve"][:, u, :], mask[:, bass.ds(b * T, T)], ALU.mult) \
        .then_inc(s["rstd"].sem, 1)
    return 2


def pe_xn_transposed(K, pe, s, b, u, bank):
    pe.wait_ge(s["xn"].sem, s["xn"].after(b))
    for t in range(T):
        mm = K.nc.tensor.transpose(K.PS[:, bank, t * P:(t + 1) * P], K.norm["xn"][:, u, t, :], K.ident[:])
    mm.then_inc(s["xnT_ps"].sem, 1)


def act_xn_transposed(K, act, s, b, u, bank, scale=1.0):
    act.wait_ge(s["xnT_ps"].sem, s["xnT_ps"].after(b))
    K.nc.scalar.activation(K.norm["xnT"][:, u, :], K.PS[:, bank, 0:S], ACT.Copy if isinstance(scale, float) else ACT.Identity, scale=scale) \
        .then_inc(s["xnT"].sem, 1)



H, DH, E = 16, 8, 32
G = 4
HG = H // G


def head_tiles(K, ctx, name):
    def sb(what, shape, dt=F32):
        return ctx.enter_context(K.nc.sbuf_tensor(name + "_" + what, shape, dt))

    h = {}
    h["qs"] = sb("q_scaled", [P, 2, T * D])
    h["ks"] = sb("k_rows", [P, 2, T * D])
    h["qe"] = sb("q_expanded", [P, 2, T * H, E], BF16)
    h["ke"] = sb("k_expanded", [P, 2, T * H, E], BF16)
    h["ve"] = sb("v_with_ones", [P, 2, T * H, E])
    h["qT"] = sb("qT", [P, 2, G, S], BF16)
    h["kT"] = sb("kT", [P, 2, G, S], BF16)
    h["nm"] = sb("minus_max", [P, 2, T, H])
    h["nr"] = sb("minus_max_rest", [P, T, H])
    h["p"] = sb("probs", [P, 2, 2 * S])
    h["oT"] = sb("outT", [P, G, S])
    h["rec"] = sb("inverse_sums", [P, T, H])
    h["o"] = sb("attention_out", [P, 2, T * D])
    return h


def dve_clear_heads(K, dve, name):
    nc, h, cleared = K.nc, K.heads, K.sem(name + "_zeroed_by_vector")
    nc.vector.memset(h["qe"][:], 0.0)
    nc.vector.memset(h["ke"][:], 0.0).then_inc(cleared, 1)
    dve.wait_ge(cleared, 1)
    nc.vector.memset(h["ke"][:, :, :, 24:27], 1.0)


def pool_clear_heads(K, pool, name):
    nc, h, cleared = K.nc, K.heads, K.sem(name + "_zeroed_by_gpsimd")
    nc.gpsimd.memset(h["ve"][:], 0.0).then_inc(cleared, 1)
    pool.wait_ge(cleared, 1)
    nc.gpsimd.memset(h["ve"][:, :, :, DH:DH + 1], 1.0)


def head_signals(K):
    names = dict(qs=1, ks=1, v=1, ke_high=1, qe_high=1, qe=1, ke=1, kT_ps=1, kT=1, qT_ps=1, qT=1, smax_ps=H, smax=H,
                 qm=1, qmT_ps=1, qmT=1, st_ps=H, p=H, oT_ps=2, ob=1, out_banks=1)
    return {k: K.rising("heads_" + k, n) for k, n in names.items()}


def parts_of(h, name, u):
    return h[name][:, u].rearrange("p h (c e) -> p h c e", e=DH)


def act_high_parts(K, act, s, b, u):
    h = K.heads
    for rows, dst, places in (("ks", "ke", slice(0, 3, 2)), ("qs", "qe", slice(0, 2))):
        act.wait_ge(s[rows].sem, s[rows].after(b))
        src = h[rows][:, u].rearrange("p (h e) -> p h e", e=DH).unsqueeze(2).broadcast_to([P, T * H, 2, DH])
        K.nc.scalar.activation(parts_of(h, dst, u)[:, :, places], src, ACT.Copy).then_inc(s[dst + "_high"].sem, 1)


def pool_low_parts(K, pool, s, b, u):
    h = K.heads
    for rows, dst, place in (("ks", "ke", 1), ("qs", "qe", 2)):
        pool.wait_ge(s[dst + "_high"].sem, s[dst + "_high"].after(b))
        parts = parts_of(h, dst, u)
        K.nc.gpsimd.tensor_tensor(parts[:, :, place], h[rows][:, u].rearrange("p (h e) -> p h e", e=DH), parts[:, :, 0], ALU.subtract) \
            .then_inc(s[dst].sem, 1)


def pe_turn_heads(K, pe, src, u, bank):
    out = K.PS[:, bank, :].bitcast(BF16)
    for t in range(T):
        for g in range(G):
            mm = K.nc.tensor.transpose(out[:, g * S + t * P:g * S + (t + 1) * P],
                                       src[:, u, t * H + g * HG:t * H + (g + 1) * HG, :].rearrange("p h e -> p (h e)"),
                                       K.identb[:])
    return mm


def pe_turn_k_and_q(K, pe, s, b, u):
    h = K.heads
    pe.wait_ge(s["ke"].sem, s["ke"].after(b))
    pe_turn_heads(K, pe, h["ke"], u, MISC).then_inc(s["kT_ps"].sem, 1)
    pe.wait_ge(s["qe"].sem, s["qe"].after(b))
    pe_turn_heads(K, pe, h["qe"], u, MISC + 1).then_inc(s["qT_ps"].sem, 1)


def act_copy_kT(K, act, s, b, u):
    act.wait_ge(s["kT_ps"].sem, s["kT_ps"].after(b))
    K.nc.scalar.activation(K.heads["kT"][:, u].rearrange("p g n -> p (g n)"), K.PS[:, MISC, :].bitcast(BF16), ACT.Copy) \
        .then_inc(s["kT"].sem, 1)


def dve_copy_qT(K, dve, s, b, u):
    dve.wait_ge(s["qT_ps"].sem, s["qT_ps"].after(b))
    K.nc.vector.tensor_copy(K.heads["qT"][:, u].rearrange("p g n -> p (g n)"), K.PS[:, MISC + 1, :].bitcast(BF16)) \
        .then_inc(s["qT"].sem, 1)


def pe_scores(K, pe, s, b, u, n, causal):
    nc, h = K.nc, K.heads
    g, j = n // HG, n % HG
    bank = SMAX0 + n % 2
    r = slice(E * j, E * (j + 1))
    if n == 0:
        pe.wait_ge(s["kT"].sem, s["kT"].after(b))
        pe.wait_ge(s["qT"].sem, s["qT"].after(b))
    if n >= 2:
        pe.wait_ge(s["smax"].sem, s["smax"].after(b, n - 1))
    for t in range(T):
        width = P * (t + 1) if causal else S
        o = K.PS[:, bank, t * S:t * S + width]
        if causal:
            nc.tensor.matmul(K.PS[:, bank, t * S:(t + 1) * S], K.identb[:], K.hide_q[:, t, :], start=True, stop=True)
        mm = nc.tensor.matmul(o, h["qT"][r, u, g, t * P:(t + 1) * P], h["kT"][r, u, g, 0:width],
                              start=not causal, stop=True, skip_group_check=causal)
    mm.then_inc(s["smax_ps"].sem, 1)


def dve_row_max(K, dve, s, b, u, n):
    dve.wait_ge(s["smax_ps"].sem, s["smax_ps"].after(b, n + 1))
    K.nc.vector.tensor_reduce(K.heads["nm"][:, u, :, n], K.PS[:, SMAX0 + n % 2, :].rearrange("p (t n) -> p t n", t=T),
                              AX_X, ALU.max, negate=True).then_inc(s["smax"].sem, 1)


def dve_place_max(K, dve, chain, s, b, u):
    nc, h = K.nc, K.heads
    qe = h["qe"][:, u].rearrange("p (t h) e -> p t h e", t=T)
    dve.wait_ge(s["smax"].sem, s["smax"].after(b))
    nc.vector.tensor_copy(qe[:, :, :, 24], h["nm"][:, u]).then_inc(chain.sem, 1)
    dve.wait_ge(chain.sem, chain.next())
    nc.vector.tensor_tensor(h["nr"][:], h["nm"][:, u], qe[:, :, :, 24], ALU.subtract).then_inc(chain.sem, 1)
    dve.wait_ge(chain.sem, chain.next())
    nc.vector.tensor_copy(qe[:, :, :, 25], h["nr"][:]).then_inc(chain.sem, 1)
    dve.wait_ge(chain.sem, chain.next())
    nc.vector.tensor_tensor(qe[:, :, :, 26], h["nr"][:], qe[:, :, :, 25], ALU.subtract).then_inc(s["qm"].sem, 1)


PLACE_MAX_STEPS = 3


def pe_turn_q_with_max(K, pe, s, b, u):
    pe.wait_ge(s["qm"].sem, s["qm"].after(b))
    pe_turn_heads(K, pe, K.heads["qe"], u, MISC).then_inc(s["qmT_ps"].sem, 1)


def dve_copy_qmT(K, dve, s, b, u):
    dve.wait_ge(s["qmT_ps"].sem, s["qmT_ps"].after(b))
    K.nc.vector.tensor_copy(K.heads["qT"][:, u].rearrange("p g n -> p (g n)"), K.PS[:, MISC, :].bitcast(BF16)) \
        .then_inc(s["qmT"].sem, 1)


def pe_scores_T(K, pe, s, b, u, n, causal):
    nc, h = K.nc, K.heads
    g, j = n // HG, n % HG
    bank = ST0 + n % 2
    r = slice(E * j, E * (j + 1))
    if n == 0:
        pe.wait_ge(s["qmT"].sem, s["qmT"].after(b))
    if not causal:
        for kt in range(T):
            mm = nc.tensor.matmul(K.PS[:, bank, kt * S:(kt + 1) * S], h["kT"][r, u, g, kt * P:(kt + 1) * P],
                                  h["qT"][r, u, g, :], start=True, stop=True)
    else:
        nc.tensor.matmul(K.PS[:, bank, 0:S], h["kT"][r, u, g, 0:P], h["qT"][r, u, g, :], start=True, stop=True)
        nc.tensor.matmul(K.PS[:, bank, 0:P], K.identb[:], K.hide_kT[:], start=False, stop=True, skip_group_check=True)
        nc.tensor.matmul(K.PS[:, bank, S:S + P], h["kT"][r, u, g, P:S], h["qT"][r, u, g, P:S], start=True, stop=False)
        mm = nc.tensor.matmul(K.PS[:, bank, S:S + P], K.identb[:], K.hide_kT[:], start=False, stop=True)
    mm.then_inc(s["st_ps"].sem, 1)


def act_probs(K, act, s, b, u, n, causal):
    act.wait_ge(s["st_ps"].sem, s["st_ps"].after(b, n + 1))
    w = S + P if causal else 2 * S
    K.nc.scalar.activation(K.heads["p"][:, n % 2, 0:w], K.PS[:, ST0 + n % 2, 0:w], ACT.Exp).then_inc(s["p"].sem, 1)


def pe_mix(K, pe, s, b, u, n, causal):
    nc, h = K.nc, K.heads
    g, j = n // HG, n % HG
    if n == 0:
        pe.wait_ge(s["out_banks"].sem, s["out_banks"].before(b))
        pe.wait_ge(s["v"].sem, s["v"].after(b))
    pe.wait_ge(s["p"].sem, s["p"].after(b, n + 1))
    for kt in range(T):
        q0 = kt * P if causal else 0
        mm = nc.tensor.matmul(K.PS[E * j:E * (j + 1), OUT0 + g // 2, (g % 2) * S + q0:(g % 2 + 1) * S],
                              h["ve"][:, u, kt * H + n, :], h["p"][:, n % 2, kt * S:(kt + 1) * S - q0],
                              start=kt == 0, stop=kt == T - 1, skip_group_check=causal)
    if n % (H // 2) == H // 2 - 1:
        mm.then_inc(s["oT_ps"].sem, 1)


def copy_outT(K, eng, s, b, half):
    eng.wait_ge(s["oT_ps"].sem, s["oT_ps"].after(b, half + 1))
    dst = K.heads["oT"][:, 2 * half:2 * half + 2, :].rearrange("p g n -> p (g n)")
    if half == 0:
        K.nc.vector.tensor_copy(dst, K.PS[:, OUT0, :]).then_inc(s["oT0"].sem, 1)
    else:
        K.nc.scalar.activation(dst, K.PS[:, OUT0 + 1, :], ACT.Copy).then_inc(s["oT1"].sem, 1)


def pe_turn_out(K, pe, s, b, u):
    pe.wait_ge(s["oT0"].sem, s["oT0"].after(b))
    pe.wait_ge(s["oT1"].sem, s["oT1"].after(b))
    for t in range(T):
        for g in range(G):
            mm = K.nc.tensor.transpose(K.PS[:, OUT0 + t, g * P:(g + 1) * P], K.heads["oT"][:, g, t * P:(t + 1) * P],
                                       K.ident[:])
    mm.then_inc(s["ob"].sem, 1)


def dve_normalise(K, dve, chain, s, b, u, signal):
    nc, h = K.nc, K.heads
    dve.wait_ge(s["ob"].sem, s["ob"].after(b))
    ob = K.PS[:, OUT0:OUT0 + T, :].rearrange("p t (h e) -> p t h e", e=E)
    nc.vector.reciprocal(h["rec"][:], ob[:, :, :, DH]).then_inc(chain.sem, 1)
    dve.wait_ge(chain.sem, chain.next())
    nc.vector.tensor_tensor(h["o"][:, u].rearrange("p (t h e) -> p t h e", t=T, e=DH), ob[:, :, :, 0:DH],
                            h["rec"][:].unsqueeze(3).broadcast_to([P, T, H, DH]), ALU.mult) \
        .then_inc(signal.sem, 1)


NORMALISE_STEPS = 1


def head_pipeline(eng, prep, fused, first, finish, rows=None):
    if rows:
        rows(0, 0)
    for _ in prep(0, 0):
        pass
    if rows:
        rows(1, 1)
    first(0, 0)

    def both(b, u, ahead):
        fused(b, u, prep(b + 1, 1 - u), ahead)
        finish(b, u)

    with eng.Fori(0, B // 2 - 1) as i:
        both(2 * i, 0, True)
        both(2 * i + 1, 1, True)
    both(B - 2, 0, False)
    fused(B - 1, 1, None, False)
    finish(B - 1, 1)


def nothing(b, u):
    pass


DVE_OUT_T = 6
PE_STAGES, ACT_STAGES = (0, 2, 5), (0, 2, 3, 5)
MAXIMA = {6: range(0, 1), 7: range(1, 3), 8: range(3, 4), 9: range(4, 6), 10: range(6, 8), 11: range(8, 10), 12: range(10, 11), 13: range(11, 13), 14: range(13, 15), 15: range(15, 16)}


def cross_attention_layer(K, name, layer, wq, wkv, mask=None, bias=None, wo=None, loaded=()):
    nc = K.nc
    h = K.heads
    s = dict(ln_signals(K), **head_signals(K))
    for extra in ("oT0", "oT1") if wo is None else ("oT0", "oT1", "o", "woT_ps", "woT", "wo_ps"):
        s[extra] = K.rising("heads_" + extra, 1)
    s["ctx"] = K.rising("ctx_tile_ready", 1)
    s["q_ps"], s["kv_ps"] = K.rising("q_in_psum", 1), K.rising("kv_in_psum", 1)
    s["pool_step"] = K.rising("pool_step", 1 + (mask is not None))
    plain = bias is None
    s["rows_step"] = K.rising("vector_rows_step", LN_STEPS)
    s["prep_step"] = K.rising("vector_prep_step", PLACE_MAX_STEPS)
    s["finish_step"] = K.rising("vector_finish_step", NORMALISE_STEPS + 1)
    scale = DH ** -0.5
    tg = K.gates[:, layer:layer + 1]

    with nc.Block() as block:

        @block.gpsimd
        def _(pool):
            def rows(b, u):
                pool_rstd(K, pool, s, b, u, mask)

            def prep(b, u):
                nc.gpsimd.tensor_copy(K.ctx_tile[:, u, :], K.ctxT[:, bass.ds(b * S, S)]).then_inc(s["ctx"].sem, 1)
                pool_low_parts(K, pool, s, b, u)
                yield

            def fused(b, u, stages, ahead):
                all_stages(stages)
                if ahead:
                    rows(b + 2, u)

            head_pipeline(pool, prep, fused, nothing, nothing, rows)

        @block.vector
        def _(dve):
            chain, row_chain = Chain(s["prep_step"]), Chain(s["rows_step"])
            ending = Chain(s["finish_step"])
            if not plain:
                for value, sem in loaded:
                    dve.wait_ge(sem, value)
                nc.vector.tensor_scalar(bias["q"][:], bias["q"][:], scale, None, ALU.mult).then_inc(K.sem("q_bias_scaled"), 1)
                dve.wait_ge(K.sem("q_bias_scaled"), 1)

            def rows(b, u):
                row_chain.start(b)
                dve_layernorm(K, dve, row_chain, s, b, u)

            def prep(b, u):
                chain.start(b)
                dve.wait_ge(s["q_ps"].sem, s["q_ps"].after(b))
                if plain:
                    nc.vector.tensor_scalar(h["qs"][:, u], K.PS[:, MISC + 1, 0:S], scale, None, ALU.mult) \
                        .then_inc(s["qs"].sem, 1)
                else:
                    nc.vector.scalar_tensor_tensor(
                        h["qs"][:, u].rearrange("p (t d) -> p t d", t=T), K.PS[:, MISC + 1, 0:S].rearrange("p (t d) -> p t d", t=T),
                        scale, bias["q"][:].unsqueeze(1).broadcast_to([P, T, D]), ALU.mult, ALU.add).then_inc(s["qs"].sem, 1)
                    dve.wait_ge(s["kv_ps"].sem, s["kv_ps"].after(b))
                    kv = K.PS[:, MISC, :].rearrange("p (t n) -> p t n", t=T)
                    nc.vector.tensor_tensor(
                        h["ve"][:, u, :, 0:DH].rearrange("p (t h) e -> p t h e", t=T), kv[:, :, D:2 * D].rearrange("p t (h e) -> p t h e", e=DH),
                        bias["v"][:].rearrange("p (h e) -> p h e", e=DH).unsqueeze(1).broadcast_to([P, T, H, DH]), ALU.add) \
                        .then_inc(s["v"].sem, 1)
                    nc.vector.tensor_tensor(
                        h["ks"][:, u].rearrange("p (t d) -> p t d", t=T), kv[:, :, 0:D],
                        bias["k"][:].unsqueeze(1).broadcast_to([P, T, D]), ALU.add).then_inc(s["ks"].sem, 1)
                dve_copy_qT(K, dve, s, b, u)
                yield

            def first(b, u):
                for n in range(H):
                    dve_row_max(K, dve, s, b, u, n)
                dve_place_max(K, dve, chain, s, b, u)
                dve_copy_qmT(K, dve, s, b, u)

            def fused(b, u, stages, ahead):
                all_stages(stages)
                for n in range(H):
                    if ahead and n == 5:
                        row_chain.start(b + 2)
                        dve_ln_stats(K, dve, row_chain, s, b + 2, u)
                    if ahead and n == 9:
                        dve_ln_rows(K, dve, row_chain, s, b + 2, u)
                    if stages:
                        dve_row_max(K, dve, s, b + 1, 1 - u, n)
                    if n == DVE_OUT_T:
                        copy_outT(K, dve, s, b, 0)
                if stages:
                    dve_place_max(K, dve, chain, s, b + 1, 1 - u)
                    dve_copy_qmT(K, dve, s, b + 1, 1 - u)

            def finish(b, u):
                ending.start(b)
                end = s["out_banks"] if wo is None else s["o"]
                dve_normalise(K, dve, ending, s, b, u, end)
                x = cols(K.X, b)
                dve.wait_ge(end.sem, end.after(b))
                if wo is None:
                    nc.vector.scalar_tensor_tensor(x, h["o"][:, u], tg, x, ALU.mult, ALU.add).then_inc(ending.sem, 1)
                    dve.wait_ge(ending.sem, ending.next())
                else:
                    dve.wait_ge(s["wo_ps"].sem, s["wo_ps"].after(b))
                    nc.vector.tensor_tensor(h["o"][:, u].rearrange("p (t d) -> p t d", t=T),
                                            K.PS[:, OUT0 + 1, 0:S].rearrange("p (t d) -> p t d", t=T),
                                            bias["o"][:].unsqueeze(1).broadcast_to([P, T, D]), ALU.add) \
                        .then_inc(s["out_banks"].sem, 1)
                    dve.wait_ge(s["out_banks"].sem, s["out_banks"].after(b))
                    nc.vector.scalar_tensor_tensor(x, h["o"][:, u], tg, x, ALU.mult, ALU.add).then_inc(ending.sem, 1)
                    dve.wait_ge(ending.sem, ending.next())

            head_pipeline(dve, prep, fused, first, finish, rows)

        @block.scalar
        def _(act):
            def prep(b, u):
                act_xn_transposed(K, act, s, b, u, MISC + 1)
                yield
                if plain:
                    act.wait_ge(s["kv_ps"].sem, s["kv_ps"].after(b))
                    kv = K.PS[:, MISC, :].rearrange("p (t n) -> p t n", t=T)
                    nc.scalar.activation(h["ve"][:, u, :, 0:DH].rearrange("p (t h) e -> p t h e", t=T),
                                         kv[:, :, D:2 * D].rearrange("p t (h e) -> p t h e", e=DH), ACT.Copy) \
                        .then_inc(s["v"].sem, 1)
                    nc.scalar.activation(h["ks"][:, u].rearrange("p (t d) -> p t d", t=T), kv[:, :, 0:D], ACT.Copy) \
                        .then_inc(s["ks"].sem, 1)
                yield
                act_high_parts(K, act, s, b, u)
                yield
                act_copy_kT(K, act, s, b, u)
                yield

            def first(b, u):
                pass

            def fused(b, u, stages, ahead):
                for n in range(H):
                    act_probs(K, act, s, b, u, n, False)
                    if stages and n in ACT_STAGES:
                        next(stages)
                copy_outT(K, act, s, b, 1)

            def finish(b, u):
                if wo is not None:
                    act.wait_ge(s["woT_ps"].sem, s["woT_ps"].after(b))
                    nc.scalar.activation(K.norm["xnT"][:, u, :], K.PS[:, OUT0, 0:S], ACT.Copy).then_inc(s["woT"].sem, 1)

            head_pipeline(act, prep, fused, first, finish)

        @block.tensor
        def _(pe):
            for value, sem in loaded:
                pe.wait_ge(sem, value)

            def prep(b, u):
                pe_xn_transposed(K, pe, s, b, u, MISC + 1)
                pe.wait_ge(s["ctx"].sem, s["ctx"].after(b))
                pe.wait_ge(s["qmT"].sem, s["qmT"].before(b))
                for t in range(T):
                    mm = nc.tensor.matmul(K.PS[:, MISC, t * 2 * D:(t + 1) * 2 * D], K.ctx_tile[:, u, t * P:(t + 1) * P],
                                          wkv[:], start=True, stop=True)
                mm.then_inc(s["kv_ps"].sem, 1)
                yield
                pe.wait_ge(s["xnT"].sem, s["xnT"].after(b))
                for t in range(T):
                    mm = nc.tensor.matmul(K.PS[:, MISC + 1, t * D:(t + 1) * D], K.norm["xnT"][:, u, t * P:(t + 1) * P],
                                          wq[:], start=True, stop=True)
                mm.then_inc(s["q_ps"].sem, 1)
                yield
                pe_turn_k_and_q(K, pe, s, b, u)
                yield

            def first(b, u):
                for n in range(H):
                    pe_scores(K, pe, s, b, u, n, False)
                pe_turn_q_with_max(K, pe, s, b, u)

            def fused(b, u, stages, ahead):
                for n in range(H):
                    pe_scores_T(K, pe, s, b, u, n, False)
                    if stages:
                        if n in PE_STAGES:
                            next(stages)
                    maxima = MAXIMA.get(n, ()) if stages else ()
                    for m in maxima[0:1]:
                        pe_scores(K, pe, s, b + 1, 1 - u, m, False)
                    if n >= 1:
                        pe_mix(K, pe, s, b, u, n - 1, False)
                    for m in maxima[1:]:
                        pe_scores(K, pe, s, b + 1, 1 - u, m, False)
                pe_mix(K, pe, s, b, u, H - 1, False)
                if stages:
                    pe_turn_q_with_max(K, pe, s, b + 1, 1 - u)

            def finish(b, u):
                pe_turn_out(K, pe, s, b, u)
                if wo is not None:
                    pe.wait_ge(s["o"].sem, s["o"].after(b))
                    for t in range(T):
                        mm = nc.tensor.transpose(K.PS[:, OUT0, t * P:(t + 1) * P], h["o"][:, u, t * P:(t + 1) * P],
                                                 K.ident[:])
                    mm.then_inc(s["woT_ps"].sem, 1)
                    pe.wait_ge(s["woT"].sem, s["woT"].after(b))
                    for t in range(T):
                        mm = nc.tensor.matmul(K.PS[:, OUT0 + 1, t * D:(t + 1) * D], K.norm["xnT"][:, u, t * P:(t + 1) * P],
                                              wo[:], start=True, stop=True)
                    mm.then_inc(s["wo_ps"].sem, 1)

            head_pipeline(pe, prep, fused, first, finish)



F0 = 512
F0C = F0 // P


def turned_bank(u):
    return MISC + 1 - 2 * u


def quantised_ffn_layer(K, W, loaded):
    nc = K.nc
    s = ln_signals(K, turned=False)
    s["pool_step"] = K.rising("pool_step", 1)
    s["prep_step"] = K.rising("vector_prep_step", LN_STEPS + 8)
    s["main_step"] = K.rising("vector_finish_step", 12)
    for n, per in dict(qx=1, qxT_ps=1, qxT=1, gu_ps=T, g=T, hq=1, hqT_ps=1, hqT=1, down_ps=1).items():
        s[n] = K.rising("signal_" + n, per)
    ws = Signal(K.sem("f0_weight_step"), 0, 1)
    tg = K.gates[:, 4:5]

    with ExitStack() as ctx:
        def sb(name, shape, dt=F32):
            return ctx.enter_context(nc.sbuf_tensor("f0_" + name, shape, dt))

        wabs, wmean, winv = sb("abs_sums", [P, 3]), sb("w_mean", [P, 3]), sb("w_inverse", [P, 3])
        wr = sb("w_rounded", [P, 3, F0])
        wq = sb("w_ternary", [P, 3, F0], BF16)
        am, r, dq = sb("row_max", [P, 2, T]), sb("row_scale", [P, 2, T]), sb("row_back", [P, 2, T, 2])
        v, qx = sb("rounded", [P, T * D]), sb("row_whole", [P, 2, T * D], BF16)
        qxT = sb("rowT", [P, 2, T * P], BF16)
        g, h = sb("gate", [P, T, F0]), sb("hidden", [P, T, F0])
        am2, r2, dd = sb("hidden_max", [P, T]), sb("hidden_scale", [P, T]), sb("hidden_back", [P, T])
        hq, hqT = sb("hidden_whole", [P, T, F0], BF16), sb("hiddenT", [P, T, F0C, P], BF16)
        weights = [W["f0_wg"], W["f0_wu"], W["f0_wd"]]

        with nc.Block() as block:

            @block.vector
            def _(dve):
                for value, sem in loaded:
                    dve.wait_ge(sem, value)
                for k, w in enumerate(weights):
                    nc.vector.tensor_reduce(wabs[:, k:k + 1], w[:], AX_X, ALU.add, apply_absolute_value=True) \
                        .then_inc(K.sem("f0_abs_sums"), 1)
                dve.wait_ge(K.sem("f0_sums_in_psum"), 1)
                w_step = K.sem("f0_weight_step")
                nc.vector.tensor_scalar(wmean[:], K.PS[:, MISC, 0:3], 1.0 / (F0 * D), 1e-5, ALU.mult, ALU.max).then_inc(w_step, 1)
                dve.wait_ge(w_step, 1)
                nc.vector.reciprocal(winv[:], wmean[:]).then_inc(w_step, 1)
                dve.wait_ge(w_step, 2)
                for k, w in enumerate(weights):
                    nc.vector.tensor_scalar(wr[:, k], w[:], winv[:, k:k + 1], ROUND, ALU.mult, ALU.add).then_inc(w_step, 1)
                dve.wait_ge(w_step, 5)
                nc.vector.tensor_scalar(wr[:], wr[:], ROUND + 1.0, ROUND - 1.0, ALU.min, ALU.max).then_inc(w_step, 1)
                dve.wait_ge(w_step, 6)
                nc.vector.tensor_scalar(wq[:], wr[:], ROUND, None, ALU.subtract).then_inc(w_step, 1)
                nc.vector.tensor_scalar(wmean[:], wmean[:], 1.0 / 127.0, None, ALU.mult).then_inc(w_step, 1)
                dve.wait_ge(w_step, 8)
                nc.vector.tensor_scalar(wmean[:, 2:3], wmean[:, 2:3], tg, None, ALU.mult).then_inc(w_step, 1)
                dve.wait_ge(w_step, 9)

                chain, main_chain = Chain(s["prep_step"]), Chain(s["main_step"])

                def prep(b, u):
                    chain.start(b)
                    dve_layernorm(K, dve, chain, s, b, u)
                    xn = K.norm["xn"][:, u]
                    dve.wait_ge(s["xn"].sem, s["xn"].after(b))
                    nc.vector.tensor_reduce(am[:, u], xn, AX_X, ALU.max, apply_absolute_value=True).then_inc(chain.sem, 1)
                    dve.wait_ge(chain.sem, chain.next())
                    nc.vector.tensor_scalar(am[:, u], am[:, u], 1e-5, None, ALU.max).then_inc(chain.sem, 1)
                    dve.wait_ge(chain.sem, chain.next())
                    nc.vector.reciprocal(r[:, u], am[:, u]).then_inc(chain.sem, 1)
                    dve.wait_ge(chain.sem, chain.next())
                    nc.vector.tensor_scalar(r[:, u], r[:, u], 127.0, None, ALU.mult).then_inc(chain.sem, 1)
                    dve.wait_ge(chain.sem, chain.next())
                    nc.vector.tensor_tensor(dq[:, u], am[:, u].unsqueeze(2).broadcast_to([P, T, 2]),
                                            wmean[:, 0:2].unsqueeze(1).broadcast_to([P, T, 2]), ALU.mult).then_inc(chain.sem, 1)
                    dve.wait_ge(chain.sem, chain.next())
                    nc.vector.tensor_scalar(v[:, 0:D], xn[:, 0], r[:, u, 0:1], ROUND, ALU.mult, ALU.add).then_inc(chain.sem, 1)
                    chain.next()
                    nc.vector.tensor_scalar(v[:, D:2 * D], xn[:, 1], r[:, u, 1:2], ROUND, ALU.mult, ALU.add).then_inc(chain.sem, 1)
                    dve.wait_ge(chain.sem, chain.next())
                    nc.vector.tensor_scalar(v[:], v[:], ROUND + 127.0, ROUND - 128.0, ALU.min, ALU.max).then_inc(chain.sem, 1)
                    dve.wait_ge(chain.sem, chain.next())
                    nc.vector.tensor_scalar(qx[:, u], v[:], ROUND, None, ALU.subtract).then_inc(s["qx"].sem, 1)
                    dve.wait_ge(s["qx"].sem, s["qx"].after(b))
                    yield

                def main(b, u, stages):
                    all_stages(stages)
                    c = main_chain
                    c.start(b)
                    for t in range(T):
                        dve.wait_ge(s["g"].sem, s["g"].after(b, t + 1))
                        nc.vector.scalar_tensor_tensor(h[:, t], K.PS[:, 2 * t + 1, :], dq[:, u, t, 1:2], g[:, t],
                                                       ALU.mult, ALU.mult).then_inc(c.sem, 1)
                        c.next()
                    dve.wait_ge(c.sem, c.reached())
                    nc.vector.tensor_reduce(am2[:], h[:], AX_X, ALU.max, apply_absolute_value=True).then_inc(c.sem, 1)
                    dve.wait_ge(c.sem, c.next())
                    nc.vector.tensor_scalar(am2[:], am2[:], 1e-5, None, ALU.max).then_inc(c.sem, 1)
                    dve.wait_ge(c.sem, c.next())
                    nc.vector.reciprocal(r2[:], am2[:]).then_inc(c.sem, 1)
                    dve.wait_ge(c.sem, c.next())
                    nc.vector.tensor_scalar(r2[:], r2[:], 127.0, None, ALU.mult).then_inc(c.sem, 1)
                    dve.wait_ge(c.sem, c.next())
                    nc.vector.tensor_scalar(dd[:], am2[:], wmean[:, 2:3], None, ALU.mult).then_inc(c.sem, 1)
                    dve.wait_ge(c.sem, c.next())
                    for t in range(T):
                        nc.vector.tensor_scalar(h[:, t], h[:, t], r2[:, t:t + 1], ROUND, ALU.mult, ALU.add).then_inc(c.sem, 1)
                        c.next()
                    dve.wait_ge(c.sem, c.reached())
                    nc.vector.tensor_scalar(h[:], h[:], ROUND + 127.0, ROUND - 128.0, ALU.min, ALU.max).then_inc(c.sem, 1)
                    dve.wait_ge(c.sem, c.next())
                    nc.vector.tensor_scalar(hq[:], h[:], ROUND, None, ALU.subtract).then_inc(s["hq"].sem, 1)
                    dve.wait_ge(s["hq"].sem, s["hq"].after(b))
                    dve.wait_ge(s["down_ps"].sem, s["down_ps"].after(b))
                    for t in range(T):
                        x = K.X[:, bass.ds(b * S + t * P, P)]
                        nc.vector.scalar_tensor_tensor(x, K.PS[:, OUT0, t * D:(t + 1) * D], dd[:, t:t + 1], x,
                                                       ALU.mult, ALU.add).then_inc(c.sem, 1)
                        c.next()
                    dve.wait_ge(c.sem, c.reached())

                software_pipeline(dve, prep, main)

            @block.gpsimd
            def _(pool):
                def prep(b, u):
                    pool_rstd(K, pool, s, b, u)
                    yield

                software_pipeline(pool, prep, lambda b, u, stages: all_stages(stages))

            @block.scalar
            def _(act):
                def prep(b, u):
                    act.wait_ge(s["qxT_ps"].sem, s["qxT_ps"].after(b))
                    nc.scalar.activation(qxT[:, u], K.PS[:, turned_bank(u), 0:P].bitcast(BF16), ACT.Copy).then_inc(s["qxT"].sem, 1)
                    yield

                def main(b, u, stages):
                    for t in range(T):
                        act.wait_ge(s["gu_ps"].sem, s["gu_ps"].after(b, t + 1))
                        nc.scalar.activation(g[:, t], K.PS[:, 2 * t, :], ACT.Silu, scale=dq[:, u, t, 0:1]).then_inc(s["g"].sem, 1)
                    next_stage(stages)
                    act.wait_ge(s["hqT_ps"].sem, s["hqT_ps"].after(b))
                    nc.scalar.activation(hqT[:].rearrange("p t c n -> p (t c n)"), K.PS[:, MISC, :].bitcast(BF16), ACT.Copy) \
                        .then_inc(s["hqT"].sem, 1)

                software_pipeline(act, prep, main)

            @block.tensor
            def _(pe):
                pe.wait_ge(K.sem("f0_abs_sums"), 3)
                nc.tensor.matmul(K.PS[:, MISC, 0:3], K.ones[:], wabs[:], start=True, stop=True) \
                    .then_inc(K.sem("f0_sums_in_psum"), 1)
                pe.wait_ge(K.sem("f0_weight_step"), 9)

                def prep(b, u):
                    pe.wait_ge(s["qx"].sem, s["qx"].after(b))
                    out = K.PS[:, turned_bank(u), :].bitcast(BF16)
                    for t in range(T):
                        mm = nc.tensor.transpose(out[:, t * P:(t + 1) * P], qx[:, u, t * D:(t + 1) * D], K.identb[:])
                    mm.then_inc(s["qxT_ps"].sem, 1)
                    yield

                def main(b, u, stages):
                    pe.wait_ge(s["qxT"].sem, s["qxT"].after(b))
                    for t in range(T):
                        for k in range(2):
                            mm = nc.tensor.matmul(K.PS[:, 2 * t + k, :], qxT[:, u, t * P:(t + 1) * P], wq[:, k], start=True, stop=True)
                        mm.then_inc(s["gu_ps"].sem, 1)
                    next_stage(stages)
                    pe.wait_ge(s["hq"].sem, s["hq"].after(b))
                    out = K.PS[:, MISC, :].bitcast(BF16)
                    for t in range(T):
                        for c in range(F0C):
                            mm = nc.tensor.transpose(out[:, t * F0 + c * P:t * F0 + (c + 1) * P], hq[:, t, c * P:(c + 1) * P], K.identb[:])
                    mm.then_inc(s["hqT_ps"].sem, 1)
                    pe.wait_ge(s["hqT"].sem, s["hqT"].after(b))
                    for t in range(T):
                        for c in range(F0C):
                            mm = nc.tensor.matmul(K.PS[:, OUT0, t * D:(t + 1) * D], hqT[:, t, c], wq[:, 2, c * D:(c + 1) * D],
                                                  start=c == 0, stop=c == F0C - 1)
                    mm.then_inc(s["down_ps"].sem, 1)

                software_pipeline(pe, prep, main)



H1, DH1 = 8, 64
I1 = H1 * DH1
C1 = I1 // P
V1 = DH1 + 1
MISC1 = 13

NORMED_PE_STAGES, NORMED_ACT_STAGES = (0, 1, 2, 3, 4, 6), (0, 1, 2, 3, 4, 6)


def x1_setup(K, W, t, dve, w_step):
    nc = K.nc
    nc.vector.tensor_tensor(t["qk8"][:], W["x1_qs_col"][:], W["x1_ks_col"][:], ALU.mult).then_inc(w_step, 1)
    dve.wait_ge(w_step, 1)
    nc.vector.tensor_scalar(t["qk8"][:], t["qk8"][:], 8.0, None, ALU.mult).then_inc(w_step, 1)
    dve.wait_ge(w_step, 2)
    nc.vector.tensor_tensor(t["nk"][:], W["x1_nk"][:], W["x1_nk"][:], ALU.mult).then_inc(w_step, 1)
    dve.wait_ge(w_step, 3)
    nc.vector.tensor_reduce(t["nk_sq"][:], t["nk"][:], AX_X, ALU.add).then_inc(w_step, 1)
    dve.wait_ge(w_step, 4)
    nc.vector.tensor_scalar(t["nk_sq"][:], t["nk_sq"][:], 1e-24, None, ALU.max).then_inc(w_step, 1)
    dve.wait_ge(w_step, 5)
    dve.wait_ge(K.sem("x1_null_norm"), 1)
    nc.vector.tensor_scalar(t["nk"][:], W["x1_nk"][:], t["nk_r"][:, 0:1], 8.0, ALU.mult, ALU.mult).then_inc(w_step, 1)
    dve.wait_ge(w_step, 6)
    nc.vector.tensor_tensor(t["nk"][:], t["nk"][:], W["x1_qs"][:], ALU.mult).then_inc(w_step, 1)
    dve.wait_ge(w_step, 7)
    nc.vector.tensor_tensor(t["nk"][:], t["nk"][:], W["x1_ks"][:], ALU.mult).then_inc(w_step, 1)
    dve.wait_ge(w_step, 8)
    nc.vector.tensor_tensor(t["sq"][:, 0].rearrange("p (h e) -> p h e", e=DH1), W["x1_wq"][:].rearrange("p (h e) -> p h e", e=DH1),
                            t["nk"][:].unsqueeze(1).broadcast_to([P, H1, DH1]), ALU.mult).then_inc(w_step, 1)
    dve.wait_ge(w_step, 9)
    nc.vector.tensor_reduce(t["wqn"][:], t["sq"][:, 0].rearrange("p (h e) -> p h e", e=DH1), AX_X, ALU.add).then_inc(w_step, 1)
    dve.wait_ge(w_step, 10)
    nc.vector.tensor_scalar(t["gout"][:], W["x1_gout"][:], K.gates[:, 1:2], None, ALU.mult).then_inc(w_step, 1)
    dve.wait_ge(w_step, 11)
    nc.vector.tensor_scalar(K.hide_cols[:], K.mask_k1c[:], 1.0, -HIDE, ALU.subtract, ALU.mult).then_inc(w_step, 1)
    dve.wait_ge(w_step, 12)
    nc.vector.tensor_scalar(K.hide_rows[:], K.mask_k1[:], 1.0, -HIDE, ALU.subtract, ALU.mult).then_inc(w_step, 1)
    dve.wait_ge(w_step, 13)


def normed_attention_layer(K, W, loaded):
    nc = K.nc
    s = ln_signals(K, turned=False)
    s["pool_step"] = K.rising("pool_step", 1)
    s["z_step"], s["norm_step"] = K.rising("pool_z_step", 1), K.rising("pool_norm_step", 2)
    s["rows_step"] = K.rising("vector_rows_step", LN_STEPS + 7)
    s["prep_step"] = K.rising("vector_prep_step", 9)
    s["finish_step"] = K.rising("vector_finish_step", 14)
    per = dict(z_stats=1, z_rstd=1, z=1, null=1, null_read=1, sq=4, qk_ssq=2, qk_r=2, q_rows=1, k_rows=1, filled=MISC1, read=MISC1,
               smax_ps=H1, smax=H1, m=1, mT_ps=1, mT=1, null_arg=1, null_p=1, null_v=1,
               st_ps=H1, p=H1, mix=2, half_read=2, o_rows=1, oT_ps=1, oT=1, wo_ps=1, out_banks=1, o_stats=1, o_rstd=1, hide=1, ctx=1)
    for n, k in per.items():
        s[n] = K.rising("signal_" + n, k)

    with ExitStack() as ctx:
        t_ = {}

        def sb(name, shape, dt=F32):
            t_[name] = ctx.enter_context(nc.sbuf_tensor("x1_" + name, shape, dt))
            return t_[name]

        qk8, nk, nk_sq, nk_r = sb("qk8", [P, 1]), sb("nk", [P, DH1]), sb("nk_sq", [P, 1]), sb("nk_r", [P, 1])
        wqn, gout = sb("wqn", [P, H1]), sb("gout", [P, D])
        zm, zr = sb("row_max", [P, 2, T]), sb("row_max_inverse", [P, 2, T])
        z, zst, zmv, zrs = sb("row_scaled", [P, 2, T, D]), sb("z_stats", [P, 2, T, 6]), sb("z_mean_var", [P, 2, T, 2]), sb("z_rstd", [P, 2, T])
        zT = sb("zT", [P, 2, T * P])
        raw, sq = sb("raw", [P, 4, I1]), sb("sq", [P, 4, I1])
        ssq, rn = sb("sum_squares", [P, 2, 4, H1]), sb("inverse_norms", [P, 2, 4, H1])
        qn, kn = sb("q_rows", [P, T, H1, P]), sb("k_rows", [P, T, I1])
        ve = sb("v_with_one", [P, 2, T, H1, V1])
        qT, kT = sb("qT", [P, 2, H1, S]), sb("kT", [P, 2, C1, S])
        nnull, nm, nrest = sb("minus_null", [P, 2, T, H1]), sb("minus_max", [P, 2, T, H1]), sb("rest", [P, T, H1])
        arg, pn, pnv = sb("null_argument", [P, 2, T, H1]), sb("null_prob", [P, 2, T, H1]), sb("null_value", [P, 2, T, H1, DH1])
        mtok, mT = sb("max_rows", [P, T, P], BF16), sb("maxT", [P, 2, S], BF16)
        hide = sb("hide_keys", [P, 2, T])
        p = sb("probs", [P, 2, T, S])
        rec, o, oT = sb("inverse_sums", [P, T, 4]), sb("out_rows", [P, T, H1, DH1]), sb("outT", [P, T, I1])
        ost, omv, ors, om, orr, ol = sb("o_stats", [P, T, 6]), sb("o_mean_var", [P, T, 2]), sb("o_rstd", [P, T]), sb("o_max", [P, T]), sb("o_max_inverse", [P, T]), sb("o_rows", [P, T, D])
        ove = sb("var_eps", [P, 2, T])

        with nc.Block() as block:

            @block.vector
            def _(dve):
                nc.vector.memset(qn[:], 0.0)
                nc.vector.memset(mtok[:], 0.0)
                nc.vector.memset(ve[:, :, :, :, DH1:V1], 1.0)
                for value, sem in loaded:
                    dve.wait_ge(sem, value)
                x1_setup(K, W, t_, dve, K.sem("x1_weight_step"))
                chain, row_chain, ending = Chain(s["prep_step"]), Chain(s["rows_step"]), Chain(s["finish_step"])

                def rows(b, u):
                    for _ in row_stages(b, u):
                        pass

                def row_stages(b, u):
                    chain = row_chain
                    chain.start(b)
                    dve_ln_stats(K, dve, chain, s, b, u)
                    yield
                    dve_ln_rows(K, dve, chain, s, b, u)
                    xn = K.norm["xn"][:, u]
                    dve.wait_ge(s["xn"].sem, s["xn"].after(b))
                    nc.vector.tensor_reduce(zm[:, u], xn, AX_X, ALU.max).then_inc(chain.sem, 1)
                    dve.wait_ge(chain.sem, chain.next())
                    nc.vector.reciprocal(zr[:, u], zm[:, u]).then_inc(chain.sem, 1)
                    dve.wait_ge(chain.sem, chain.next())
                    nc.vector.tensor_tensor(z[:, u], xn, zr[:, u].unsqueeze(2).broadcast_to([P, T, D]), ALU.mult).then_inc(chain.sem, 1)
                    dve.wait_ge(chain.sem, chain.next())
                    for t in range(T):
                        if t == 0:
                            settled(dve, K)
                        nc.vector.bn_stats(zst[:, u, t], z[:, u, t]).then_inc(chain.sem, 1)
                        chain.next()
                    dve.wait_ge(chain.sem, chain.reached())
                    settled(dve, K)
                    nc.vector.bn_aggr(zmv[:, u, 0], zst[:, u, 0]).then_inc(chain.sem, 1)
                    chain.next()
                    nc.vector.bn_aggr(zmv[:, u, 1], zst[:, u, 1]).then_inc(s["z_stats"].sem, 1)
                    yield
                    dve.wait_ge(s["z_rstd"].sem, s["z_rstd"].after(b))
                    nc.vector.tensor_scalar(z[:, u, 0], z[:, u, 0], zmv[:, u, 0, 0:1], zrs[:, u, 0:1], ALU.subtract, ALU.mult).then_inc(chain.sem, 1)
                    chain.next()
                    nc.vector.tensor_scalar(z[:, u, 1], z[:, u, 1], zmv[:, u, 1, 0:1], zrs[:, u, 1:2], ALU.subtract, ALU.mult) \
                        .then_inc(s["z"].sem, 1)
                    yield

                def prep(b, u):
                    chain.start(b)
                    for order, (half, src) in enumerate(((1, "q"), (0, "k"))):
                        dve.wait_ge(s["sq"].sem, s["sq"].after(b, 2 * order + 2))
                        nc.vector.tensor_reduce(ssq[:, u, 2 * half:2 * half + 2], sq[:, 2 * half:2 * half + 2].rearrange("p t (h e) -> p t h e", e=DH1),
                                                AX_X, ALU.add).then_inc(s["qk_ssq"].sem, 1)
                        dve.wait_ge(s["qk_r"].sem, s["qk_r"].after(b, order + 1))
                        dve.wait_ge(s["read"].sem, s["read"].after(b, 5 + 2 * order))
                        for t in range(T):
                            r = raw[:, 2 * half + t].rearrange("p (h e) -> p h e", e=DH1)
                            f = rn[:, u, 2 * half + t].unsqueeze(2).broadcast_to([P, H1, DH1])
                            if src == "k":
                                ins = nc.vector.tensor_tensor(kn[:, t].rearrange("p (h e) -> p h e", e=DH1), r, f, ALU.mult)
                                ins.then_inc(chain.sem if t == 0 else s["k_rows"].sem, 1)
                                if t == 0:
                                    chain.next()
                            else:
                                for odd in range(2):
                                    ins = nc.vector.tensor_tensor(qn[:, t, odd::2, odd * DH1:(odd + 1) * DH1], r[:, odd::2], f[:, odd::2], ALU.mult)
                                    if (t, odd) == (1, 1):
                                        ins.then_inc(s["q_rows"].sem, 1)
                                    else:
                                        ins.then_inc(chain.sem, 1)
                                        chain.next()
                    dve.wait_ge(s["null"].sem, s["null"].after(b))
                    nc.vector.tensor_tensor(nnull[:, u], K.PS[:, SMAX0 + 1, 0:T * H1].rearrange("p (t h) -> p t h", t=T),
                                            rn[:, u, 2:4], ALU.mult).then_inc(s["null_read"].sem, 1)
                    dve.wait_ge(s["null_read"].sem, s["null_read"].after(b))
                    nc.vector.tensor_scalar(nnull[:, u], nnull[:, u], -1.0, None, ALU.mult).then_inc(chain.sem, 1)
                    dve.wait_ge(chain.sem, chain.next())
                    yield

                def row_max(b, u, n):
                    dve.wait_ge(s["smax_ps"].sem, s["smax_ps"].after(b, n + 1))
                    nc.vector.tensor_reduce(nm[:, u, :, n], K.PS[:, SMAX0 + n % 2, :].rearrange("p (t n) -> p t n", t=T),
                                            AX_X, ALU.max, negate=True).then_inc(s["smax"].sem, 1)

                def place_max(b, u):
                    m = mtok[:, :, 0:3 * H1].rearrange("p t (h i) -> p t h i", i=3)
                    dve.wait_ge(s["smax"].sem, s["smax"].after(b))
                    nc.vector.tensor_tensor(nm[:, u], nm[:, u], nnull[:, u], ALU.min).then_inc(chain.sem, 1)
                    dve.wait_ge(chain.sem, chain.next())
                    nc.vector.tensor_copy(m[:, :, :, 0], nm[:, u]).then_inc(chain.sem, 1)
                    dve.wait_ge(chain.sem, chain.next())
                    nc.vector.tensor_tensor(nrest[:], nm[:, u], m[:, :, :, 0], ALU.subtract).then_inc(chain.sem, 1)
                    dve.wait_ge(chain.sem, chain.next())
                    nc.vector.tensor_copy(m[:, :, :, 1], nrest[:]).then_inc(chain.sem, 1)
                    dve.wait_ge(chain.sem, chain.next())
                    nc.vector.tensor_tensor(m[:, :, :, 2], nrest[:], m[:, :, :, 1], ALU.subtract).then_inc(s["m"].sem, 1)
                    nc.vector.tensor_tensor(arg[:, u], nm[:, u], nnull[:, u], ALU.subtract).then_inc(s["null_arg"].sem, 1)

                def first(b, u, later=None):
                    for n in range(H1):
                        row_max(b, u, n)
                        if later and n in (0, 3, 6):
                            next(later)
                    place_max(b, u)

                def out_half(b, u, half):
                    hs = slice(4 * half, 4 * half + 4)
                    dve.wait_ge(s["mix"].sem, s["mix"].after(b, half + 1))
                    if half == 0:
                        dve.wait_ge(s["null_v"].sem, s["null_v"].after(b))
                    ob = K.PS[:, OUT0:OUT0 + T, 0:4 * V1].rearrange("p t (h e) -> p t h e", e=V1)
                    nc.vector.tensor_tensor(rec[:], ob[:, :, :, DH1], pn[:, u, :, hs], ALU.add).then_inc(ending.sem, 1)
                    dve.wait_ge(ending.sem, ending.next())
                    nc.vector.reciprocal(rec[:], rec[:]).then_inc(ending.sem, 1)
                    dve.wait_ge(ending.sem, ending.next())
                    nc.vector.tensor_tensor(o[:, :, hs], ob[:, :, :, 0:DH1], pnv[:, u, :, hs], ALU.add).then_inc(s["half_read"].sem, 1)
                    dve.wait_ge(s["half_read"].sem, s["half_read"].after(b, half + 1))
                    ins = nc.vector.tensor_tensor(o[:, :, hs], o[:, :, hs], rec[:].unsqueeze(3).broadcast_to([P, T, 4, DH1]), ALU.mult)
                    if half == 0:
                        ins.then_inc(ending.sem, 1)
                        dve.wait_ge(ending.sem, ending.next())
                    else:
                        ins.then_inc(s["o_rows"].sem, 1)

                def fused(b, u, stages, ahead):
                    ending.start(b)
                    if stages:
                        next(stages)
                    out_half(b, u, 0)
                    out_half(b, u, 1)
                    if stages:
                        first(b + 1, 1 - u, row_stages(b + 2, u) if ahead else None)

                def finish(b, u):
                    dve.wait_ge(s["wo_ps"].sem, s["wo_ps"].after(b))
                    po = K.PS[:, OUT0, 0:T * D].rearrange("p (t d) -> p t d", t=T)
                    nc.vector.tensor_reduce(om[:], po, AX_X, ALU.max).then_inc(ending.sem, 1)
                    dve.wait_ge(ending.sem, ending.next())
                    nc.vector.reciprocal(orr[:], om[:]).then_inc(ending.sem, 1)
                    dve.wait_ge(ending.sem, ending.next())
                    nc.vector.tensor_tensor(ol[:], po, orr[:].unsqueeze(2).broadcast_to([P, T, D]), ALU.mult).then_inc(s["out_banks"].sem, 1)
                    dve.wait_ge(s["out_banks"].sem, s["out_banks"].after(b))
                    settled(dve, K)
                    for t in range(T):
                        nc.vector.bn_stats(ost[:, t], ol[:, t]).then_inc(ending.sem, 1)
                        ending.next()
                    dve.wait_ge(ending.sem, ending.reached())
                    settled(dve, K)
                    nc.vector.bn_aggr(omv[:, 0], ost[:, 0]).then_inc(ending.sem, 1)
                    ending.next()
                    nc.vector.bn_aggr(omv[:, 1], ost[:, 1]).then_inc(s["o_stats"].sem, 1)
                    dve.wait_ge(s["o_rstd"].sem, s["o_rstd"].after(b))
                    for t in range(T):
                        nc.vector.tensor_scalar(ol[:, t], ol[:, t], omv[:, t, 0:1], ors[:, t:t + 1], ALU.subtract, ALU.mult).then_inc(ending.sem, 1)
                        ending.next()
                    dve.wait_ge(ending.sem, ending.reached())
                    nc.vector.tensor_tensor(ol[:], ol[:], gout[:].unsqueeze(1).broadcast_to([P, T, D]), ALU.mult).then_inc(ending.sem, 1)
                    dve.wait_ge(ending.sem, ending.next())
                    x = cols(K.X, b)
                    nc.vector.tensor_tensor(x, ol[:].rearrange("p t d -> p (t d)"), x, ALU.add).then_inc(ending.sem, 1)
                    dve.wait_ge(ending.sem, ending.next())

                head_pipeline(dve, prep, fused, first, finish, rows)

            @block.gpsimd
            def _(pool):
                for value, sem in loaded:
                    pool.wait_ge(sem, value)
                pool.wait_ge(K.sem("x1_weight_step"), 5)
                nc.gpsimd.tensor_tensor(nk_r[:], nk_sq[:], K.neghalf[:, 0:1], ALU.pow).then_inc(K.sem("x1_null_norm"), 1)
                pool.wait_ge(K.sem("x1_weight_step"), 12)
                ps, norm_step = s["z_step"], s["norm_step"]

                def rows(b, u):
                    nc.gpsimd.tensor_copy(K.ctx_tile[:, u, :], K.ctxT[:, bass.ds(b * S, S)]).then_inc(s["ctx"].sem, 1)
                    pool_rstd(K, pool, s, b, u)
                    pool.wait_ge(s["z_stats"].sem, s["z_stats"].after(b))
                    nc.gpsimd.tensor_tensor(ove[:, 0], zmv[:, u, :, 1], K.eps5[:, 0:T], ALU.add).then_inc(ps.sem, 1)
                    pool.wait_ge(ps.sem, ps.after(b))
                    nc.gpsimd.tensor_tensor(zrs[:, u], ove[:, 0], K.neghalf[:, 0:T], ALU.pow).then_inc(s["z_rstd"].sem, 1)

                def prep(b, u):
                    nc.gpsimd.tensor_copy(hide[:, u, :], K.hide_cols[:, bass.ds(b * T, T)]).then_inc(s["hide"].sem, 1)
                    for order, half in enumerate((1, 0)):
                        pool.wait_ge(s["qk_ssq"].sem, s["qk_ssq"].after(b, order + 1))
                        sl = slice(2 * half, 2 * half + 2)
                        settled(pool, K)
                        nc.gpsimd.tensor_scalar(ssq[:, u, sl], ssq[:, u, sl], 1e-24, None, ALU.max) \
                            .then_inc(norm_step.sem, 1)
                        pool.wait_ge(norm_step.sem, norm_step.after(b, 1 + order))
                        nc.gpsimd.tensor_tensor(rn[:, u, sl], ssq[:, u, sl], K.neghalf[:, 0:T].unsqueeze(2).broadcast_to([P, T, H1]), ALU.pow) \
                            .then_inc(s["qk_r"].sem, 1)
                    yield

                def null_values(b, u):
                    pool.wait_ge(s["null_p"].sem, s["null_p"].after(b))
                    nc.gpsimd.tensor_tensor(pnv[:, u].rearrange("p t h e -> p (t h) e"), pn[:, u].rearrange("p t h -> p (t h)").unsqueeze(2).broadcast_to([P, T * H1, DH1]),
                                            W["x1_nv"][:].unsqueeze(1).broadcast_to([P, T * H1, DH1]), ALU.mult).then_inc(s["null_v"].sem, 1)

                def fused(b, u, stages, ahead):
                    if stages:
                        next(stages)
                    if ahead:
                        rows(b + 2, u)
                    if stages:
                        null_values(b + 1, 1 - u)

                def finish(b, u):
                    pool.wait_ge(s["o_stats"].sem, s["o_stats"].after(b))
                    nc.gpsimd.tensor_tensor(ove[:, 1], omv[:, :, 1], K.eps5[:, 0:T], ALU.add).then_inc(K.sem("x1_pool_ending"), 1)
                    pool.wait_ge(K.sem("x1_pool_ending"), b + 1)
                    nc.gpsimd.tensor_tensor(ors[:], ove[:, 1], K.neghalf[:, 0:T], ALU.pow).then_inc(s["o_rstd"].sem, 1)

                head_pipeline(pool, prep, fused, null_values, finish, rows)

            @block.scalar
            def _(act):
                act.wait_ge(K.sem("x1_weight_step"), 2)

                def read_bank(b, u, f, emit):
                    act.wait_ge(s["filled"].sem, s["filled"].after(b, f + 1))
                    emit(K.PS[:, MISC + (u + f) % 2, :]).then_inc(s["read"].sem, 1)

                def copy(dst, scale=None):
                    def emit(bank):
                        n = 1
                        for k in dst.shape[1:]:
                            n *= k
                        src = bank[:, 0:n]
                        if len(dst.shape) == 3:
                            src = src.rearrange("p (a b) -> p a b", a=dst.shape[1])
                        if scale is None:
                            return nc.scalar.activation(dst, src, ACT.Copy)
                        return nc.scalar.activation(dst, src, ACT.Identity, scale=scale)
                    return emit

                def prep(b, u):
                    f = 0
                    for t in range(T):
                        read_bank(b, u, f, copy(ve[:, u, t, :, 0:DH1])); f += 1
                    read_bank(b, u, f, copy(zT[:, u], W["x1_gnorm"][:, 0:1])); f += 1
                    yield
                    for k in (1, 0):
                        for t in range(T):
                            def both(bank, k=k, t=t):
                                nc.scalar.activation(sq[:, 2 * k + t], bank, ACT.Square).then_inc(s["sq"].sem, 1)
                                return nc.scalar.activation(raw[:, 2 * k + t], bank, ACT.Copy)
                            read_bank(b, u, f, both); f += 1
                        yield
                    for c in range(H1 // 2):
                        read_bank(b, u, f, copy(qT[:, u, 2 * c:2 * c + 2].rearrange("p c n -> p (c n)"), qk8[:, 0:1])); f += 1
                        if c % 2 == 1:
                            yield
                    for c in range(C1 // 2):
                        read_bank(b, u, f, copy(kT[:, u, 2 * c:2 * c + 2].rearrange("p c n -> p (c n)"))); f += 1
                    yield

                def maxima(b, u):
                    act.wait_ge(s["null_arg"].sem, s["null_arg"].after(b))
                    nc.scalar.activation(pn[:, u], arg[:, u], ACT.Exp).then_inc(s["null_p"].sem, 1)
                    act.wait_ge(s["mT_ps"].sem, s["mT_ps"].after(b))
                    nc.scalar.activation(mT[:, u], K.PS[:, SMAX0, 0:P].bitcast(BF16), ACT.Copy).then_inc(s["mT"].sem, 1)

                def fused(b, u, stages, ahead):
                    act.wait_ge(s["hide"].sem, s["hide"].after(b))
                    for n in range(H1):
                        act.wait_ge(s["st_ps"].sem, s["st_ps"].after(b, n + 1))
                        for kt in range(T):
                            ins = nc.scalar.activation(p[:, n % 2, kt], K.PS[:, ST0 + n % 2, kt * S:(kt + 1) * S], ACT.Exp, bias=hide[:, u, kt:kt + 1])
                        ins.then_inc(s["p"].sem, 1)
                        for _ in range(NORMED_ACT_STAGES.count(n) if stages else 0):
                            next(stages)
                    act.wait_ge(s["oT_ps"].sem, s["oT_ps"].after(b))
                    nc.scalar.activation(oT[:], K.PS[:, OUT0:OUT0 + T, :], ACT.Copy).then_inc(s["oT"].sem, 1)
                    if stages:
                        maxima(b + 1, 1 - u)

                def finish(b, u):
                    pass

                head_pipeline(act, prep, fused, maxima, finish)

            @block.tensor
            def _(pe):
                for value, sem in loaded:
                    pe.wait_ge(sem, value)
                pe.wait_ge(K.sem("x1_weight_step"), 13)
                def fill(b, u, f, emit):
                    pe.wait_ge(s["read"].sem, b * MISC1 + (s["read"].base + f - 1))
                    emit(K.PS[:, MISC + (u + f) % 2, :]).then_inc(s["filled"].sem, 1)

                def prep(b, u):
                    f = 0
                    pe.wait_ge(s["ctx"].sem, s["ctx"].after(b))
                    for t in range(T):
                        fill(b, u, f, lambda bank: nc.tensor.matmul(bank, K.ctx_tile[:, u, t * P:(t + 1) * P], W["x1_wv"][:], start=True, stop=True)); f += 1
                    pe.wait_ge(s["z"].sem, s["z"].after(b))

                    def turn_z(bank):
                        for t in range(T):
                            mm = nc.tensor.transpose(bank[:, t * P:(t + 1) * P], z[:, u, t], K.ident[:])
                        return mm
                    fill(b, u, f, turn_z); f += 1
                    yield
                    pe.wait_ge(s["read"].sem, s["read"].after(b, f))
                    for t in range(T):
                        fill(b, u, f, lambda bank: nc.tensor.matmul(bank, zT[:, u, t * P:(t + 1) * P], W["x1_wq"][:], start=True, stop=True)); f += 1
                    for t in range(T):
                        mm = nc.tensor.matmul(K.PS[:, SMAX0 + 1, t * H1:(t + 1) * H1], zT[:, u, t * P:(t + 1) * P], wqn[:], start=True, stop=True)
                    mm.then_inc(s["null"].sem, 1)
                    yield
                    for t in range(T):
                        fill(b, u, f, lambda bank: nc.tensor.matmul(bank, K.ctx_tile[:, u, t * P:(t + 1) * P], W["x1_wk"][:], start=True, stop=True)); f += 1
                    yield
                    pe.wait_ge(s["q_rows"].sem, s["q_rows"].after(b))

                    def turn_q(c):
                        def emit(bank):
                            for cc in range(2):
                                for t in range(T):
                                    mm = nc.tensor.transpose(bank[:, cc * S + t * P:cc * S + (t + 1) * P], qn[:, t, 2 * c + cc], K.ident[:])
                            return mm
                        return emit
                    for c in range(H1 // 2):
                        fill(b, u, f, turn_q(c)); f += 1
                        if c % 2 == 1:
                            yield
                    pe.wait_ge(s["k_rows"].sem, s["k_rows"].after(b))

                    def turn_k(c):
                        def emit(bank):
                            for cc in range(2):
                                for t in range(T):
                                    mm = nc.tensor.transpose(bank[:, cc * S + t * P:cc * S + (t + 1) * P], kn[:, t, (2 * c + cc) * P:(2 * c + cc + 1) * P], K.ident[:])
                            return mm
                        return emit
                    for c in range(C1 // 2):
                        fill(b, u, f, turn_k(c)); f += 1
                    yield

                def scores(b, u, n):
                    if n == 0:
                        pe.wait_ge(s["read"].sem, s["read"].after(b))
                        pe.wait_ge(s["null_read"].sem, s["null_read"].after(b))
                    if n >= 2:
                        pe.wait_ge(s["smax"].sem, s["smax"].after(b, n - 1))
                    for t in range(T):
                        o_ = K.PS[:, SMAX0 + n % 2, t * S:(t + 1) * S]
                        nc.tensor.matmul(o_, K.identb[:], K.hide_rows[:, bass.ds(b * S, S)], start=True, stop=False)
                        mm = nc.tensor.matmul(o_, qT[:, u, n, t * P:(t + 1) * P], kT[:, u, n // 2, :], start=False, stop=True)
                    mm.then_inc(s["smax_ps"].sem, 1)

                def turn_max(b, u):
                    pe.wait_ge(s["m"].sem, s["m"].after(b))
                    for t in range(T):
                        mm = nc.tensor.transpose(K.PS[:, SMAX0, :].bitcast(BF16)[:, t * P:(t + 1) * P], mtok[:, t], K.identb[:])
                    mm.then_inc(s["mT_ps"].sem, 1)

                def scores_T(b, u, n):
                    if n == 0:
                        pe.wait_ge(s["mT"].sem, s["mT"].after(b))
                    for kt in range(T):
                        o_ = K.PS[:, ST0 + n % 2, kt * S:(kt + 1) * S]
                        nc.tensor.matmul(o_, kT[:, u, n // 2, kt * P:(kt + 1) * P], qT[:, u, n, :], start=True, stop=False)
                        mm = nc.tensor.matmul(o_, K.pick_max[:, n, :], mT[:, u], start=False, stop=True)
                    mm.then_inc(s["st_ps"].sem, 1)

                def mix(b, u, n):
                    if n == 0:
                        pe.wait_ge(s["out_banks"].sem, s["out_banks"].before(b))
                    if n == H1 // 2:
                        pe.wait_ge(s["half_read"].sem, s["half_read"].after(b, 1))
                    pe.wait_ge(s["p"].sem, s["p"].after(b, n + 1))
                    c = (n % 4) * V1
                    for t in range(T):
                        for kt in range(T):
                            mm = nc.tensor.matmul(K.PS[:, OUT0 + t, c:c + V1], p[:, n % 2, kt, t * P:(t + 1) * P], ve[:, u, kt, n, :],
                                                  start=kt == 0, stop=kt == T - 1)
                    if n % 4 == 3:
                        mm.then_inc(s["mix"].sem, 1)

                def first(b, u):
                    for n in range(H1):
                        scores(b, u, n)
                    turn_max(b, u)

                def fused(b, u, stages, ahead):
                    for n in range(H1):
                        scores_T(b, u, n)
                        for _ in range(NORMED_PE_STAGES.count(n) if stages else 0):
                            next(stages)
                        if n >= 1:
                            mix(b, u, n - 1)
                    mix(b, u, H1 - 1)
                    if stages:
                        for n in range(H1):
                            scores(b + 1, 1 - u, n)
                    turn_out(b, u)
                    if stages:
                        turn_max(b + 1, 1 - u)

                def turn_out(b, u):
                    pe.wait_ge(s["o_rows"].sem, s["o_rows"].after(b))
                    for t in range(T):
                        for c in range(C1):
                            mm = nc.tensor.transpose(K.PS[:, OUT0 + t, c * P:(c + 1) * P],
                                                     o[:, t, 2 * c:2 * c + 2].rearrange("p h e -> p (h e)"), K.ident[:])
                    mm.then_inc(s["oT_ps"].sem, 1)

                def finish(b, u):
                    pe.wait_ge(s["oT"].sem, s["oT"].after(b))
                    for t in range(T):
                        for c in range(C1):
                            mm = nc.tensor.matmul(K.PS[:, OUT0, t * D:(t + 1) * D], oT[:, t, c * P:(c + 1) * P], W["x1_wo"][:, c * D:(c + 1) * D],
                                                  start=c == 0, stop=c == C1 - 1)
                    mm.then_inc(s["wo_ps"].sem, 1)

                head_pipeline(pe, prep, fused, first, finish)



LAT = 64
LATENT_PE_STAGES, LATENT_ACT_STAGES = (0, 1, 4, 5, 8), (0, 4, 7, 8)
LATENT_MAXIMA = {9: range(0, 2), 10: range(2, 4), 11: range(4, 7), 12: range(7, 9), 13: range(9, 12), 14: range(12, 14), 15: range(14, 16)}


def latent_attention_layer(K, W, loaded):
    nc = K.nc
    h = K.heads
    s = dict(ln_signals(K), **head_signals(K))
    for extra in ("oT0", "oT1", "o", "woT_ps", "woT", "wo_ps"):
        s[extra] = K.rising("heads_" + extra, 1)
    for extra in ("rms_sum", "rms_r", "rms", "lat_stats", "lat_rstd", "lat", "latT_ps", "latT"):
        s[extra] = K.rising("signal_" + extra, 1)
    s["q_ps"], s["kv_ps"] = K.rising("q_in_psum", 1), K.rising("kv_in_psum", 1)
    s["pool_step"] = K.rising("pool_step", 1)
    s["latent_step"] = K.rising("pool_latent_step", 1)
    s["rows_step"] = K.rising("vector_rows_step", LN_STEPS + 2)
    s["prep_step"] = K.rising("vector_prep_step", 4 + 6 + PLACE_MAX_STEPS)
    s["finish_step"] = K.rising("vector_finish_step", NORMALISE_STEPS + 1)
    tg = K.gates[:, 5:6]

    with ExitStack() as ctx:
        def sb(name, shape, dt=F32):
            return ctx.enter_context(nc.sbuf_tensor("f1_" + name, shape, dt))

        sq, ss, rr, rn = sb("squares", [P, T, D]), sb("square_sums", [P, 2, T]), sb("inverse_rms", [P, 2, T]), sb("rms_rows", [P, 2, T, D])
        lst, lmv, lve, lrs = sb("lat_stats", [P, T, 6]), sb("lat_mean_var", [P, 2, T, 2]), sb("lat_var_eps", [P, T]), sb("lat_rstd", [P, 2, T])
        lat, latT = sb("lat_rows", [P, T, P]), sb("latT", [P, 2, T * P])
        ra, rb = sb("turned_a", [P, T * H, DH]), sb("turned_b", [P, T * H, DH])
        wukv = sb("w_k_v", [P, 2 * D])
        rope = sb("rope_for_q", [P, 2, T, DH])

        with nc.Block() as block:

            @block.gpsimd
            def _(pool):
                ps = s["latent_step"]

                def rows(b, u):
                    pool_rstd(K, pool, s, b, u)
                    pool.wait_ge(s["rms_sum"].sem, s["rms_sum"].after(b))
                    nc.gpsimd.tensor_tensor(rr[:, u], ss[:, u], K.neghalf[:, 0:T], ALU.pow).then_inc(s["rms_r"].sem, 1)

                def prep(b, u):
                    pool.wait_ge(s["lat_stats"].sem, s["lat_stats"].after(b))
                    nc.gpsimd.tensor_tensor(lve[:], lmv[:, u, :, 1], K.eps5[:, 0:T], ALU.add).then_inc(ps.sem, 1)
                    pool.wait_ge(ps.sem, ps.after(b))
                    nc.gpsimd.tensor_tensor(lrs[:, u], lve[:], K.neghalf[:, 0:T], ALU.pow).then_inc(s["lat_rstd"].sem, 1)
                    pool_low_parts(K, pool, s, b, u)
                    yield

                def fused(b, u, stages, ahead):
                    all_stages(stages)
                    if ahead:
                        rows(b + 2, u)

                head_pipeline(pool, prep, fused, nothing, nothing, rows)

            @block.vector
            def _(dve):
                setup = K.sem("f1_setup_step")
                nc.vector.memset(lat[:], 0.0)
                nc.vector.memset(wukv[:], 0.0).then_inc(setup, 1)
                for value, sem in loaded:
                    dve.wait_ge(sem, value)
                dve.wait_ge(setup, 1)
                nc.vector.tensor_copy(wukv[0:LAT, :], W["f1_wukv"][:]).then_inc(setup, 1)
                nc.vector.tensor_scalar(rope[:].rearrange("p a t e -> p (a t e)"), W["f1_rope"][:], DH ** -0.5, None, ALU.mult).then_inc(setup, 1)
                dve.wait_ge(setup, 3)
                chain, row_chain, ending = Chain(s["prep_step"]), Chain(s["rows_step"]), Chain(s["finish_step"])

                def rotate(src, tables, dst, signal, last_reads):
                    x_ = src.rearrange("p t (h e) -> p t h e", e=DH)
                    a4, b4 = (v.rearrange("p (t h) e -> p t h e", t=T) for v in (ra[:], rb[:]))
                    cos, sin = (tables[:, k].unsqueeze(2).broadcast_to([P, T, H, DH]) for k in range(2))
                    hf = DH // 2
                    nc.vector.tensor_tensor(a4, x_, cos, ALU.mult).then_inc(chain.sem, 1)
                    chain.next()
                    nc.vector.tensor_tensor(b4[:, :, :, 0:hf], x_[:, :, :, hf:DH], sin[:, :, :, 0:hf], ALU.mult).then_inc(chain.sem, 1)
                    chain.next()
                    last = nc.vector.tensor_tensor(b4[:, :, :, hf:DH], x_[:, :, :, 0:hf], sin[:, :, :, hf:DH], ALU.mult)
                    last.then_inc(chain.sem, 1)
                    dve.wait_ge(chain.sem, chain.next())
                    nc.vector.tensor_tensor(dst, ra[:].rearrange("p h e -> p (h e)"), rb[:].rearrange("p h e -> p (h e)"), ALU.add).then_inc(signal.sem, 1)

                def rows(b, u):
                    for _ in row_stages(b, u):
                        pass

                def row_stages(b, u):
                    row_chain.start(b)
                    dve_ln_stats(K, dve, row_chain, s, b, u)
                    yield
                    y = cols(K.Y, b).rearrange("p (t d) -> p t d", t=T)
                    dve_ln_rows(K, dve, row_chain, s, b, u, y)
                    dve.wait_ge(s["xn"].sem, s["xn"].after(b))
                    nc.vector.tensor_tensor(sq[:], y, y, ALU.mult).then_inc(row_chain.sem, 1)
                    dve.wait_ge(row_chain.sem, row_chain.next())
                    nc.vector.tensor_reduce(ss[:, u], sq[:], AX_X, ALU.add).then_inc(row_chain.sem, 1)
                    dve.wait_ge(row_chain.sem, row_chain.next())
                    nc.vector.tensor_scalar(ss[:, u], ss[:, u], 1.0 / D, 1e-6, ALU.mult, ALU.add).then_inc(s["rms_sum"].sem, 1)
                    yield
                    dve.wait_ge(s["rms_r"].sem, s["rms_r"].after(b))
                    nc.vector.tensor_tensor(rn[:, u], y, rr[:, u].unsqueeze(2).broadcast_to([P, T, D]), ALU.mult).then_inc(s["rms"].sem, 1)
                    yield

                def prep(b, u):
                    chain.start(b)
                    dve.wait_ge(s["q_ps"].sem, s["q_ps"].after(b))
                    ql = K.PS[:, MISC + 1, 0:T * (D + LAT)].rearrange("p (t n) -> p t n", t=T)
                    settled(dve, K)
                    for t in range(T):
                        nc.vector.bn_stats(lst[:, t], ql[:, t, D:D + LAT]).then_inc(chain.sem, 1)
                        chain.next()
                    dve.wait_ge(chain.sem, chain.reached())
                    settled(dve, K)
                    nc.vector.bn_aggr(lmv[:, u, 0], lst[:, 0]).then_inc(chain.sem, 1)
                    chain.next()
                    nc.vector.bn_aggr(lmv[:, u, 1], lst[:, 1]).then_inc(s["lat_stats"].sem, 1)
                    dve.wait_ge(s["lat_rstd"].sem, s["lat_rstd"].after(b))
                    nc.vector.tensor_scalar(lat[:, 0, 0:LAT], ql[:, 0, D:D + LAT], lmv[:, u, 0, 0:1], lrs[:, u, 0:1], ALU.subtract, ALU.mult).then_inc(chain.sem, 1)
                    chain.next()
                    nc.vector.tensor_scalar(lat[:, 1, 0:LAT], ql[:, 1, D:D + LAT], lmv[:, u, 1, 0:1], lrs[:, u, 1:2], ALU.subtract, ALU.mult) \
                        .then_inc(s["lat"].sem, 1)
                    rotate(ql[:, :, 0:D], rope, h["qs"][:, u], s["qs"], None)
                    dve.wait_ge(s["qs"].sem, s["qs"].after(b))
                    dve.wait_ge(s["kv_ps"].sem, s["kv_ps"].after(b))
                    kv = K.PS[:, MISC, :].rearrange("p (t n) -> p t n", t=T)
                    nc.vector.tensor_copy(h["ve"][:, u, :, 0:DH].rearrange("p (t h) e -> p t h e", t=T),
                                          kv[:, :, D:2 * D].rearrange("p t (h e) -> p t h e", e=DH)).then_inc(s["v"].sem, 1)
                    rotate(kv[:, :, 0:D], W["f1_rope"][:].rearrange("p (a t e) -> p a t e", a=2, t=T), h["ks"][:, u], s["ks"], None)
                    dve_copy_qT(K, dve, s, b, u)
                    yield

                def first(b, u):
                    for n in range(H):
                        dve_row_max(K, dve, s, b, u, n)
                    dve_place_max(K, dve, chain, s, b, u)
                    dve_copy_qmT(K, dve, s, b, u)

                def fused(b, u, stages, ahead):
                    all_stages(stages)
                    later = row_stages(b + 2, u) if ahead else None
                    for n in range(H):
                        if later and n in (3, 6, 9):
                            next(later)
                        if stages:
                            dve_row_max(K, dve, s, b + 1, 1 - u, n)
                        if n == DVE_OUT_T:
                            copy_outT(K, dve, s, b, 0)
                    if stages:
                        dve_place_max(K, dve, chain, s, b + 1, 1 - u)
                        dve_copy_qmT(K, dve, s, b + 1, 1 - u)

                def finish(b, u):
                    ending.start(b)
                    dve_normalise(K, dve, ending, s, b, u, s["o"])
                    dve.wait_ge(s["wo_ps"].sem, s["wo_ps"].after(b))
                    y1 = cols(K.Y, b)
                    nc.vector.tensor_tensor(y1, K.PS[:, OUT0 + 1, 0:S], y1, ALU.add).then_inc(s["out_banks"].sem, 1)
                    dve.wait_ge(s["out_banks"].sem, s["out_banks"].after(b))
                    x = cols(K.X, b)
                    nc.vector.scalar_tensor_tensor(x, y1, tg, x, ALU.mult, ALU.add).then_inc(ending.sem, 1)
                    dve.wait_ge(ending.sem, ending.next())

                head_pipeline(dve, prep, fused, first, finish, rows)

            @block.scalar
            def _(act):
                for value, sem in loaded:
                    act.wait_ge(sem, value)

                def prep(b, u):
                    act.wait_ge(s["xnT_ps"].sem, s["xnT_ps"].after(b))
                    nc.scalar.activation(K.norm["xnT"][:, u, :], K.PS[:, MISC + 1, 0:S], ACT.Identity, scale=W["f1_norm1"][:, 0:1]) \
                        .then_inc(s["xnT"].sem, 1)
                    yield
                    act.wait_ge(s["latT_ps"].sem, s["latT_ps"].after(b))
                    nc.scalar.activation(latT[:, u], K.PS[:, MISC, 0:S], ACT.Identity, scale=W["f1_ln_g"][:, 0:1], bias=W["f1_ln_b"][:, 0:1]) \
                        .then_inc(s["latT"].sem, 1)
                    yield
                    act_high_parts(K, act, s, b, u)
                    yield
                    act_copy_kT(K, act, s, b, u)
                    yield

                def first(b, u):
                    pass

                def fused(b, u, stages, ahead):
                    for n in range(H):
                        act_probs(K, act, s, b, u, n, True)
                        for _ in range(LATENT_ACT_STAGES.count(n) if stages else 0):
                            next(stages)
                    copy_outT(K, act, s, b, 1)

                def finish(b, u):
                    act.wait_ge(s["woT_ps"].sem, s["woT_ps"].after(b))
                    nc.scalar.activation(K.norm["xnT"][:, u, :], K.PS[:, OUT0, 0:S], ACT.Copy).then_inc(s["woT"].sem, 1)

                head_pipeline(act, prep, fused, first, finish)

            @block.tensor
            def _(pe):
                for value, sem in loaded:
                    pe.wait_ge(sem, value)
                pe.wait_ge(K.sem("f1_setup_step"), 3)

                def prep(b, u):
                    pe.wait_ge(s["rms"].sem, s["rms"].after(b))
                    for t in range(T):
                        mm = nc.tensor.transpose(K.PS[:, MISC + 1, t * P:(t + 1) * P], rn[:, u, t], K.ident[:])
                    mm.then_inc(s["xnT_ps"].sem, 1)
                    yield
                    pe.wait_ge(s["xnT"].sem, s["xnT"].after(b))
                    for t in range(T):
                        mm = nc.tensor.matmul(K.PS[:, MISC + 1, t * (D + LAT):(t + 1) * (D + LAT)], K.norm["xnT"][:, u, t * P:(t + 1) * P],
                                              W["f1_wqd"][:], start=True, stop=True)
                    mm.then_inc(s["q_ps"].sem, 1)
                    yield
                    pe.wait_ge(s["lat"].sem, s["lat"].after(b))
                    pe.wait_ge(s["qmT"].sem, s["qmT"].before(b))
                    for t in range(T):
                        mm = nc.tensor.transpose(K.PS[:, MISC, t * P:(t + 1) * P], lat[:, t], K.ident[:])
                    mm.then_inc(s["latT_ps"].sem, 1)
                    yield
                    pe.wait_ge(s["latT"].sem, s["latT"].after(b))
                    for t in range(T):
                        mm = nc.tensor.matmul(K.PS[:, MISC, t * 2 * D:(t + 1) * 2 * D], latT[:, u, t * P:(t + 1) * P], wukv[:],
                                              start=True, stop=True)
                    mm.then_inc(s["kv_ps"].sem, 1)
                    yield
                    pe_turn_k_and_q(K, pe, s, b, u)
                    yield

                def first(b, u):
                    for n in range(H):
                        pe_scores(K, pe, s, b, u, n, True)
                    pe_turn_q_with_max(K, pe, s, b, u)

                def fused(b, u, stages, ahead):
                    for n in range(H):
                        pe_scores_T(K, pe, s, b, u, n, True)
                        if stages and n in LATENT_PE_STAGES:
                            next(stages)
                        maxima = LATENT_MAXIMA.get(n, ()) if stages else ()
                        for m in maxima[0:1]:
                            pe_scores(K, pe, s, b + 1, 1 - u, m, True)
                        if n >= 1:
                            pe_mix(K, pe, s, b, u, n - 1, True)
                        for m in maxima[1:]:
                            pe_scores(K, pe, s, b + 1, 1 - u, m, True)
                    pe_mix(K, pe, s, b, u, H - 1, True)
                    if stages:
                        pe_turn_q_with_max(K, pe, s, b + 1, 1 - u)

                def finish(b, u):
                    pe_turn_out(K, pe, s, b, u)
                    pe.wait_ge(s["o"].sem, s["o"].after(b))
                    for t in range(T):
                        mm = nc.tensor.transpose(K.PS[:, OUT0, t * P:(t + 1) * P], h["o"][:, u, t * P:(t + 1) * P], K.ident[:])
                    mm.then_inc(s["woT_ps"].sem, 1)
                    pe.wait_ge(s["woT"].sem, s["woT"].after(b))
                    for t in range(T):
                        mm = nc.tensor.matmul(K.PS[:, OUT0 + 1, t * D:(t + 1) * D], K.norm["xnT"][:, u, t * P:(t + 1) * P],
                                              W["f1_wo"][:], start=True, stop=True)
                    mm.then_inc(s["wo_ps"].sem, 1)

                head_pipeline(pe, prep, fused, first, finish)


NE1, HE1 = 4, 512
CE1 = HE1 // P


def first_of_four(nc, dve, chain, lg, mx, eq, oh, run):
    nc.vector.tensor_reduce(mx, lg, AX_X, ALU.max).then_inc(chain.sem, 1)
    dve.wait_ge(chain.sem, chain.next())
    nc.vector.tensor_tensor(eq, lg, mx.unsqueeze(2).broadcast_to([P, T, NE1]), ALU.is_ge).then_inc(chain.sem, 1)
    dve.wait_ge(chain.sem, chain.next())
    nc.vector.tensor_copy(oh[:, :, 0], eq[:, :, 0]).then_inc(chain.sem, 1)
    chain.next()
    nc.vector.tensor_tensor(oh[:, :, 1], eq[:, :, 1], eq[:, :, 0], ALU.is_gt).then_inc(chain.sem, 1)
    chain.next()
    nc.vector.tensor_tensor(run[:, :, 0], eq[:, :, 0], eq[:, :, 1], ALU.max).then_inc(chain.sem, 1)
    dve.wait_ge(chain.sem, chain.next())
    nc.vector.tensor_tensor(oh[:, :, 2], eq[:, :, 2], run[:, :, 0], ALU.is_gt).then_inc(chain.sem, 1)
    chain.next()
    nc.vector.tensor_tensor(run[:, :, 1], run[:, :, 0], eq[:, :, 2], ALU.max).then_inc(chain.sem, 1)
    dve.wait_ge(chain.sem, chain.next())
    nc.vector.tensor_tensor(oh[:, :, 3], eq[:, :, 3], run[:, :, 1], ALU.is_gt).then_inc(chain.sem, 1)
    dve.wait_ge(chain.sem, chain.next())


def expert_layer(K, W, loaded):
    nc = K.nc
    s = {}
    per = dict(rms_sum=1, rms_r=1, rms=1, rT_ps=1, rT=1, logits=1, up_a=NE1, up_b=NE1, ha=NE1, hb=NE1, down_ps=NE1, one_hot=1, bias=1)
    for n, k in per.items():
        s[n] = K.rising("signal_" + n, k)
    s["pool_step"] = K.rising("pool_step", 2)
    s["prep_step"] = K.rising("vector_prep_step", 2 + 1 + 8)
    s["main_step"] = K.rising("vector_finish_step", NE1 * T + 1)
    tg = K.gates[:, 5:6]

    with ExitStack() as ctx:
        def sb(name, shape, dt=F32):
            return ctx.enter_context(nc.sbuf_tensor("m1_" + name, shape, dt))

        sq, ss, rr, rn = sb("squares", [P, T, D]), sb("square_sums", [P, 2, T]), sb("inverse_rms", [P, 2, T]), sb("rms_rows", [P, 2, T, D])
        rT = sb("rowsT", [P, 2, T * P])
        lg, mx, eq, run = sb("logits", [P, T, NE1]), sb("logit_max", [P, T]), sb("equals_max", [P, T, NE1]), sb("taken", [P, T, 2])
        oh, ohg = sb("one_hot", [P, T, NE1]), sb("gated_one_hot", [P, 2, T, NE1])
        hT = sb("hiddenT", [P, 2, CE1, S])
        bt = sb("biases", [P, 2, NE1, S])

        with nc.Block() as block:

            @block.gpsimd
            def _(pool):
                for value, sem in loaded:
                    pool.wait_ge(sem, value)
                ps = s["pool_step"]

                def prep(b, u):
                    pool.wait_ge(s["rms_sum"].sem, s["rms_sum"].after(b))
                    nc.gpsimd.tensor_tensor(rr[:, u], ss[:, u], K.neghalf[:, 0:T], ALU.pow).then_inc(s["rms_r"].sem, 1)
                    pool.wait_ge(s["one_hot"].sem, s["one_hot"].after(b))
                    nc.gpsimd.tensor_tensor(bt[:, u].rearrange("p e (t d) -> p e t d", t=T),
                                            W["f1_b2"][:].rearrange("p (e d) -> p e d", e=NE1).unsqueeze(2).broadcast_to([P, NE1, T, D]),
                                            ohg[:, u].rearrange("p t e -> p e t").unsqueeze(3).broadcast_to([P, NE1, T, D]), ALU.mult) \
                        .then_inc(ps.sem, 1)
                    pool.wait_ge(ps.sem, ps.after(b, 1))
                    nc.gpsimd.tensor_tensor(bt[:, u, 0:2], bt[:, u, 0:2], bt[:, u, 2:4], ALU.add).then_inc(ps.sem, 1)
                    pool.wait_ge(ps.sem, ps.after(b, 2))
                    nc.gpsimd.tensor_tensor(bt[:, u, 0], bt[:, u, 0], bt[:, u, 1], ALU.add).then_inc(s["bias"].sem, 1)
                    yield

                software_pipeline(pool, prep, lambda b, u, stages: all_stages(stages))

            @block.vector
            def _(dve):
                for value, sem in loaded:
                    dve.wait_ge(sem, value)
                chain, ending = Chain(s["prep_step"]), Chain(s["main_step"])

                def prep(b, u):
                    chain.start(b)
                    y1 = cols(K.Y, b)
                    nc.vector.tensor_tensor(sq[:].rearrange("p t d -> p (t d)"), y1, y1, ALU.mult).then_inc(chain.sem, 1)
                    dve.wait_ge(chain.sem, chain.next())
                    nc.vector.tensor_reduce(ss[:, u], sq[:], AX_X, ALU.add).then_inc(chain.sem, 1)
                    dve.wait_ge(chain.sem, chain.next())
                    nc.vector.tensor_scalar(ss[:, u], ss[:, u], 1.0 / D, 1e-6, ALU.mult, ALU.add).then_inc(s["rms_sum"].sem, 1)
                    yield
                    dve.wait_ge(s["rms_r"].sem, s["rms_r"].after(b))
                    nc.vector.tensor_tensor(rn[:, u], y1.rearrange("p (t d) -> p t d", t=T), rr[:, u].unsqueeze(2).broadcast_to([P, T, D]), ALU.mult) \
                        .then_inc(s["rms"].sem, 1)
                    yield
                    dve.wait_ge(s["logits"].sem, s["logits"].after(b))
                    nc.vector.tensor_tensor(lg[:], K.PS[:, MISC + 1, 0:T * NE1].rearrange("p (t e) -> p t e", t=T),
                                            W["f1_gate_b"][:].unsqueeze(1).broadcast_to([P, T, NE1]), ALU.add).then_inc(chain.sem, 1)
                    dve.wait_ge(chain.sem, chain.next())
                    first_of_four(nc, dve, chain, lg[:], mx[:], eq[:], oh, run)
                    nc.vector.tensor_scalar(ohg[:, u], oh[:], tg, None, ALU.mult).then_inc(s["one_hot"].sem, 1)
                    dve.wait_ge(s["one_hot"].sem, s["one_hot"].after(b))
                    yield

                def main(b, u, stages):
                    ending.start(b)

                    def add_expert(e):
                        dve.wait_ge(s["down_ps"].sem, s["down_ps"].after(b, e + 1))
                        for t in range(T):
                            x = K.X[:, bass.ds(b * S + t * P, P)]
                            if t == 0 and e > 0:
                                dve.wait_ge(ending.sem, ending.reached())
                            ins = nc.vector.scalar_tensor_tensor(x, K.PS[:, OUT0 + e % 2, t * D:(t + 1) * D], ohg[:, u, t, e:e + 1], x, ALU.mult, ALU.add)
                            ins.then_inc(ending.sem, 1)
                            ending.next()

                    for e in range(NE1):
                        dve.wait_ge(s["up_b"].sem, s["up_b"].after(b, e + 1))
                        for c in range(2, CE1):
                            ins = nc.vector.tensor_scalar(hT[:, e % 2, c], K.PS[:, 2 * (e % 2) + 1, (c - 2) * S:(c - 1) * S],
                                                          W["f1_b1"][:, e * CE1 + c:e * CE1 + c + 1], 0.0, ALU.add, ALU.max)
                        ins.then_inc(s["hb"].sem, 1)
                        if e >= 1:
                            add_expert(e - 1)
                        if e != 2:
                            next_stage(stages)
                    add_expert(NE1 - 1)
                    dve.wait_ge(ending.sem, ending.reached())
                    dve.wait_ge(s["bias"].sem, s["bias"].after(b))
                    x = cols(K.X, b)
                    nc.vector.tensor_tensor(x, x, bt[:, u, 0], ALU.add).then_inc(ending.sem, 1)
                    dve.wait_ge(ending.sem, ending.next())

                software_pipeline(dve, prep, main)

            @block.scalar
            def _(act):
                for value, sem in loaded:
                    act.wait_ge(sem, value)

                def prep(b, u):
                    act.wait_ge(s["rT_ps"].sem, s["rT_ps"].after(b))
                    nc.scalar.activation(rT[:, u, :], K.PS[:, MISC, 0:S], ACT.Identity, scale=W["f1_norm2"][:, 0:1]).then_inc(s["rT"].sem, 1)
                    yield

                def main(b, u, stages):
                    for e in range(NE1):
                        act.wait_ge(s["up_a"].sem, s["up_a"].after(b, e + 1))
                        for c in range(2):
                            ins = nc.scalar.activation(hT[:, e % 2, c], K.PS[:, 2 * (e % 2), c * S:(c + 1) * S], ACT.Relu,
                                                       bias=W["f1_b1"][:, e * CE1 + c:e * CE1 + c + 1])
                        ins.then_inc(s["ha"].sem, 1)
                        if e == 2:
                            next_stage(stages)

                software_pipeline(act, prep, main)

            @block.tensor
            def _(pe):
                for value, sem in loaded:
                    pe.wait_ge(sem, value)

                def prep(b, u):
                    pe.wait_ge(s["rms"].sem, s["rms"].after(b))
                    for t in range(T):
                        mm = nc.tensor.transpose(K.PS[:, MISC, t * P:(t + 1) * P], rn[:, u, t], K.ident[:])
                    mm.then_inc(s["rT_ps"].sem, 1)
                    yield
                    pe.wait_ge(s["rT"].sem, s["rT"].after(b))
                    for t in range(T):
                        mm = nc.tensor.matmul(K.PS[:, MISC + 1, t * NE1:(t + 1) * NE1], rT[:, u, t * P:(t + 1) * P], W["f1_gate_w"][:],
                                              start=True, stop=True)
                    mm.then_inc(s["logits"].sem, 1)
                    yield

                def main(b, u, stages):
                    def up(e):
                        for c in range(CE1):
                            mm = nc.tensor.matmul(K.PS[:, 2 * (e % 2) + c // 2, (c % 2) * S:(c % 2 + 1) * S],
                                                  W["f1_w1"][:, (e * CE1 + c) * P:(e * CE1 + c + 1) * P], rT[:, u, :], start=True, stop=True)
                            if c % 2:
                                mm.then_inc(s["up_a" if c == 1 else "up_b"].sem, 1)

                    def down(e):
                        pe.wait_ge(s["ha"].sem, s["ha"].after(b, e + 1))
                        pe.wait_ge(s["hb"].sem, s["hb"].after(b, e + 1))
                        for t in range(T):
                            for c in range(CE1):
                                mm = nc.tensor.matmul(K.PS[:, OUT0 + e % 2, t * D:(t + 1) * D], hT[:, e % 2, c, t * P:(t + 1) * P],
                                                      W["f1_w2"][:, (e * CE1 + c) * D:(e * CE1 + c + 1) * D], start=c == 0, stop=c == CE1 - 1)
                        mm.then_inc(s["down_ps"].sem, 1)

                    for e in range(NE1):
                        up(e)
                        if e >= 2:
                            next_stage(stages)
                        if e >= 1:
                            down(e - 1)
                    down(NE1 - 1)

                software_pipeline(pe, prep, main)


def latent_moe_layer(K, W, loaded):
    latent_attention_layer(K, W, loaded)
    expert_layer(K, W, loaded)



NE2, HE2, K2 = 16, 64, 8
F2 = NE2 * HE2
HC2 = 512
F2C = F2 // P


def routed_ffn_layer(K, W, loaded, load_late):
    nc = K.nc
    s = ln_signals(K)
    s["pool_step"] = K.rising("pool_step", 1)
    s["prep_step"] = K.rising("vector_prep_step", LN_STEPS + 2 + 2 * T + 3)
    s["main_step"] = K.rising("vector_finish_step", T)
    per = dict(row_sum=1, row_r=1, logits=1, scores=1, weights=1, gu_ps=3 * T, g=3 * T, silu=3 * T, h=3 * T, hw=2 * T, hT_ps=3 * T, hT=3 * T, down_ps=1)
    for n, k in per.items():
        s[n] = K.rising("signal_" + n, k)
    tg = K.gates[:, 6:7]

    with ExitStack() as ctx:
        def sb(name, shape, dt=F32):
            return ctx.enter_context(nc.sbuf_tensor("f2_" + name, shape, dt))

        gsq, gss, gr, gn, gT = sb("gate_squares", [NE2, D]), sb("gate_sum", [NE2, 1]), sb("gate_r", [NE2, 1]), sb("gate_rows", [NE2, D]), sb("gateT", [P, NE2])
        sq, ss, rr = sb("squares", [P, T, D]), sb("square_sums", [P, 2, T]), sb("inverse_norms", [P, 2, T])
        sc, top, left, sel = sb("scores", [P, 2, T, NE2]), sb("top", [P, T, K2]), sb("left", [P, T, NE2]), sb("selected", [P, T, NE2])
        tot, wt = sb("top_sum", [P, T]), sb("weights", [P, 2, T, NE2])
        g, h = sb("gate", [P, 2, HC2]), sb("hidden", [P, 2, HC2])
        hT = sb("hiddenT", [P, 2, HC2])

        steps = [(t, c) for t in range(T) for c in range(3)]
        width = (HC2, HC2, HE2)

        with nc.Block() as block:

            @block.sync
            def _(sp):
                load_late(sp)

            @block.vector
            def _(dve):
                for value, sem in loaded:
                    dve.wait_ge(sem, value)
                setup = K.sem("f2_setup_step")
                nc.vector.tensor_tensor(gsq[:], W["f2_gate_w"][:], W["f2_gate_w"][:], ALU.mult).then_inc(setup, 1)
                dve.wait_ge(setup, 1)
                nc.vector.tensor_reduce(gss[:], gsq[:], AX_X, ALU.add).then_inc(setup, 1)
                dve.wait_ge(setup, 2)
                nc.vector.tensor_scalar(gss[:], gss[:], 1e-24, None, ALU.max).then_inc(setup, 1)
                dve.wait_ge(K.sem("f2_gate_norm"), 1)
                nc.vector.tensor_scalar(gn[:], W["f2_gate_w"][:], gr[:, 0:1], None, ALU.mult).then_inc(setup, 1)
                dve.wait_ge(K.sem("f2_gate_turned"), 1)
                nc.vector.tensor_copy(gT[:], K.PS[:, MISC, 0:NE2]).then_inc(setup, 1)
                chain, ending = Chain(s["prep_step"]), Chain(s["main_step"])

                def prep(b, u):
                    chain.start(b)
                    dve_ln_stats(K, dve, chain, s, b, u)
                    yield
                    dve_ln_rows(K, dve, chain, s, b, u)
                    y = K.norm["xn"][:, u]
                    dve.wait_ge(s["xn"].sem, s["xn"].after(b))
                    nc.vector.tensor_tensor(sq[:], y, y, ALU.mult).then_inc(chain.sem, 1)
                    dve.wait_ge(chain.sem, chain.next())
                    nc.vector.tensor_reduce(ss[:, u], sq[:], AX_X, ALU.add).then_inc(chain.sem, 1)
                    dve.wait_ge(chain.sem, chain.next())
                    nc.vector.tensor_scalar(ss[:, u], ss[:, u], 1e-24, None, ALU.max).then_inc(s["row_sum"].sem, 1)
                    yield
                    dve.wait_ge(s["scores"].sem, s["scores"].after(b))
                    settled(dve, K)
                    for t in range(T):
                        nc.vector.max(top[:, t], sc[:, u, t]).then_inc(chain.sem, 1)
                        chain.next()
                    dve.wait_ge(chain.sem, chain.reached())
                    settled(dve, K)
                    for t in range(T):
                        nc.vector.match_replace(left[:, t], top[:, t], sc[:, u, t], -1.0).then_inc(chain.sem, 1)
                        chain.next()
                    dve.wait_ge(chain.sem, chain.reached())
                    nc.vector.tensor_reduce(tot[:], top[:], AX_X, ALU.add).then_inc(chain.sem, 1)
                    chain.next()
                    nc.vector.scalar_tensor_tensor(sel[:], left[:], 0.0, sc[:, u], ALU.is_lt, ALU.mult).then_inc(chain.sem, 1)
                    dve.wait_ge(chain.sem, chain.next())
                    nc.vector.reciprocal(tot[:], tot[:]).then_inc(chain.sem, 1)
                    dve.wait_ge(chain.sem, chain.next())
                    nc.vector.tensor_tensor(wt[:, u], sel[:], tot[:].unsqueeze(2).broadcast_to([P, T, NE2]), ALU.mult).then_inc(s["weights"].sem, 1)
                    yield

                def main(b, u, stages):
                    ending.start(b)
                    for n, (t, c) in enumerate(steps):
                        w = width[c]
                        dve.wait_ge(s["g"].sem, s["g"].after(b, n + 1))
                        nc.vector.tensor_tensor(g[:, n % 2, 0:w], K.PS[:, 2 * (n % 2), 0:w], g[:, n % 2, 0:w], ALU.mult).then_inc(s["silu"].sem, 1)
                        dve.wait_ge(s["silu"].sem, s["silu"].after(b, n + 1))
                        nc.vector.tensor_tensor(h[:, n % 2, 0:w], K.PS[:, 2 * (n % 2) + 1, 0:w], g[:, n % 2, 0:w], ALU.mult).then_inc(s["h"].sem, 1)
                        if n in (0, 1, 5):
                            next_stage(stages)
                    dve.wait_ge(s["down_ps"].sem, s["down_ps"].after(b))
                    for t in range(T):
                        x = K.X[:, bass.ds(b * S + t * P, P)]
                        nc.vector.scalar_tensor_tensor(x, K.PS[:, OUT0, t * D:(t + 1) * D], tg, x, ALU.mult, ALU.add).then_inc(ending.sem, 1)
                        ending.next()
                    dve.wait_ge(ending.sem, ending.reached())

                software_pipeline(dve, prep, main)

            @block.gpsimd
            def _(pool):
                pool.wait_ge(K.sem("f2_setup_step"), 3)
                nc.gpsimd.tensor_tensor(gr[:], gss[:], K.neghalf[0:NE2, 0:1], ALU.pow).then_inc(K.sem("f2_gate_norm"), 1)

                def prep(b, u):
                    pool_rstd(K, pool, s, b, u)
                    pool.wait_ge(s["row_sum"].sem, s["row_sum"].after(b))
                    nc.gpsimd.tensor_tensor(rr[:, u], ss[:, u], K.neghalf[:, 0:T], ALU.pow).then_inc(s["row_r"].sem, 1)
                    yield

                def main(b, u, stages):
                    pool.wait_ge(s["weights"].sem, s["weights"].after(b))
                    for n, (t, c) in enumerate(steps):
                        if c == 2:
                            if t == 0:
                                all_stages(stages)
                            continue
                        pool.wait_ge(s["h"].sem, s["h"].after(b, n + 1))
                        hw = h[:, n % 2].rearrange("p (e j) -> p e j", j=HE2)
                        ne = HC2 // HE2
                        nc.gpsimd.tensor_tensor(hw, hw, wt[:, u, t, c * ne:(c + 1) * ne].unsqueeze(2).broadcast_to([P, ne, HE2]), ALU.mult) \
                            .then_inc(s["hw"].sem, 1)

                software_pipeline(pool, prep, main)

            @block.scalar
            def _(act):
                def prep(b, u):
                    act_xn_transposed(K, act, s, b, u, MISC + 1 - 2 * u)
                    yield
                    act.wait_ge(s["row_r"].sem, s["row_r"].after(b))
                    act.wait_ge(s["logits"].sem, s["logits"].after(b))
                    for t in range(T):
                        ins = nc.scalar.activation(sc[:, u, t], K.PS[:, MISC + 1 - 2 * u, S + t * NE2:S + (t + 1) * NE2], ACT.Sigmoid, scale=rr[:, u, t:t + 1])
                    ins.then_inc(s["scores"].sem, 1)
                    yield

                def main(b, u, stages):
                    def turned(n):
                        act.wait_ge(s["hT_ps"].sem, s["hT_ps"].after(b, n + 1))
                        w = width[steps[n][1]]
                        if w == HC2:
                            ins = nc.scalar.activation(hT[:, n % 2], K.PS[:, MISC, :], ACT.Copy)
                        else:
                            ins = nc.scalar.activation(hT[0:HE2, n % 2, 0:P], K.PS[0:HE2, MISC, 0:P], ACT.Copy)
                        ins.then_inc(s["hT"].sem, 1)

                    for n, (t, c) in enumerate(steps):
                        w = width[c]
                        act.wait_ge(s["gu_ps"].sem, s["gu_ps"].after(b, n + 1))
                        if n >= 2:
                            act.wait_ge(s["h"].sem, s["h"].after(b, n - 1))
                        nc.scalar.activation(g[:, n % 2, 0:w], K.PS[:, 2 * (n % 2), 0:w], ACT.Sigmoid).then_inc(s["g"].sem, 1)
                        if n >= 1:
                            turned(n - 1)
                        if n >= 4:
                            next_stage(stages)
                    turned(len(steps) - 1)

                software_pipeline(act, prep, main)

            @block.tensor
            def _(pe):
                pe.wait_ge(K.sem("f2_setup_step"), 4)
                nc.tensor.transpose(K.PS[:, MISC, 0:NE2], gn[:], K.ident[0:NE2, 0:NE2]).then_inc(K.sem("f2_gate_turned"), 1)
                pe.wait_ge(K.sem("f2_setup_step"), 5)

                def prep(b, u):
                    bank = MISC + 1 - 2 * u
                    pe_xn_transposed(K, pe, s, b, u, bank)
                    yield
                    pe.wait_ge(s["xnT"].sem, s["xnT"].after(b))
                    for t in range(T):
                        mm = nc.tensor.matmul(K.PS[:, bank, S + t * NE2:S + (t + 1) * NE2], K.norm["xnT"][:, u, t * P:(t + 1) * P], gT[:], start=True, stop=True)
                    mm.then_inc(s["logits"].sem, 1)
                    yield

                def main(b, u, stages):
                    def up(n):
                        t, c = steps[n]
                        w = width[c]
                        for k, name in enumerate(("f2_wg", "f2_wu")):
                            mm = nc.tensor.matmul(K.PS[:, 2 * (n % 2) + k, 0:w], K.norm["xnT"][:, u, t * P:(t + 1) * P], W[name][:, c * HC2:c * HC2 + w],
                                                  start=True, stop=True)
                        mm.then_inc(s["gu_ps"].sem, 1)

                    def turn(n):
                        t, c = steps[n]
                        if n >= 1:
                            pe.wait_ge(s["hT"].sem, s["hT"].after(b, n))
                        if c < 2:
                            pe.wait_ge(s["hw"].sem, s["hw"].after(b, 2 * t + c + 1))
                            for k in range(HC2 // P):
                                mm = nc.tensor.transpose(K.PS[:, MISC, k * P:(k + 1) * P], h[:, n % 2, k * P:(k + 1) * P], K.ident[:])
                        else:
                            pe.wait_ge(s["h"].sem, s["h"].after(b, n + 1))
                            settled(pe, K)
                            mm = nc.tensor.transpose(K.PS[0:HE2, MISC, 0:P], h[:, n % 2, 0:HE2], K.ident[:])
                        mm.then_inc(s["hT_ps"].sem, 1)

                    def down(n):
                        t, c = steps[n]
                        pe.wait_ge(s["hT"].sem, s["hT"].after(b, n + 1))
                        out = K.PS[:, OUT0, t * D:(t + 1) * D]
                        if c < 2:
                            for k in range(HC2 // P):
                                mm = nc.tensor.matmul(out, hT[:, n % 2, k * P:(k + 1) * P], W["f2_wd"][:, (4 * c + k) * D:(4 * c + k + 1) * D],
                                                      start=c == 0 and k == 0, stop=False)
                        else:
                            mm = nc.tensor.matmul(out, hT[0:HE2, n % 2, 0:P], W["f2_sd"][:], start=False, stop=True)
                        return mm

                    for n in range(len(steps)):
                        up(n)
                        if n >= 4:
                            next_stage(stages)
                        if n >= 1:
                            turn(n - 1)
                        if n >= 2:
                            down(n - 2)
                    down(len(steps) - 2)
                    turn(len(steps) - 1)
                    down(len(steps) - 1).then_inc(s["down_ps"].sem, 1)

                software_pipeline(pe, prep, main)



H3, DH3 = 2, 64
KT3 = 2 * T
V3 = DH3 + 1
U3 = 4
MISC3 = 7
LATENTS_PE_STAGES, LATENTS_ACT_STAGES = (0, 1, 3), (0, 1, 3)


def perceiver_attention_layer(K, W, loaded):
    nc = K.nc
    s = ln_signals(K, turned=False)
    s["pool_step"] = K.rising("pool_step", 3)
    s["rows_step"] = K.rising("vector_rows_step", LN_STEPS + 4 + 4)
    s["prep_step"] = K.rising("vector_prep_step", 1 + 1 + 3)
    s["finish_step"] = K.rising("vector_finish_step", 1 + 1)
    per = dict(c_stats=1, c_rstd=1, c_rows=1, z_stats=1, z_rstd=1, z=1, sq=1, ssq=1, r=1, q_rows=1, k_rows=1, filled=MISC3, read=MISC3,
               smax_ps=U3, smax=U3, m=1, mT_ps=1, mT=1, st_ps=U3, p=U3, mix=1, o=1, oT_ps=1, oT=1, wo_ps=1, out_banks=1, hide=1)
    for n, k in per.items():
        s[n] = K.rising("signal_" + n, k)
    tg = K.gates[:, 3:4]

    with ExitStack() as ctx:
        def sb(name, shape, dt=F32):
            return ctx.enter_context(nc.sbuf_tensor("x3_" + name, shape, dt))

        qk = sb("qk_gain", [P, 1])
        cst, cmv, cve, crs = sb("c_stats", [P, T, 6]), sb("c_mean_var", [P, 2, T, 2]), sb("c_var_eps", [P, T]), sb("c_rstd", [P, 2, T])
        cn, cnT = sb("c_rows", [P, 2, T, C]), sb("cT", [C, 2, S])
        zst, zmv, zve, zrs = sb("z_stats", [P, T, 6]), sb("z_mean_var", [P, 2, T, 2]), sb("z_var_eps", [P, T]), sb("z_rstd", [P, 2, T])
        z, zT = sb("latent_rows", [P, 2, T, D]), sb("latentT", [P, 2, S])
        raw, sq = sb("raw", [P, 3, T, D]), sb("sq", [P, 3, T, D])
        ssq, rn = sb("sum_squares", [P, 2, 3, T, H3]), sb("inverse_norms", [P, 2, 3, T, H3])
        qn, kn = sb("q_rows", [P, T, H3, P]), sb("k_rows", [P, KT3, P])
        ve = sb("v_with_one", [P, 2, KT3, H3, V3])
        qT, kT = sb("qT", [P, 2, H3, S]), sb("kT", [P, 2, KT3 * P])
        nm, nrest = sb("minus_max", [P, 2, T, H3]), sb("rest", [P, T, H3])
        mtok, mT = sb("max_rows", [P, T, P], BF16), sb("maxT", [P, 2, S], BF16)
        hide = sb("hide_keys", [P, 2, T])
        p = sb("probs", [P, 2, 2, S])
        rec, o, oT = sb("inverse_sums", [P, T, H3]), sb("out_rows", [P, 2, T, H3, DH3]), sb("outT", [P, S])

        with nc.Block() as block:

            @block.vector
            def _(dve):
                nc.vector.memset(qn[:], 0.0)
                nc.vector.memset(mtok[:], 0.0)
                nc.vector.memset(ve[:, :, :, :, DH3:V3], 1.0)
                for value, sem in loaded:
                    dve.wait_ge(sem, value)
                setup = K.sem("x3_setup_step")
                nc.vector.tensor_tensor(qk[:], W["x3_qg"][:], W["x3_kg"][:], ALU.mult).then_inc(setup, 1)
                dve.wait_ge(setup, 1)
                nc.vector.tensor_scalar(qk[:], qk[:], DH3 ** -0.5, None, ALU.mult).then_inc(setup, 1)
                nc.vector.tensor_scalar(K.hide_cols[:], K.mask_k3c[:], 1.0, -HIDE, ALU.subtract, ALU.mult).then_inc(setup, 1)
                nc.vector.tensor_scalar(K.hide_rows[:], K.mask_k3[:], 1.0, -HIDE, ALU.subtract, ALU.mult).then_inc(setup, 1)
                dve.wait_ge(setup, 4)
                chain, row_chain, ending = Chain(s["prep_step"]), Chain(s["rows_step"]), Chain(s["finish_step"])

                def stats(b, u, st, mv, rows, signal):
                    settled(dve, K)
                    for t in range(T):
                        nc.vector.bn_stats(st[:, t], rows(t)).then_inc(row_chain.sem, 1)
                        row_chain.next()
                    dve.wait_ge(row_chain.sem, row_chain.reached())
                    settled(dve, K)
                    nc.vector.bn_aggr(mv[:, u, 0], st[:, 0]).then_inc(row_chain.sem, 1)
                    row_chain.next()
                    nc.vector.bn_aggr(mv[:, u, 1], st[:, 1]).then_inc(signal.sem, 1)

                def normalise(b, u, dst, rows, mv, rs, rstd, signal):
                    dve.wait_ge(rstd.sem, rstd.after(b))
                    nc.vector.tensor_scalar(dst[:, u, 0], rows(0), mv[:, u, 0, 0:1], rs[:, u, 0:1], ALU.subtract, ALU.mult).then_inc(row_chain.sem, 1)
                    row_chain.next()
                    nc.vector.tensor_scalar(dst[:, u, 1], rows(1), mv[:, u, 1, 0:1], rs[:, u, 1:2], ALU.subtract, ALU.mult).then_inc(signal.sem, 1)

                def rows(b, u):
                    for _ in row_stages(b, u):
                        pass

                def row_stages(b, u):
                    row_chain.start(b)
                    c_rows = lambda t: K.ctx_rows[:, bass.ds(b * (T * C) + t * C, C)]
                    stats(b, u, cst, cmv, c_rows, s["c_stats"])
                    dve_ln_stats(K, dve, row_chain, s, b, u)
                    yield
                    normalise(b, u, cn, c_rows, cmv, crs, s["c_rstd"], s["c_rows"])
                    dve_ln_rows(K, dve, row_chain, s, b, u)
                    dve.wait_ge(s["xn"].sem, s["xn"].after(b))
                    y = lambda t: K.norm["xn"][:, u, t]
                    stats(b, u, zst, zmv, y, s["z_stats"])
                    yield
                    normalise(b, u, z, y, zmv, zrs, s["z_rstd"], s["z"])
                    yield

                def prep(b, u):
                    chain.start(b)
                    dve.wait_ge(s["sq"].sem, s["sq"].after(b))
                    nc.vector.tensor_reduce(ssq[:, u].rearrange("p k t h -> p (k t h)"), sq[:].rearrange("p k t (h e) -> p (k t h) e", e=DH3), AX_X, ALU.add).then_inc(chain.sem, 1)
                    dve.wait_ge(chain.sem, chain.next())
                    nc.vector.tensor_scalar(ssq[:, u], ssq[:, u], 1.0 / DH3, 1e-16, ALU.mult, ALU.max).then_inc(s["ssq"].sem, 1)
                    dve.wait_ge(s["r"].sem, s["r"].after(b))
                    nc.vector.tensor_tensor(kn[:].rearrange("p k (h e) -> p (k h) e", e=DH3), raw[:, 1:3].rearrange("p k t (h e) -> p (k t h) e", e=DH3),
                                            rn[:, u, 1:3].rearrange("p k t h -> p (k t h)").unsqueeze(2).broadcast_to([P, KT3 * H3, DH3]), ALU.mult) \
                        .then_inc(s["k_rows"].sem, 1)
                    for hd in range(H3):
                        es = slice(hd * DH3, (hd + 1) * DH3)
                        ins = nc.vector.tensor_tensor(qn[:, :, hd, es], raw[:, 0, :, es], rn[:, u, 0, :, hd:hd + 1].broadcast_to([P, T, DH3]), ALU.mult)
                        if hd == 0:
                            ins.then_inc(chain.sem, 1)
                            chain.next()
                    ins.then_inc(s["q_rows"].sem, 1)
                    yield

                def row_max(b, u, i):
                    dve.wait_ge(s["smax_ps"].sem, s["smax_ps"].after(b, i + 1))
                    nc.vector.tensor_reduce(nm[:, u, i % 2, i // 2:i // 2 + 1], K.PS[:, SMAX0 + i % 2, :], AX_X, ALU.max, negate=True) \
                        .then_inc(s["smax"].sem, 1)

                def place_max(b, u):
                    m = mtok[:, :, 0:3 * H3].rearrange("p t (h i) -> p t h i", i=3)
                    dve.wait_ge(s["smax"].sem, s["smax"].after(b))
                    nc.vector.tensor_copy(m[:, :, :, 0], nm[:, u]).then_inc(chain.sem, 1)
                    dve.wait_ge(chain.sem, chain.next())
                    nc.vector.tensor_tensor(nrest[:], nm[:, u], m[:, :, :, 0], ALU.subtract).then_inc(chain.sem, 1)
                    dve.wait_ge(chain.sem, chain.next())
                    nc.vector.tensor_copy(m[:, :, :, 1], nrest[:]).then_inc(chain.sem, 1)
                    dve.wait_ge(chain.sem, chain.next())
                    nc.vector.tensor_tensor(m[:, :, :, 2], nrest[:], m[:, :, :, 1], ALU.subtract).then_inc(s["m"].sem, 1)

                def first(b, u, later=None):
                    for i in range(U3):
                        row_max(b, u, i)
                        if later and i < 3:
                            next(later)
                    place_max(b, u)

                def fused(b, u, stages, ahead):
                    all_stages(stages)
                    ending.start(b)
                    dve.wait_ge(s["mix"].sem, s["mix"].after(b))
                    ob = K.PS[:, OUT0:OUT0 + T, 0:H3 * V3].rearrange("p t (h e) -> p t h e", e=V3)
                    nc.vector.reciprocal(rec[:], ob[:, :, :, DH3]).then_inc(ending.sem, 1)
                    dve.wait_ge(ending.sem, ending.next())
                    nc.vector.tensor_tensor(o[:, u], ob[:, :, :, 0:DH3], rec[:].unsqueeze(3).broadcast_to([P, T, H3, DH3]), ALU.mult).then_inc(s["o"].sem, 1)
                    if stages:
                        first(b + 1, 1 - u, row_stages(b + 2, u) if ahead else None)

                def finish(b, u):
                    dve.wait_ge(s["wo_ps"].sem, s["wo_ps"].after(b))
                    o3 = o[:, u].rearrange("p t h e -> p t (h e)")
                    nc.vector.tensor_tensor(o3, K.PS[:, OUT0 + 1, 0:S].rearrange("p (t d) -> p t d", t=T),
                                            W["x3_bo"][:].unsqueeze(1).broadcast_to([P, T, D]), ALU.add).then_inc(s["out_banks"].sem, 1)
                    dve.wait_ge(s["out_banks"].sem, s["out_banks"].after(b))
                    x = cols(K.X, b)
                    nc.vector.scalar_tensor_tensor(x, o[:, u].rearrange("p t h e -> p (t h e)"), tg, x, ALU.mult, ALU.add).then_inc(ending.sem, 1)
                    dve.wait_ge(ending.sem, ending.next())

                head_pipeline(dve, prep, fused, first, finish, rows)

            @block.gpsimd
            def _(pool):
                pool.wait_ge(K.sem("x3_setup_step"), 3)
                ps = s["pool_step"]

                def rstd(b, u, k, stats, mv, ve_, rs, signal):
                    pool.wait_ge(stats.sem, stats.after(b))
                    nc.gpsimd.tensor_tensor(ve_[:], mv[:, u, :, 1], K.eps5[:, 0:T], ALU.add).then_inc(ps.sem, 1)
                    pool.wait_ge(ps.sem, ps.after(b, k))
                    nc.gpsimd.tensor_tensor(rs[:, u], ve_[:], K.neghalf[:, 0:T], ALU.pow).then_inc(signal.sem, 1)

                def rows(b, u):
                    rstd(b, u, 1, s["c_stats"], cmv, cve, crs, s["c_rstd"])
                    pool.wait_ge(s["stats"].sem, s["stats"].after(b))
                    n = K.norm
                    nc.gpsimd.tensor_tensor(n["ve"][:, u, :], n["mv"][:, u, :, 1], K.eps5[:, 0:T], ALU.add).then_inc(ps.sem, 1)
                    pool.wait_ge(ps.sem, ps.after(b, 2))
                    nc.gpsimd.tensor_tensor(n["rs"][:, u, :], n["ve"][:, u, :], K.neghalf[:, 0:T], ALU.pow).then_inc(s["rstd"].sem, 1)
                    rstd(b, u, 3, s["z_stats"], zmv, zve, zrs, s["z_rstd"])

                def prep(b, u):
                    nc.gpsimd.tensor_copy(hide[:, u, :], K.hide_cols[:, bass.ds(b * T, T)]).then_inc(s["hide"].sem, 1)
                    pool.wait_ge(s["ssq"].sem, s["ssq"].after(b))
                    nc.gpsimd.tensor_tensor(rn[:, u].rearrange("p k t h -> p (k t h)"), ssq[:, u].rearrange("p k t h -> p (k t h)"),
                                            K.neghalf[:, 0:1].broadcast_to([P, 3 * T * H3]), ALU.pow).then_inc(s["r"].sem, 1)
                    yield

                def fused(b, u, stages, ahead):
                    all_stages(stages)
                    if ahead:
                        rows(b + 2, u)

                head_pipeline(pool, prep, fused, nothing, nothing, rows)

            @block.scalar
            def _(act):
                for value, sem in loaded:
                    act.wait_ge(sem, value)
                act.wait_ge(K.sem("x3_setup_step"), 2)

                def bank_of(b, u, f):
                    act.wait_ge(s["filled"].sem, s["filled"].after(b, f + 1))
                    return K.PS[:, MISC + (u + f) % 2, :]

                def prep(b, u):
                    read = s["read"].sem
                    nc.scalar.activation(cnT[:, u], bank_of(b, u, 0)[0:C, 0:S], ACT.Identity, scale=W["x3_lx_g"][:, 0:1], bias=W["x3_lx_b"][:, 0:1]).then_inc(read, 1)
                    nc.scalar.activation(zT[:, u], bank_of(b, u, 1)[:, 0:S], ACT.Identity, scale=W["x3_ll_g"][:, 0:1], bias=W["x3_ll_b"][:, 0:1]).then_inc(read, 1)
                    yield
                    bank = bank_of(b, u, 2)[:, :].rearrange("p (t n) -> p t n", t=T)
                    nc.scalar.activation(raw[:, 1], bank[:, :, 0:D], ACT.Copy)
                    nc.scalar.activation(sq[:, 1], bank[:, :, 0:D], ACT.Square)
                    nc.scalar.activation(ve[:, u, 0:T, :, 0:DH3], bank[:, :, D:2 * D].rearrange("p t (h e) -> p t h e", e=DH3), ACT.Copy).then_inc(read, 1)
                    for t in range(T):
                        bank = bank_of(b, u, 3 + t)
                        nc.scalar.activation(raw[:, 0::2, t], bank[:, 0:2 * D].rearrange("p (k d) -> p k d", k=2), ACT.Copy)
                        ins = nc.scalar.activation(sq[:, 0::2, t], bank[:, 0:2 * D].rearrange("p (k d) -> p k d", k=2), ACT.Square)
                        if t == T - 1:
                            ins.then_inc(s["sq"].sem, 1)
                        nc.scalar.activation(ve[:, u, T + t, :, 0:DH3], bank[:, 2 * D:3 * D].rearrange("p (h e) -> p h e", e=DH3), ACT.Copy).then_inc(read, 1)
                    yield
                    nc.scalar.activation(kT[:, u], bank_of(b, u, 5), ACT.Copy).then_inc(read, 1)
                    nc.scalar.activation(qT[:, u].rearrange("p h n -> p (h n)"), bank_of(b, u, 6), ACT.Identity, scale=qk[:, 0:1]).then_inc(read, 1)
                    yield

                def maxima(b, u):
                    act.wait_ge(s["mT_ps"].sem, s["mT_ps"].after(b))
                    nc.scalar.activation(mT[:, u], K.PS[:, SMAX0, 0:P].bitcast(BF16), ACT.Copy).then_inc(s["mT"].sem, 1)

                def fused(b, u, stages, ahead):
                    act.wait_ge(s["hide"].sem, s["hide"].after(b))
                    for i in range(U3):
                        act.wait_ge(s["st_ps"].sem, s["st_ps"].after(b, i + 1))
                        bank = K.PS[:, ST0 + i % 2, :]
                        if i % 2 == 0:
                            for kt in range(2):
                                ins = nc.scalar.activation(p[:, 0, kt], bank[:, kt * S:(kt + 1) * S], ACT.Exp, bias=hide[:, u, kt:kt + 1])
                        else:
                            ins = nc.scalar.activation(p[:, 1].rearrange("p k n -> p (k n)"), bank, ACT.Exp)
                        ins.then_inc(s["p"].sem, 1)
                        if stages and i in LATENTS_ACT_STAGES:
                            next(stages)
                    act.wait_ge(s["oT_ps"].sem, s["oT_ps"].after(b))
                    nc.scalar.activation(oT[:], K.PS[:, OUT0, 0:S], ACT.Copy).then_inc(s["oT"].sem, 1)
                    if stages:
                        maxima(b + 1, 1 - u)

                head_pipeline(act, prep, fused, maxima, nothing)

            @block.tensor
            def _(pe):
                for value, sem in loaded:
                    pe.wait_ge(sem, value)
                pe.wait_ge(K.sem("x3_setup_step"), 4)

                def bank_for(b, u, f):
                    pe.wait_ge(s["read"].sem, b * MISC3 + (s["read"].base + f - 1))
                    return K.PS[:, MISC + (u + f) % 2, :]

                def prep(b, u):
                    filled = s["filled"].sem
                    pe.wait_ge(s["c_rows"].sem, s["c_rows"].after(b))
                    bank = bank_for(b, u, 0)
                    for t in range(T):
                        mm = nc.tensor.transpose(bank[0:C, t * P:(t + 1) * P], cn[:, u, t], K.ident[:])
                    mm.then_inc(filled, 1)
                    pe.wait_ge(s["z"].sem, s["z"].after(b))
                    bank = bank_for(b, u, 1)
                    for t in range(T):
                        mm = nc.tensor.transpose(bank[:, t * P:(t + 1) * P], z[:, u, t], K.ident[:])
                    mm.then_inc(filled, 1)
                    yield
                    pe.wait_ge(s["read"].sem, s["read"].after(b, 2))
                    bank = bank_for(b, u, 2)
                    for t in range(T):
                        mm = nc.tensor.matmul(bank[:, t * 2 * D:(t + 1) * 2 * D], cnT[:, u, t * P:(t + 1) * P], W["x3_wkv"][:], start=True, stop=True)
                    mm.then_inc(filled, 1)
                    for t in range(T):
                        bank = bank_for(b, u, 3 + t)
                        nc.tensor.matmul(bank[:, 0:3 * D], zT[:, u, t * P:(t + 1) * P], W["x3_wql"][:], start=True, stop=True).then_inc(filled, 1)
                    yield
                    pe.wait_ge(s["k_rows"].sem, s["k_rows"].after(b))
                    bank = bank_for(b, u, 5)
                    for kt in range(KT3):
                        mm = nc.tensor.transpose(bank[:, kt * P:(kt + 1) * P], kn[:, kt], K.ident[:])
                    mm.then_inc(filled, 1)
                    pe.wait_ge(s["q_rows"].sem, s["q_rows"].after(b))
                    bank = bank_for(b, u, 6)
                    for hd in range(H3):
                        for t in range(T):
                            mm = nc.tensor.transpose(bank[:, hd * S + t * P:hd * S + (t + 1) * P], qn[:, t, hd], K.ident[:])
                    mm.then_inc(filled, 1)
                    yield

                def scores(b, u, i):
                    n, t = i // 2, i % 2
                    if i == 0:
                        pe.wait_ge(s["read"].sem, s["read"].after(b))
                    if i >= 2:
                        pe.wait_ge(s["smax"].sem, s["smax"].after(b, i - 1))
                    bank = K.PS[:, SMAX0 + i % 2, :]
                    nc.tensor.matmul(bank[:, 0:S], K.identb[:], K.hide_rows[:, bass.ds(b * S, S)], start=True, stop=True)
                    nc.tensor.matmul(bank, qT[:, u, n, t * P:(t + 1) * P], kT[:, u, :], start=False, stop=True, skip_group_check=True) \
                        .then_inc(s["smax_ps"].sem, 1)

                def turn_max(b, u):
                    pe.wait_ge(s["m"].sem, s["m"].after(b))
                    for t in range(T):
                        mm = nc.tensor.transpose(K.PS[:, SMAX0, :].bitcast(BF16)[:, t * P:(t + 1) * P], mtok[:, t], K.identb[:])
                    mm.then_inc(s["mT_ps"].sem, 1)

                def scores_T(b, u, i):
                    n, half = i // 2, i % 2
                    if i == 0:
                        pe.wait_ge(s["mT"].sem, s["mT"].after(b))
                    for k in range(2):
                        kt = 2 * half + k
                        o_ = K.PS[:, ST0 + i % 2, k * S:(k + 1) * S]
                        nc.tensor.matmul(o_, kT[:, u, kt * P:(kt + 1) * P], qT[:, u, n, :], start=True, stop=False)
                        mm = nc.tensor.matmul(o_, K.pick_max[:, n, :], mT[:, u], start=False, stop=True)
                    mm.then_inc(s["st_ps"].sem, 1)

                def mix(b, u, i):
                    n, half = i // 2, i % 2
                    if i == 0:
                        pe.wait_ge(s["out_banks"].sem, s["out_banks"].before(b))
                    pe.wait_ge(s["p"].sem, s["p"].after(b, i + 1))
                    for t in range(T):
                        for k in range(2):
                            mm = nc.tensor.matmul(K.PS[:, OUT0 + t, n * V3:(n + 1) * V3], p[:, i % 2, k, t * P:(t + 1) * P], ve[:, u, 2 * half + k, n, :],
                                                  start=half == 0 and k == 0, stop=half == 1 and k == 1)
                    if i == U3 - 1:
                        mm.then_inc(s["mix"].sem, 1)

                def first(b, u):
                    for i in range(U3):
                        scores(b, u, i)
                    turn_max(b, u)

                def turn_out(b, u):
                    pe.wait_ge(s["o"].sem, s["o"].after(b))
                    for t in range(T):
                        mm = nc.tensor.transpose(K.PS[:, OUT0, t * P:(t + 1) * P], o[:, u, t].rearrange("p h e -> p (h e)"), K.ident[:])
                    mm.then_inc(s["oT_ps"].sem, 1)

                def fused(b, u, stages, ahead):
                    for i in range(U3):
                        scores_T(b, u, i)
                        if stages and i in LATENTS_PE_STAGES:
                            next(stages)
                        if i >= 1:
                            mix(b, u, i - 1)
                    mix(b, u, U3 - 1)
                    if stages:
                        for i in range(U3):
                            scores(b + 1, 1 - u, i)
                    turn_out(b, u)
                    if stages:
                        turn_max(b + 1, 1 - u)

                def finish(b, u):
                    pe.wait_ge(s["oT"].sem, s["oT"].after(b))
                    for t in range(T):
                        mm = nc.tensor.matmul(K.PS[:, OUT0 + 1, t * D:(t + 1) * D], oT[:, t * P:(t + 1) * P], W["x3_wo"][:], start=True, stop=True)
                    mm.then_inc(s["wo_ps"].sem, 1)

                head_pipeline(pe, prep, fused, first, finish)



NE3, HE3, K3 = 8, 256, 2
CE3 = HE3 // P


def top2_moe_layer(K, W, loaded):
    nc = K.nc
    s = ln_signals(K)
    s["pool_step"] = K.rising("pool_step", 1)
    s["prep_step"] = K.rising("vector_prep_step", LN_STEPS + 3 + T + 3 + 6 + 3)
    s["main_step"] = K.rising("vector_finish_step", NE3 * T)
    per = dict(logits=1, minus_max=1, e=1, weights=1, gu_ps=NE3, g=NE3, h=NE3, down_ps=NE3)
    for n, k in per.items():
        s[n] = K.rising("signal_" + n, k)
    tg = K.gates[:, 7:8]

    with ExitStack() as ctx:
        def sb(name, shape, dt=F32):
            return ctx.enter_context(nc.sbuf_tensor("f3_" + name, shape, dt))

        nm, e_, tot = sb("minus_max", [P, 2, T]), sb("exps", [P, 2, T, NE3]), sb("sums", [P, T])
        sc, top = sb("scores", [P, T, NE3]), sb("top", [P, T, 8])
        gt, eq, ca, cb, ngt = (sb(n, [P, T, NE3]) for n in ("greater", "equal", "count_a", "count_b", "n_greater_pad"))
        wt = sb("weights", [P, 2, T, NE3])
        g, hT = sb("gate", [P, 2, 2 * S]), sb("hiddenT", [P, 2, CE3, S])

        with nc.Block() as block:

            @block.vector
            def _(dve):
                chain, ending = Chain(s["prep_step"]), Chain(s["main_step"])

                def prep(b, u):
                    chain.start(b)
                    dve_ln_stats(K, dve, chain, s, b, u)
                    yield
                    dve_ln_rows(K, dve, chain, s, b, u)
                    yield
                    dve.wait_ge(s["logits"].sem, s["logits"].after(b))
                    lg = K.PS[:, MISC + u, S:S + T * NE3].rearrange("p (t e) -> p t e", t=T)
                    nc.vector.tensor_reduce(nm[:, u], lg, AX_X, ALU.max, negate=True).then_inc(s["minus_max"].sem, 1)
                    yield
                    dve.wait_ge(s["e"].sem, s["e"].after(b))
                    nc.vector.tensor_reduce(tot[:], e_[:, u], AX_X, ALU.add).then_inc(chain.sem, 1)
                    dve.wait_ge(chain.sem, chain.next())
                    nc.vector.reciprocal(tot[:], tot[:]).then_inc(chain.sem, 1)
                    dve.wait_ge(chain.sem, chain.next())
                    last = nc.vector.tensor_tensor(sc[:], e_[:, u], tot[:].unsqueeze(2).broadcast_to([P, T, NE3]), ALU.mult)
                    last.then_inc(chain.sem, 1)
                    dve.wait_ge(chain.sem, chain.next())
                    settled(dve, K)
                    for t in range(T):
                        nc.vector.max(top[:, t], sc[:, t]).then_inc(chain.sem, 1)
                        chain.next()
                    dve.wait_ge(chain.sem, chain.reached())
                    second = top[:, :, 1:2].broadcast_to([P, T, NE3])
                    nc.vector.tensor_tensor(gt[:], sc[:], second, ALU.is_gt).then_inc(chain.sem, 1)
                    chain.next()
                    nc.vector.tensor_tensor(eq[:], sc[:], second, ALU.is_equal).then_inc(chain.sem, 1)
                    dve.wait_ge(chain.sem, chain.next())
                    nc.vector.tensor_reduce(ngt[:, :, 0], gt[:], AX_X, ALU.add).then_inc(chain.sem, 1)
                    dve.wait_ge(chain.sem, chain.next())
                    src = eq
                    for sh, dst in ((1, ca), (2, cb), (4, ca)):
                        nc.vector.tensor_copy(dst[:, :, 0:sh], src[:, :, 0:sh]).then_inc(chain.sem, 1)
                        chain.next()
                        nc.vector.tensor_tensor(dst[:, :, sh:], src[:, :, sh:], src[:, :, 0:NE3 - sh], ALU.add).then_inc(chain.sem, 1)
                        dve.wait_ge(chain.sem, chain.next())
                        src = dst
                    nc.vector.tensor_tensor(ca[:], ca[:], ngt[:, :, 0:1].broadcast_to([P, T, NE3]), ALU.add).then_inc(chain.sem, 1)
                    dve.wait_ge(chain.sem, chain.next())
                    nc.vector.scalar_tensor_tensor(eq[:], ca[:], float(K3), eq[:], ALU.is_le, ALU.mult).then_inc(chain.sem, 1)
                    dve.wait_ge(chain.sem, chain.next())
                    nc.vector.tensor_tensor(gt[:], gt[:], eq[:], ALU.add).then_inc(chain.sem, 1)
                    dve.wait_ge(chain.sem, chain.next())
                    nc.vector.scalar_tensor_tensor(wt[:, u], gt[:], tg, sc[:], ALU.mult, ALU.mult).then_inc(s["weights"].sem, 1)
                    dve.wait_ge(s["weights"].sem, s["weights"].after(b))
                    yield

                def main(b, u, stages):
                    ending.start(b)

                    def add_expert(e):
                        dve.wait_ge(s["down_ps"].sem, s["down_ps"].after(b, e + 1))
                        if e > 0:
                            dve.wait_ge(ending.sem, ending.reached())
                        for t in range(T):
                            x = K.X[:, bass.ds(b * S + t * P, P)]
                            nc.vector.scalar_tensor_tensor(x, K.PS[:, OUT0 + e % 2, t * D:(t + 1) * D], wt[:, u, t, e:e + 1], x, ALU.mult, ALU.add).then_inc(ending.sem, 1)
                            ending.next()

                    for e in range(NE3):
                        dve.wait_ge(s["g"].sem, s["g"].after(b, e + 1))
                        nc.vector.tensor_tensor(hT[:, e % 2].rearrange("p c n -> p (c n)"), K.PS[:, 2 * (e % 2) + 1, :], g[:, e % 2], ALU.mult) \
                            .then_inc(s["h"].sem, 1)
                        if e >= 1:
                            add_expert(e - 1)
                        if e in (0, 1, 4):
                            next_stage(stages)
                    add_expert(NE3 - 1)
                    dve.wait_ge(ending.sem, ending.reached())
                    next_stage(stages)

                software_pipeline(dve, prep, main)

            @block.gpsimd
            def _(pool):
                def prep(b, u):
                    pool_rstd(K, pool, s, b, u)
                    yield

                software_pipeline(pool, prep, lambda b, u, stages: all_stages(stages))

            @block.scalar
            def _(act):
                def prep(b, u):
                    act_xn_transposed(K, act, s, b, u, MISC + u)
                    yield
                    act.wait_ge(s["minus_max"].sem, s["minus_max"].after(b))
                    for t in range(T):
                        ins = nc.scalar.activation(e_[:, u, t], K.PS[:, MISC + u, S + t * NE3:S + (t + 1) * NE3], ACT.Exp, bias=nm[:, u, t:t + 1])
                    ins.then_inc(s["e"].sem, 1)
                    yield

                def main(b, u, stages):
                    for e in range(NE3):
                        act.wait_ge(s["gu_ps"].sem, s["gu_ps"].after(b, e + 1))
                        nc.scalar.activation(g[:, e % 2], K.PS[:, 2 * (e % 2), :], ACT.Silu).then_inc(s["g"].sem, 1)
                        if e in (2, 7):
                            next_stage(stages)

                software_pipeline(act, prep, main)

            @block.tensor
            def _(pe):
                for value, sem in loaded:
                    pe.wait_ge(sem, value)

                def prep(b, u):
                    pe_xn_transposed(K, pe, s, b, u, MISC + u)
                    yield
                    pe.wait_ge(s["xnT"].sem, s["xnT"].after(b))
                    for t in range(T):
                        mm = nc.tensor.matmul(K.PS[:, MISC + u, S + t * NE3:S + (t + 1) * NE3], K.norm["xnT"][:, u, t * P:(t + 1) * P], W["f3_gate_w"][:],
                                              start=True, stop=True)
                    mm.then_inc(s["logits"].sem, 1)
                    yield

                def main(b, u, stages):
                    def up(e):
                        for k, name in enumerate(("f3_w1", "f3_w3")):
                            for c in range(CE3):
                                mm = nc.tensor.matmul(K.PS[:, 2 * (e % 2) + k, c * S:(c + 1) * S], W[name][:, e * HE3 + c * P:e * HE3 + (c + 1) * P],
                                                      K.norm["xnT"][:, u, :], start=True, stop=True)
                        mm.then_inc(s["gu_ps"].sem, 1)

                    def down(e):
                        pe.wait_ge(s["h"].sem, s["h"].after(b, e + 1))
                        for t in range(T):
                            for c in range(CE3):
                                mm = nc.tensor.matmul(K.PS[:, OUT0 + e % 2, t * D:(t + 1) * D], hT[:, e % 2, c, t * P:(t + 1) * P],
                                                      W["f3_w2"][:, (e * CE3 + c) * D:(e * CE3 + c + 1) * D], start=c == 0, stop=c == CE3 - 1)
                        mm.then_inc(s["down_ps"].sem, 1)

                    for e in range(NE3):
                        up(e)
                        if e in (2, 3):
                            next_stage(stages)
                        if e >= 1:
                            down(e - 1)
                    down(NE3 - 1)

                software_pipeline(pe, prep, main)



def build(nc, a, out):
    with ExitStack() as ctx:
        K = Core(nc, ctx, a)
        K.X = K.sb("x_resident", [P, B * S])
        K.ident = K.sb("identity", [P, P])
        K.identb = K.sb("identity_bf16", [P, P], BF16)
        K.eps5 = K.sb("eps_1e5", [P, 2 * T])
        K.neghalf = K.sb("minus_half", [P, 4 * T])
        K.ctxT = K.sb("contextT", [C, B * S])
        K.ctx_tile = K.sb("context_tile", [C, 2, S])
        K.ones = K.sb("ones", [P, P])
        K.mask_u8 = K.sb("mask_queries_u8", [P, B * T], U8)
        K.mask_q = K.sb("mask_queries", [P, B * T])
        K.g_all = K.sb("gate_values", [P, 8])
        K.gates = K.sb("gate_tanh", [P, 8])
        K.mask_k1, K.mask_k1c = K.sb("mask_keys_u8", [P, B * S], U8), K.sb("mask_key_columns_u8", [P, B * T], U8)
        K.hide_rows, K.hide_cols = K.sb("hide_key_rows", [P, B * S], BF16), K.sb("hide_key_columns", [P, B * T])
        K.pick_max = K.sb("pick_max", [P, H1, P], BF16)
        K.hide_q, K.hide_kT = K.sb("hide_later_keys", [P, T, S], BF16), K.sb("hide_later_keysT", [P, P], BF16)
        K.ctx_rows = K.sb("context_rows", [P, B * T * C])
        K.mask_k3, K.mask_k3c = K.sb("mask_ctx_u8", [P, B * S], U8), K.sb("mask_ctx_columns_u8", [P, B * T], U8)
        K.PS = ctx.enter_context(nc.psum_tensor("banks", [P, 8, 512], F32))
        K.norm = norm_tiles(K)
        W = {}
        for name, shape in WEIGHTS.items():
            if name[:2] not in LATE:
                W[name] = K.sb("w_" + name, list(shape))
        heads_memory = ctx.enter_context(ExitStack())
        K.heads = head_tiles(K, heads_memory, "early_heads")
        first_loaded = K.sem("first_inputs_loaded")
        for name in CREDITS:
            K.sem(name)
            K.totals[name] = CREDITS[name]
        groups = {}
        setup_memory = ExitStack()
        pick_f = setup_memory.enter_context(nc.sbuf_tensor("pick_max_f32", [P, H1, P], F32))
        hide_f = setup_memory.enter_context(nc.sbuf_tensor("hide_later_f32", [P, T * S + P], F32))

        def load(sp, wanted):
            for name in WEIGHTS:
                g = name[:2]
                if wanted(g):
                    sp.dma_start(W[name][:], a[name]).then_inc(K.sem("weights_loaded_" + g), 16)
                    groups[g] = groups.get(g, 0) + 16

        def place_late():
            for name, shape in WEIGHTS.items():
                if name[:2] in LATE:
                    W[name] = K.sb("w_" + name, list(shape))

        with nc.Block() as block:

            @block.sync
            def _(sp):
                sp.dma_start(K.X[:].rearrange("p (n d) -> p n d", d=D), a["x"].rearrange("(n p) d -> p n d", p=P)) \
                    .then_inc(first_loaded, 16)
                sp.dma_start(K.ctxT[:], a["ctxT"]).then_inc(first_loaded, 16)
                sp.dma_start(K.ident[:], a["identity"]).then_inc(first_loaded, 16)
                sp.dma_start(K.mask_u8[:], a["mask_queries"]).then_inc(first_loaded, 16)
                sp.dma_start(K.g_all[:], a["gates"]).then_inc(first_loaded, 16)
                sp.dma_start(K.mask_k1[:], a["mask_keys"]).then_inc(first_loaded, 16)
                sp.dma_start(K.mask_k1c[:], a["mask_key_columns"]).then_inc(first_loaded, 16)
                sp.dma_start(pick_f[:].rearrange("p h n -> p (h n)"), a["pick_max"]).then_inc(first_loaded, 16)
                sp.dma_start(hide_f[:], a["hide_later"]).then_inc(first_loaded, 16)
                sp.dma_start(K.ctx_rows[:].rearrange("p (n d) -> p n d", d=C), a["ctx"].rearrange("(n p) d -> p n d", p=P)).then_inc(first_loaded, 16)
                sp.dma_start(K.mask_k3[:], a["mask_ctx"]).then_inc(first_loaded, 16)
                sp.dma_start(K.mask_k3c[:], a["mask_ctx_columns"]).then_inc(first_loaded, 16)
                load(sp, lambda g: g not in LATE)

            @block.gpsimd
            def _(pool):
                nc.gpsimd.memset(K.eps5[:], 1e-5)
                nc.gpsimd.memset(K.neghalf[:], -0.5)
                pool_clear_heads(K, pool, "early_heads")
                for name, n in CREDITS.items():
                    pool.sem_inc(K.sem(name), n)

            @block.vector
            def _(dve):
                nc.vector.memset(K.ones[:], 1.0)
                dve_clear_heads(K, dve, "early_heads")
                dve.wait_ge(first_loaded, 16 * 12)
                nc.vector.tensor_copy(K.identb[:], K.ident[:])
                nc.vector.tensor_copy(K.pick_max[:], pick_f[:])
                nc.vector.tensor_copy(K.hide_q[:].rearrange("p t n -> p (t n)"), hide_f[:, 0:T * S])
                nc.vector.tensor_copy(K.hide_kT[:], hide_f[:, T * S:T * S + P])
                nc.vector.tensor_copy(K.mask_q[:], K.mask_u8[:])

            @block.scalar
            def _(act):
                act.wait_ge(first_loaded, 16 * 12)
                nc.scalar.activation(K.gates[:], K.g_all[:], ACT.Tanh)

        setup_memory.close()

        def loaded(g):
            return [(groups[g], K.sem("weights_loaded_" + g))]

        def heads_again():
            K.heads = head_tiles(K, heads_memory, "late_heads")
            K.Y = heads_memory.enter_context(nc.sbuf_tensor("y1_resident", [P, B * S], F32))
            with nc.Block() as block:

                @block.gpsimd
                def _(pool):
                    pool_clear_heads(K, pool, "late_heads")

                @block.vector
                def _(dve):
                    dve_clear_heads(K, dve, "late_heads")

        cross_attention_layer(K, "x0", 0, W["x0_wq"], W["x0_wkv"], mask=K.mask_q, loaded=loaded("x0"))
        quantised_ffn_layer(K, W, loaded("f0"))
        heads_memory.close()
        normed_attention_layer(K, W, loaded("x1"))
        heads_again()
        latent_moe_layer(K, W, loaded("f1"))
        cross_attention_layer(K, "x2", 2, W["x2_wq"], W["x2_wkv"], bias=dict(q=W["x2_bq"], k=W["x2_bk"], v=W["x2_bv"], o=W["x2_bo"]), wo=W["x2_wo"], loaded=loaded("x2"))
        heads_memory.close()
        place_late()
        routed_ffn_layer(K, W, loaded("f2"), lambda sp: load(sp, lambda g: g in LATE))
        perceiver_attention_layer(K, W, loaded("x3"))
        top2_moe_layer(K, W, loaded("f3"))

        stored = K.sem("result_stored")
        with nc.Block() as block:

            @block.sync
            def _(sp):
                sp.dma_start(out.rearrange("(n p) d -> p n d", p=P), K.X[:].rearrange("p (n d) -> p n d", d=D)) \
                    .then_inc(stored, 16)
                sp.wait_ge(stored, 16)


LATE = ("x3", "f3")
CREDITS = {"heads_out_banks": 1, "heads_qmT": 1, "signal_out_banks": 1, "signal_read": 2}
WEIGHTS = {
    "x0_wq": (P, D), "x0_wkv": (C, 2 * D),
    "f0_wg": (P, F0), "f0_wu": (P, F0), "f0_wd": (P, F0),
    "x1_wq": (P, I1), "x1_wk": (C, I1), "x1_wv": (C, I1), "x1_wo": (P, C1 * D), "x1_gnorm": (P, 1), "x1_gout": (P, D),
    "x1_nk": (P, DH1), "x1_nv": (P, DH1), "x1_qs": (P, DH1), "x1_ks": (P, DH1), "x1_qs_col": (P, 1), "x1_ks_col": (P, 1),
    "x2_wq": (P, D), "x2_wkv": (C, 2 * D), "x2_bq": (P, D), "x2_bk": (P, D), "x2_bv": (P, D), "x2_wo": (P, D), "x2_bo": (P, D),
    "f2_gate_w": (NE2, D), "f2_wg": (P, F2 + HE2), "f2_wu": (P, F2 + HE2), "f2_wd": (P, F2C * D), "f2_sd": (HE2, D),
    "x3_wql": (P, 3 * D), "x3_wkv": (C, 2 * D), "x3_wo": (P, D), "x3_bo": (P, D), "x3_qg": (P, 1), "x3_kg": (P, 1),
    "x3_lx_g": (C, 1), "x3_lx_b": (C, 1), "x3_ll_g": (P, 1), "x3_ll_b": (P, 1),
    "f3_gate_w": (P, NE3), "f3_w1": (P, NE3 * HE3), "f3_w3": (P, NE3 * HE3), "f3_w2": (P, NE3 * CE3 * D),
    "f1_norm1": (P, 1), "f1_norm2": (P, 1), "f1_ln_g": (P, 1), "f1_ln_b": (P, 1), "f1_wqd": (P, D + LAT), "f1_wukv": (LAT, 2 * D),
    "f1_wo": (P, D), "f1_rope": (P, 2 * T * DH), "f1_gate_w": (P, NE1), "f1_gate_b": (P, NE1), "f1_w1": (P, NE1 * HE1),
    "f1_b1": (P, NE1 * CE1), "f1_w2": (P, NE1 * CE1 * D), "f1_b2": (P, NE1 * D),
}


def lay_out(i):
    import numpy as np

    def T_(m):
        return np.ascontiguousarray(np.asarray(m).T)

    def rows(v):
        return np.ascontiguousarray(np.broadcast_to(np.asarray(v).reshape(1, -1), (P, np.asarray(v).size)))

    a = {}
    a["x"] = np.ascontiguousarray(np.asarray(i["x"]).reshape(B * S, D))
    a["ctxT"] = T_(np.asarray(i["ctx_768"]).reshape(B * S, C))
    a["identity"] = np.eye(P, dtype=np.float32)
    a["mask_queries"] = np.ascontiguousarray(np.asarray(i["mask_BxS_bk0"]).reshape(B * T, P).T)
    a["gates"] = rows(np.concatenate([np.asarray(i["g_xattn"]), np.asarray(i["g_ffn"])]))
    a["x0_wq"] = T_(i["L0_xattn_Wq"])
    a["x0_wkv"] = T_(i["L0_xattn_Wkv"])
    def chunked(m):
        m = np.asarray(m)
        return np.ascontiguousarray(m.reshape(-1, P, m.shape[-1]).transpose(1, 0, 2).reshape(P, -1))

    a["f0_wg"] = T_(i["L0_ffn_w_gate"])
    a["f0_wu"] = T_(i["L0_ffn_w_up"])
    a["f0_wd"] = chunked(T_(i["L0_ffn_w_down"]))
    def col(v, n=1):
        return np.ascontiguousarray(np.tile(np.asarray(v), n).reshape(-1, 1))

    mask1 = np.asarray(i["mask_BxS2_bf1"])
    a["mask_keys"] = rows(mask1)
    a["mask_key_columns"] = np.ascontiguousarray(mask1.reshape(B * T, P).T)
    pick = np.zeros((P, H1, P), np.float32)
    for n in range(H1):
        pick[3 * n:3 * n + 3, n] = 1.0
    a["pick_max"] = pick.reshape(P, -1)
    wkv = np.asarray(i["L1_xattn_Wkv"])
    a["x1_wq"] = np.ascontiguousarray(i["L1_xattn_Wq"])
    a["x1_wk"] = np.ascontiguousarray(wkv[:, :I1])
    a["x1_wv"] = np.ascontiguousarray(wkv[:, I1:])
    a["x1_wo"] = chunked(i["L1_xattn_Wo"])
    a["x1_gnorm"] = col(i["L1_xattn_g_norm"])
    a["x1_gout"] = rows(i["L1_xattn_g_out"])
    a["x1_nk"], a["x1_nv"] = rows(np.asarray(i["L1_xattn_null_kv"])[0]), rows(np.asarray(i["L1_xattn_null_kv"])[1])
    a["x1_qs"], a["x1_ks"] = rows(i["L1_xattn_q_scale"]), rows(i["L1_xattn_k_scale"])
    a["x1_qs_col"], a["x1_ks_col"] = col(i["L1_xattn_q_scale"], 2), col(i["L1_xattn_k_scale"], 2)
    def padded_col(v):
        v = np.asarray(v)
        return np.ascontiguousarray(np.concatenate([v, np.zeros(P - v.size, v.dtype)]).reshape(-1, 1))

    def cat(*ms):
        return np.ascontiguousarray(np.concatenate(ms, axis=1))

    a["f1_norm1"], a["f1_norm2"] = col(i["L1_ffn_norm1_w"]), col(i["L1_ffn_norm2_w"])
    a["f1_ln_g"], a["f1_ln_b"] = padded_col(i["L1_ffn_ln_g"]), padded_col(i["L1_ffn_ln_b"])
    a["f1_wqd"] = cat(T_(i["L1_ffn_Wq"]), T_(i["L1_ffn_Wdkv"]))
    a["f1_wukv"] = cat(T_(i["L1_ffn_Wuk"]), T_(i["L1_ffn_Wuv"]))
    a["f1_wo"] = T_(i["L1_ffn_Wo"])
    half = DH // 2
    freq = (np.float32(1.0) / np.float32(10000.0) ** (np.arange(half, dtype=np.float32) / np.float32(half))).astype(np.float32)
    ang = np.arange(S, dtype=np.float32)[:, None] * freq[None, :]
    cos, sin = np.cos(ang).astype(np.float32), np.sin(ang).astype(np.float32)
    tables = np.stack([np.concatenate([cos, cos], 1), np.concatenate([-sin, sin], 1)])
    a["f1_rope"] = np.ascontiguousarray(tables.reshape(2, T, P, DH).transpose(2, 0, 1, 3).reshape(P, -1))
    later = np.arange(S)[None, :] > np.arange(S)[:, None]
    hide = np.where(later, np.float32(HIDE), np.float32(0.0)).astype(np.float32)
    a["hide_later"] = cat(hide.reshape(T, P, S).transpose(1, 0, 2).reshape(P, -1), hide[:P, :P].T)
    a["f1_gate_w"], a["f1_gate_b"] = T_(i["L1_ffn_gate_w"]), rows(i["L1_ffn_gate_b"])
    a["f1_w1"] = np.ascontiguousarray(np.asarray(i["L1_ffn_W1"]).reshape(NE1 * HE1, D).T)
    a["f1_b1"] = np.ascontiguousarray(np.asarray(i["L1_ffn_b1"]).reshape(NE1 * CE1, P).T)
    a["f1_w2"] = np.ascontiguousarray(np.asarray(i["L1_ffn_W2"]).reshape(NE1, D, CE1, P).transpose(3, 0, 2, 1).reshape(P, -1))
    a["f1_b2"] = rows(i["L1_ffn_b2"])
    wkv2, bkv2 = np.asarray(i["L2_xattn_Wkv"]).reshape(H, 2, DH, C), np.asarray(i["L2_xattn_bkv"]).reshape(H, 2, DH)
    a["x2_wq"], a["x2_wo"] = T_(i["L2_xattn_Wq"]), T_(i["L2_xattn_Wo"])
    a["x2_wkv"] = T_(wkv2.transpose(1, 0, 2, 3).reshape(2 * D, C))
    a["x2_bq"], a["x2_bo"] = rows(i["L2_xattn_bq"]), rows(i["L2_xattn_bo"])
    a["x2_bk"], a["x2_bv"] = rows(bkv2[:, 0]), rows(bkv2[:, 1])
    a["f2_gate_w"] = np.ascontiguousarray(i["L2_ffn_gate_w"])

    def side_by_side(m):
        return np.asarray(m).transpose(1, 0, 2).reshape(D, -1)

    a["f2_wg"] = cat(side_by_side(i["L2_ffn_w_gate"]), np.asarray(i["L2_ffn_sw_gate"]))
    a["f2_wu"] = cat(side_by_side(i["L2_ffn_w_up"]), np.asarray(i["L2_ffn_sw_up"]))
    a["f2_wd"] = chunked(np.asarray(i["L2_ffn_w_down"]).reshape(F2, D))
    a["f2_sd"] = np.ascontiguousarray(i["L2_ffn_sw_down"])
    a["ctx"] = np.ascontiguousarray(np.asarray(i["ctx_768"]).reshape(B * S, C))
    mask3 = np.asarray(i["mask_BxS2_bk0"])
    a["mask_ctx"] = rows(mask3)
    a["mask_ctx_columns"] = np.ascontiguousarray(mask3.reshape(B * T, P).T)
    a["x3_wql"] = cat(T_(i["L3_xattn_Wq"]), T_(i["L3_xattn_Wlkv"]))
    a["x3_wkv"], a["x3_wo"], a["x3_bo"] = T_(i["L3_xattn_Wkv"]), T_(i["L3_xattn_Wo"]), rows(i["L3_xattn_bo"])
    a["x3_qg"], a["x3_kg"] = col(i["L3_xattn_qn_g"], 2), col(i["L3_xattn_kn_g"], 2)
    a["x3_lx_g"], a["x3_lx_b"] = col(i["L3_xattn_ln_x_g"]), col(i["L3_xattn_ln_x_b"])
    a["x3_ll_g"], a["x3_ll_b"] = col(i["L3_xattn_ln_l_g"]), col(i["L3_xattn_ln_l_b"])
    a["f3_gate_w"] = T_(i["L3_ffn_gate_w"])
    a["f3_w1"], a["f3_w3"] = np.ascontiguousarray(side_by_side(i["L3_ffn_w1"])), np.ascontiguousarray(side_by_side(i["L3_ffn_w3"]))
    a["f3_w2"] = chunked(np.asarray(i["L3_ffn_w2"]).reshape(NE3 * HE3, D))
    return a


def kernel(**inputs):
    import numpy as np
    import concourse.bacc as bacc
    from concourse.bass_utils import run_bass_kernel_spmd

    nc = bacc.Bacc("TRN2", target_bir_lowering=False, num_devices=1)
    arrays = {f"in_{n}": v for n, v in lay_out(inputs).items()}
    a = {n[3:]: nc.dram_tensor(n, v.shape, mybir.dt.from_np(v.dtype), kind="ExternalInput").ap() for n, v in arrays.items()}
    out = nc.dram_tensor("out", (B * S, D), F32, kind="ExternalOutput").ap()
    build(nc, a, out)
    r = run_bass_kernel_spmd(nc, [arrays], core_ids=[0])
    return np.asarray(r.results[0]["out"]).reshape(B, S, D)
```
